# Optimizing a Trainium2 kernel written in Bass

```python
import numpy as np
import jax
import jax.numpy as jnp

def _softmax(x, axis=-1):
    return jax.nn.softmax(x, axis=axis)

def _gelu(x):
    return jax.nn.gelu(x, approximate=True)

def _silu(x):
    return jax.nn.silu(x)

def _sigmoid(x):
    return jax.nn.sigmoid(x)

def _layernorm(x, axis=-1, eps=1e-05):
    m = jnp.mean(x, axis=axis, keepdims=True)
    v = jnp.var(x, axis=axis, keepdims=True)
    return (x - m) / jnp.sqrt(v + eps)

def _scatter_add(tgt, idx, src, axis=0):
    return tgt.at[idx].add(src)

def _segment_sum(src, seg, n):
    return jax.ops.segment_sum(src, seg, n)
kernel_name = 'mk_flamingo_gated_d4_seqx_r8_f83aea'

def setup_inputs(seed: int=0):
    np.random.seed(seed)
    _w = jnp.asarray

    def _rec_inputs():
        import jax
        import jax.numpy as jnp
        _rk = jax.random.key(seed)
        x = 7.22e-05 + 1 * jax.random.normal(jax.random.fold_in(_rk, 1), (4, 512, 128), jnp.float32)
        _lenS = 512 - jax.random.randint(jax.random.fold_in(_rk, 7), (4,), 0, max(1, 512 // 4) + 1, jnp.int32)
        _lenS2 = 154 - jax.random.randint(jax.random.fold_in(_rk, 8), (4,), 0, max(1, 154 // 4) + 1, jnp.int32)
        _ctx_768P = jax.random.normal(jax.random.fold_in(_rk, 11), (4, 16, 96), jnp.float32)
        _ctx_768c = jax.random.dirichlet(jax.random.fold_in(_rk, 511), 0.3 * jnp.ones((16,), jnp.float32), (4, 154))
        _ctx_768t = jnp.einsum('bsk,bkd->bsd', _ctx_768c, _ctx_768P)
        _ctx_768t = _ctx_768t * jax.lax.rsqrt(jnp.mean(jnp.square(_ctx_768t)) + 1e-12) * 0.953939
        ctx_768 = 3.88148e-05 + 0.999967 * (_ctx_768t + 0.3 * jax.random.normal(jax.random.fold_in(_rk, 611), (4, 154, 96), jnp.float32))
        _validS = jnp.arange(512)[None, :] < _lenS[:, None]
        _validS2 = jnp.arange(154)[None, :] < _lenS2[:, None]
        _causal = jnp.tril(jnp.ones((512, 512), dtype=bool))
        mask_BxS_bf1 = jnp.ones((4, 512), dtype=bool)
        mask_BxS2_bf1 = jnp.ones((4, 154), dtype=bool)
        mask_BxS2_bk0 = jnp.logical_not(jnp.broadcast_to(_validS2[:, :], (4, 154)))
        _g = jax.random.normal(jax.random.fold_in(_rk, 9001), (2, 4), jnp.float32)
        _g = jnp.sign(_g) * jnp.maximum(jnp.abs(_g), 1.0) + (_g == 0) * 1.0
        g_xattn = _g[0]
        g_ffn = _g[1]
        return (x, ctx_768, mask_BxS_bf1, mask_BxS2_bf1, mask_BxS2_bk0, g_xattn, g_ffn)
    x, ctx_768, mask_BxS_bf1, mask_BxS2_bf1, mask_BxS2_bk0, g_xattn, g_ffn = _rec_inputs()

    def _L0_xattn_setup():
        import jax, jax.numpy as jnp
        import numpy as np
        B, T, DT, G, DV = (16, 64, 128, 72, 96)
        H, DH = (4, 32)
        INNER = H * DH
        HID = 4 * DT
        N_STATE = 64
        K_TOP = 32

        def layernorm(x, g, b, eps=1e-05):
            m = x.mean(-1, keepdims=True)
            v = x.var(-1, keepdims=True)
            return (x - m) * jax.lax.rsqrt(v + eps) * g + b

        def s4d(x, log_dt, A_re, A_im, C_re, C_im, D_skip):
            Bb, L, D = x.shape
            dt = jnp.exp(log_dt)
            A = A_re + 1j * A_im
            C = C_re + 1j * C_im
            dtA = dt[:, None] * A
            dC = C * (jnp.exp(dtA) - 1.0) / A
            powers = jnp.exp(dtA[:, :, None] * jnp.arange(L))
            K = 2.0 * jnp.einsum('dn,dnl->dl', dC, powers).real
            n = 2 * L
            Kf = jnp.fft.rfft(K, n=n, axis=-1)
            xf = jnp.fft.rfft(x, n=n, axis=1)
            y = jnp.fft.irfft(xf * Kf.T[None], n=n, axis=1)[:, :L]
            return y + x * D_skip
        key = jax.random.key(seed)
        ks = jax.random.split(key, 16)
        s = 0.02
        inp = {'x_text': jax.random.normal(ks[0], (B, T, DT), jnp.float32), 'x_vision': jax.random.normal(ks[1], (B, G, DV), jnp.float32), 'text_mask': jnp.ones((B, T), bool), 'vision_mask': jnp.ones((B, G), bool), 'Wq': jax.random.normal(ks[2], (DT, INNER), jnp.float32) * s, 'Wk': jax.random.normal(ks[3], (DV, INNER), jnp.float32) * s, 'Wv': jax.random.normal(ks[4], (DV, DT), jnp.float32) * s, 'W_film_in': jax.random.normal(ks[5], (DT, 2 * DT), jnp.float32) * s, 'b_film_in': jnp.zeros((2 * DT,), jnp.float32), 'W_film_out': jax.random.normal(ks[6], (DT, 2 * DT), jnp.float32) * s, 'b_film_out': jnp.zeros((2 * DT,), jnp.float32), 'g_norm_in': jnp.ones((DT,), jnp.float32), 'b_norm_in': jnp.zeros((DT,), jnp.float32), 'g_norm_out': jnp.ones((DT,), jnp.float32), 'b_norm_out': jnp.zeros((DT,), jnp.float32), 'g_ffn': jnp.ones((DT,), jnp.float32), 'b_ffn': jnp.zeros((DT,), jnp.float32), 'W1': jax.random.normal(ks[7], (DT, HID), jnp.float32) * s, 'b1': jnp.zeros((HID,), jnp.float32), 'W2': jax.random.normal(ks[8], (HID, DT), jnp.float32) * s, 'b2': jnp.zeros((DT,), jnp.float32), 'log_dt': jnp.log(0.001) + jax.random.uniform(ks[9], (DT,), jnp.float32) * (jnp.log(0.1) - jnp.log(0.001)), 'A_re': -0.5 * jnp.ones((DT, N_STATE), jnp.float32), 'A_im': jnp.tile(jnp.pi * jnp.arange(N_STATE, dtype=jnp.float32), (DT, 1)), 'C_re': jax.random.normal(ks[10], (DT, N_STATE), jnp.float32) * 0.5 ** 0.5, 'C_im': jax.random.normal(ks[11], (DT, N_STATE), jnp.float32) * 0.5 ** 0.5, 'D_skip': jax.random.normal(ks[12], (DT,), jnp.float32), 'mod_gate': jnp.array(0.5, jnp.float32)}
        return inp
    _L0_xattn_all = _L0_xattn_setup()
    _L0_xattn_in = {k: v for k, v in _L0_xattn_all.items() if k in ('Wq', 'Wk', 'Wv', 'W_film_in', 'b_film_in', 'W_film_out', 'b_film_out', 'g_norm_in', 'b_norm_in', 'g_norm_out', 'b_norm_out', 'g_ffn', 'b_ffn', 'W1', 'b1', 'W2', 'b2', 'log_dt', 'A_re', 'A_im', 'C_re', 'C_im', 'D_skip', 'mod_gate')}
    del _L0_xattn_all

    def _L0_ffn_setup():
        import jax, jax.numpy as jnp
        import numpy as np
        LN_EPS = 0.001
        EPS = 1e-05
        QB = 128.0

        def ste_round(x):
            return x + jax.lax.stop_gradient(jnp.round(x) - x)
        key = jax.random.key(seed)
        k1, k2 = jax.random.split(key)
        x = jax.random.normal(k1, (4, 1024, 128), dtype=jnp.float32)
        weight = jax.random.normal(k2, (128, 128), dtype=jnp.float32) * 0.02
        ln_gamma = jnp.ones((128,), dtype=jnp.float32)
        ln_beta = jnp.zeros((128,), dtype=jnp.float32)
        return {'x': x, 'weight': weight, 'ln_gamma': ln_gamma, 'ln_beta': ln_beta}
    _L0_ffn_all = _L0_ffn_setup()
    _L0_ffn_in = {k: v for k, v in _L0_ffn_all.items() if k in ('weight', 'ln_gamma', 'ln_beta')}
    del _L0_ffn_all

    def _L1_xattn_setup():
        import jax, jax.numpy as jnp
        import numpy as np
        DIM_IN, DIM_LAT, DIM_HEAD = (96, 128, 64)
        INNER = max(DIM_LAT, DIM_IN)
        HEADS = INNER // DIM_HEAD
        SCALE = DIM_HEAD ** (-0.5)
        RMS_EPS = 1e-08
        LN_EPS = 1e-05

        def layernorm(x, g, b):
            mu = jnp.mean(x, axis=-1, keepdims=True)
            var = jnp.mean((x - mu) ** 2, axis=-1, keepdims=True)
            return (x - mu) * jax.lax.rsqrt(var + LN_EPS) * g + b

        def rmsnorm(x, gamma):
            norm = jnp.sqrt(jnp.sum(x * x, axis=-1, keepdims=True)) * x.shape[-1] ** (-0.5)
            return x / jnp.maximum(norm, RMS_EPS) * gamma
        key = jax.random.key(seed)
        ks = jax.random.split(key, 12)
        b, n, m = (4, 512, 64)
        x = jax.random.normal(ks[0], (b, n, DIM_IN), jnp.float32)
        latents = jax.random.normal(ks[1], (b, m, DIM_LAT), jnp.float32)
        mask = jax.random.randint(ks[2], (b, n), 0, 2).astype(bool)
        s = lambda k, sh, fan: jax.random.normal(k, sh, jnp.float32) * fan ** (-0.5)
        return {'x': x, 'latents': latents, 'mask': mask, 'ln_x_g': jnp.ones((DIM_IN,), jnp.float32), 'ln_x_b': jnp.zeros((DIM_IN,), jnp.float32), 'ln_l_g': jnp.ones((DIM_LAT,), jnp.float32), 'ln_l_b': jnp.zeros((DIM_LAT,), jnp.float32), 'qn_g': jnp.ones((DIM_HEAD,), jnp.float32), 'kn_g': jnp.ones((DIM_HEAD,), jnp.float32), 'Wq': s(ks[3], (INNER, DIM_LAT), DIM_LAT), 'Wkv': s(ks[4], (2 * INNER, DIM_IN), DIM_IN), 'Wlkv': s(ks[5], (2 * INNER, DIM_LAT), DIM_LAT), 'Wo': s(ks[6], (DIM_LAT, INNER), INNER), 'bo': jnp.zeros((DIM_LAT,), jnp.float32)}
    _L1_xattn_all = _L1_xattn_setup()
    _L1_xattn_in = {k: v for k, v in _L1_xattn_all.items() if k in ('ln_x_g', 'ln_x_b', 'ln_l_g', 'ln_l_b', 'qn_g', 'kn_g', 'Wq', 'Wkv', 'Wlkv', 'Wo', 'bo')}
    del _L1_xattn_all

    def _L1_ffn_setup():
        import jax, jax.numpy as jnp
        import numpy as np
        H = 128
        E = 64
        K = 8
        G = 8
        TOPK_GROUP = 4
        I_MOE = 64
        I_SHARED = 256
        SCALE = 2.5

        def relu2(x):
            return jnp.square(jax.nn.relu(x))

        def _route(xf, router_w, correction_bias):
            T = xf.shape[0]
            logits = xf @ router_w.T
            scores = jax.nn.sigmoid(logits)
            sfc = scores + correction_bias[None, :]
            grp = sfc.reshape(T, G, E // G)
            top2, _ = jax.lax.top_k(grp, 2)
            group_scores = top2.sum(-1)
            _, gidx = jax.lax.top_k(group_scores, TOPK_GROUP)
            gmask = jnp.zeros((T, G), sfc.dtype).at[jnp.arange(T)[:, None], gidx].set(1.0)
            emask = jnp.repeat(gmask, E // G, axis=1)
            masked = jnp.where(emask > 0, sfc, 0.0)
            _, tidx = jax.lax.top_k(masked, K)
            tw = jnp.take_along_axis(scores, tidx, axis=1)
            tw = tw / (tw.sum(-1, keepdims=True) + 1e-20)
            return (tidx, tw * SCALE)
        key = jax.random.key(seed)
        ks = jax.random.split(key, 7)
        x = jax.random.normal(ks[0], (2, 128, H), dtype=jnp.float32)
        router_w = jax.random.normal(ks[1], (E, H), dtype=jnp.float32) * 0.02
        correction_bias = jax.random.normal(ks[2], (E,), dtype=jnp.float32) * 0.01
        up_w = jax.random.normal(ks[3], (E, H, I_MOE), dtype=jnp.float32) * 0.02
        down_w = jax.random.normal(ks[4], (E, I_MOE, H), dtype=jnp.float32) * 0.02
        shared_up_w = jax.random.normal(ks[5], (H, I_SHARED), dtype=jnp.float32) * 0.02
        shared_down_w = jax.random.normal(ks[6], (I_SHARED, H), dtype=jnp.float32) * 0.02
        return {'x': x, 'router_w': router_w, 'correction_bias': correction_bias, 'up_w': up_w, 'down_w': down_w, 'shared_up_w': shared_up_w, 'shared_down_w': shared_down_w}
    _L1_ffn_all = _L1_ffn_setup()
    _L1_ffn_in = {k: v for k, v in _L1_ffn_all.items() if k in ('router_w', 'correction_bias', 'up_w', 'down_w', 'shared_up_w', 'shared_down_w')}
    del _L1_ffn_all

    def _L2_xattn_setup():
        import jax, jax.numpy as jnp
        import numpy as np
        HEADS = 16
        DIM_HEAD = 64
        key = jax.random.key(seed)
        ks = jax.random.split(key, 7)
        b, n, m = (2, 256, 128)
        query_dim, context_dim = (128, 96)
        inner = HEADS * DIM_HEAD
        s_q = 1.0 / np.sqrt(query_dim)
        s_c = 1.0 / np.sqrt(context_dim)
        s_i = 1.0 / np.sqrt(inner)
        return {'x': jax.random.normal(ks[0], (b, n, query_dim), jnp.float32), 'context': jax.random.normal(ks[1], (b, m, context_dim), jnp.float32), 'Wq': jax.random.normal(ks[2], (query_dim, inner), jnp.float32) * s_q, 'Wk': jax.random.normal(ks[3], (context_dim, inner), jnp.float32) * s_c, 'Wv': jax.random.normal(ks[4], (context_dim, inner), jnp.float32) * s_c, 'Wo': jax.random.normal(ks[5], (inner, query_dim), jnp.float32) * s_i, 'bo': jax.random.normal(ks[6], (query_dim,), jnp.float32) * 0.01}
    _L2_xattn_all = _L2_xattn_setup()
    _L2_xattn_in = {k: v for k, v in _L2_xattn_all.items() if k in ('Wq', 'Wk', 'Wv', 'Wo', 'bo')}
    del _L2_xattn_all

    def _L2_ffn_setup():
        import jax, jax.numpy as jnp
        import numpy as np
        B, S, H, I, E, K = (2, 64, 128, 64, 64, 8)
        key = jax.random.key(seed)
        ks = jax.random.split(key, 8)
        return {'hidden_states': jax.random.normal(ks[0], (B, S, H), dtype=jnp.float32), 'router_w': jax.random.normal(ks[1], (H, E), dtype=jnp.float32) * 0.02, 'shared_gate_w': jax.random.normal(ks[2], (H, I), dtype=jnp.float32) * 0.02, 'shared_up_w': jax.random.normal(ks[3], (H, I), dtype=jnp.float32) * 0.02, 'shared_down_w': jax.random.normal(ks[4], (I, H), dtype=jnp.float32) * 0.02, 'expert_gate_k': jax.random.normal(ks[5], (E, H, I), dtype=jnp.float32) * 0.02, 'expert_up_k': jax.random.normal(ks[6], (E, H, I), dtype=jnp.float32) * 0.02, 'expert_down_k': jax.random.normal(ks[7], (E, I, H), dtype=jnp.float32) * 0.02}
    _L2_ffn_all = _L2_ffn_setup()
    _L2_ffn_in = {k: v for k, v in _L2_ffn_all.items() if k in ('router_w', 'shared_gate_w', 'shared_up_w', 'shared_down_w', 'expert_gate_k', 'expert_up_k', 'expert_down_k')}
    del _L2_ffn_all

    def _L3_xattn_setup():
        import jax, jax.numpy as jnp
        import numpy as np
        HEADS = 8
        DIM_HEAD = 128
        ATTN_MATRIX_SCALE = 1.5
        SCALE = DIM_HEAD ** (-0.5)

        def _split_heads(t):
            b, n, _ = t.shape
            t = t.reshape(b, n, HEADS, DIM_HEAD)
            return t.transpose(2, 0, 1, 3).reshape(HEADS, b * n, DIM_HEAD)
        key = jax.random.key(seed)
        ks = jax.random.split(key, 7)
        b, n, m = (2, 256, 256)
        qd, cd, inner = (128, 96, HEADS * DIM_HEAD)
        x = jax.random.normal(ks[0], (b, n, qd), dtype=jnp.float32)
        context = jax.random.normal(ks[1], (b, m, cd), dtype=jnp.float32)
        Wq = jax.random.normal(ks[2], (qd, inner), dtype=jnp.float32) * qd ** (-0.5)
        Wk = jax.random.normal(ks[3], (cd, inner), dtype=jnp.float32) * cd ** (-0.5)
        Wv = jax.random.normal(ks[4], (cd, inner), dtype=jnp.float32) * cd ** (-0.5)
        Wout = jax.random.normal(ks[5], (inner, qd), dtype=jnp.float32) * inner ** (-0.5)
        bout = jnp.zeros((qd,), dtype=jnp.float32)
        return {'x': x, 'context': context, 'Wq': Wq, 'Wk': Wk, 'Wv': Wv, 'Wout': Wout, 'bout': bout}
    _L3_xattn_all = _L3_xattn_setup()
    _L3_xattn_in = {k: v for k, v in _L3_xattn_all.items() if k in ('Wq', 'Wk', 'Wv', 'Wout', 'bout')}
    del _L3_xattn_all

    def _L3_ffn_setup():
        import jax, jax.numpy as jnp
        import numpy as np
        D_MODEL = 128
        D_FF = 512
        NUM_EXPERTS = 8
        TOP_K = 2
        key = jax.random.key(seed)
        ks = jax.random.split(key, 8)
        s_in = 1.0 / np.sqrt(D_MODEL)
        s_ff = 1.0 / np.sqrt(D_FF)
        x = jax.random.normal(ks[0], (2, 256, D_MODEL), dtype=jnp.float32)
        Wg = jax.random.uniform(ks[1], (D_MODEL, NUM_EXPERTS), minval=-s_in, maxval=s_in, dtype=jnp.float32)
        bg = jax.random.uniform(ks[2], (NUM_EXPERTS,), minval=-s_in, maxval=s_in, dtype=jnp.float32)
        W1 = jax.random.uniform(ks[3], (NUM_EXPERTS, D_MODEL, D_FF), minval=-s_in, maxval=s_in, dtype=jnp.float32)
        b1 = jax.random.uniform(ks[4], (NUM_EXPERTS, D_FF), minval=-s_in, maxval=s_in, dtype=jnp.float32)
        W2 = jax.random.uniform(ks[5], (NUM_EXPERTS, D_FF, D_MODEL), minval=-s_ff, maxval=s_ff, dtype=jnp.float32)
        b2 = jax.random.uniform(ks[6], (NUM_EXPERTS, D_MODEL), minval=-s_ff, maxval=s_ff, dtype=jnp.float32)
        return {'x': x, 'Wg': Wg, 'bg': bg, 'W1': W1, 'b1': b1, 'W2': W2, 'b2': b2}
    _L3_ffn_all = _L3_ffn_setup()
    _L3_ffn_in = {k: v for k, v in _L3_ffn_all.items() if k in ('Wg', 'bg', 'W1', 'b1', 'W2', 'b2')}
    del _L3_ffn_all
    return {'x': x, 'ctx_768': ctx_768, 'mask_BxS_bf1': mask_BxS_bf1, 'mask_BxS2_bf1': mask_BxS2_bf1, 'mask_BxS2_bk0': mask_BxS2_bk0, 'g_xattn': g_xattn, 'g_ffn': g_ffn, 'L0_xattn_Wq': _L0_xattn_in['Wq'], 'L0_xattn_Wk': _L0_xattn_in['Wk'], 'L0_xattn_Wv': _L0_xattn_in['Wv'], 'L0_xattn_W_film_in': _L0_xattn_in['W_film_in'], 'L0_xattn_b_film_in': _L0_xattn_in['b_film_in'], 'L0_xattn_W_film_out': _L0_xattn_in['W_film_out'], 'L0_xattn_b_film_out': _L0_xattn_in['b_film_out'], 'L0_xattn_g_norm_in': _L0_xattn_in['g_norm_in'], 'L0_xattn_b_norm_in': _L0_xattn_in['b_norm_in'], 'L0_xattn_g_norm_out': _L0_xattn_in['g_norm_out'], 'L0_xattn_b_norm_out': _L0_xattn_in['b_norm_out'], 'L0_xattn_g_ffn': _L0_xattn_in['g_ffn'], 'L0_xattn_b_ffn': _L0_xattn_in['b_ffn'], 'L0_xattn_W1': _L0_xattn_in['W1'], 'L0_xattn_b1': _L0_xattn_in['b1'], 'L0_xattn_W2': _L0_xattn_in['W2'], 'L0_xattn_b2': _L0_xattn_in['b2'], 'L0_xattn_log_dt': _L0_xattn_in['log_dt'], 'L0_xattn_A_re': _L0_xattn_in['A_re'], 'L0_xattn_A_im': _L0_xattn_in['A_im'], 'L0_xattn_C_re': _L0_xattn_in['C_re'], 'L0_xattn_C_im': _L0_xattn_in['C_im'], 'L0_xattn_D_skip': _L0_xattn_in['D_skip'], 'L0_xattn_mod_gate': _L0_xattn_in['mod_gate'], 'L0_ffn_weight': _L0_ffn_in['weight'], 'L0_ffn_ln_gamma': _L0_ffn_in['ln_gamma'], 'L0_ffn_ln_beta': _L0_ffn_in['ln_beta'], 'L1_xattn_ln_x_g': _L1_xattn_in['ln_x_g'], 'L1_xattn_ln_x_b': _L1_xattn_in['ln_x_b'], 'L1_xattn_ln_l_g': _L1_xattn_in['ln_l_g'], 'L1_xattn_ln_l_b': _L1_xattn_in['ln_l_b'], 'L1_xattn_qn_g': _L1_xattn_in['qn_g'], 'L1_xattn_kn_g': _L1_xattn_in['kn_g'], 'L1_xattn_Wq': _L1_xattn_in['Wq'], 'L1_xattn_Wkv': _L1_xattn_in['Wkv'], 'L1_xattn_Wlkv': _L1_xattn_in['Wlkv'], 'L1_xattn_Wo': _L1_xattn_in['Wo'], 'L1_xattn_bo': _L1_xattn_in['bo'], 'L1_ffn_router_w': _L1_ffn_in['router_w'], 'L1_ffn_correction_bias': _L1_ffn_in['correction_bias'], 'L1_ffn_up_w': _L1_ffn_in['up_w'], 'L1_ffn_down_w': _L1_ffn_in['down_w'], 'L1_ffn_shared_up_w': _L1_ffn_in['shared_up_w'], 'L1_ffn_shared_down_w': _L1_ffn_in['shared_down_w'], 'L2_xattn_Wq': _L2_xattn_in['Wq'], 'L2_xattn_Wk': _L2_xattn_in['Wk'], 'L2_xattn_Wv': _L2_xattn_in['Wv'], 'L2_xattn_Wo': _L2_xattn_in['Wo'], 'L2_xattn_bo': _L2_xattn_in['bo'], 'L2_ffn_router_w': _L2_ffn_in['router_w'], 'L2_ffn_shared_gate_w': _L2_ffn_in['shared_gate_w'], 'L2_ffn_shared_up_w': _L2_ffn_in['shared_up_w'], 'L2_ffn_shared_down_w': _L2_ffn_in['shared_down_w'], 'L2_ffn_expert_gate_k': _L2_ffn_in['expert_gate_k'], 'L2_ffn_expert_up_k': _L2_ffn_in['expert_up_k'], 'L2_ffn_expert_down_k': _L2_ffn_in['expert_down_k'], 'L3_xattn_Wq': _L3_xattn_in['Wq'], 'L3_xattn_Wk': _L3_xattn_in['Wk'], 'L3_xattn_Wv': _L3_xattn_in['Wv'], 'L3_xattn_Wout': _L3_xattn_in['Wout'], 'L3_xattn_bout': _L3_xattn_in['bout'], 'L3_ffn_Wg': _L3_ffn_in['Wg'], 'L3_ffn_bg': _L3_ffn_in['bg'], 'L3_ffn_W1': _L3_ffn_in['W1'], 'L3_ffn_b1': _L3_ffn_in['b1'], 'L3_ffn_W2': _L3_ffn_in['W2'], 'L3_ffn_b2': _L3_ffn_in['b2']}

def reference(x, ctx_768, mask_BxS_bf1, mask_BxS2_bf1, mask_BxS2_bk0, g_xattn, g_ffn, L0_xattn_Wq, L0_xattn_Wk, L0_xattn_Wv, L0_xattn_W_film_in, L0_xattn_b_film_in, L0_xattn_W_film_out, L0_xattn_b_film_out, L0_xattn_g_norm_in, L0_xattn_b_norm_in, L0_xattn_g_norm_out, L0_xattn_b_norm_out, L0_xattn_g_ffn, L0_xattn_b_ffn, L0_xattn_W1, L0_xattn_b1, L0_xattn_W2, L0_xattn_b2, L0_xattn_log_dt, L0_xattn_A_re, L0_xattn_A_im, L0_xattn_C_re, L0_xattn_C_im, L0_xattn_D_skip, L0_xattn_mod_gate, L0_ffn_weight, L0_ffn_ln_gamma, L0_ffn_ln_beta, L1_xattn_ln_x_g, L1_xattn_ln_x_b, L1_xattn_ln_l_g, L1_xattn_ln_l_b, L1_xattn_qn_g, L1_xattn_kn_g, L1_xattn_Wq, L1_xattn_Wkv, L1_xattn_Wlkv, L1_xattn_Wo, L1_xattn_bo, L1_ffn_router_w, L1_ffn_correction_bias, L1_ffn_up_w, L1_ffn_down_w, L1_ffn_shared_up_w, L1_ffn_shared_down_w, L2_xattn_Wq, L2_xattn_Wk, L2_xattn_Wv, L2_xattn_Wo, L2_xattn_bo, L2_ffn_router_w, L2_ffn_shared_gate_w, L2_ffn_shared_up_w, L2_ffn_shared_down_w, L2_ffn_expert_gate_k, L2_ffn_expert_up_k, L2_ffn_expert_down_k, L3_xattn_Wq, L3_xattn_Wk, L3_xattn_Wv, L3_xattn_Wout, L3_xattn_bout, L3_ffn_Wg, L3_ffn_bg, L3_ffn_W1, L3_ffn_b1, L3_ffn_W2, L3_ffn_b2):
    import jax
    import jax.numpy as jnp

    def _L0_xattn_ref(x_text, x_vision, text_mask, vision_mask, Wq, Wk, Wv, W_film_in, b_film_in, W_film_out, b_film_out, g_norm_in, b_norm_in, g_norm_out, b_norm_out, g_ffn, b_ffn, W1, b1, W2, b2, log_dt, A_re, A_im, C_re, C_im, D_skip, mod_gate):
        import jax, jax.numpy as jnp
        import numpy as np
        B, T, DT, G, DV = (16, 64, 128, 72, 96)
        H, DH = (4, 32)
        INNER = H * DH
        HID = 4 * DT
        N_STATE = 64
        K_TOP = 32

        def layernorm(x, g, b, eps=1e-05):
            m = x.mean(-1, keepdims=True)
            v = x.var(-1, keepdims=True)
            return (x - m) * jax.lax.rsqrt(v + eps) * g + b

        def s4d(x, log_dt, A_re, A_im, C_re, C_im, D_skip):
            Bb, L, D = x.shape
            dt = jnp.exp(log_dt)
            A = A_re + 1j * A_im
            C = C_re + 1j * C_im
            dtA = dt[:, None] * A
            dC = C * (jnp.exp(dtA) - 1.0) / A
            powers = jnp.exp(dtA[:, :, None] * jnp.arange(L))
            K = 2.0 * jnp.einsum('dn,dnl->dl', dC, powers).real
            n = 2 * L
            Kf = jnp.fft.rfft(K, n=n, axis=-1)
            xf = jnp.fft.rfft(x, n=n, axis=1)
            y = jnp.fft.irfft(xf * Kf.T[None], n=n, axis=1)[:, :L]
            return y + x * D_skip
        Bb, Tt, D = x_text.shape
        Gg = x_vision.shape[1]
        Q = (x_text @ Wq).reshape(Bb, Tt, H, DH)
        K = (x_vision @ Wk).reshape(Bb, Gg, H, DH)
        scores = jnp.einsum('bthd,bghd->bhtg', Q, K) / np.sqrt(DH).astype(np.float32)
        scores = jnp.where(vision_mask[:, None, None, :], scores, -jnp.inf)
        topv, topi = jax.lax.top_k(scores, K_TOP)
        probs = jax.nn.softmax(topv, axis=-1)
        bi = jnp.arange(Bb)[:, None, None, None]
        hi = jnp.arange(H)[None, :, None, None]
        ti = jnp.arange(Tt)[None, None, :, None]
        attn = jnp.zeros_like(scores).at[bi, hi, ti, topi].set(probs)
        attn_mean = attn.mean(axis=1)
        V = x_vision @ Wv
        c_t = jnp.einsum('btg,bgd->btd', attn_mean, V)
        c_t = c_t * text_mask[..., None]
        x = layernorm(x_text, g_norm_in, b_norm_in)
        scale_in, shift_in = jnp.split(c_t @ W_film_in + b_film_in, 2, axis=-1)
        x = x * (1.0 + mod_gate * scale_in) + mod_gate * shift_in
        y = s4d(x, log_dt, A_re, A_im, C_re, C_im, D_skip)
        scale_out, shift_out = jnp.split(c_t @ W_film_out + b_film_out, 2, axis=-1)
        y = y * (1.0 + mod_gate * scale_out) + mod_gate * shift_out
        xt = x_text + y
        h = layernorm(xt, g_ffn, b_ffn)
        h = jax.nn.gelu(h @ W1 + b1, approximate=False) @ W2 + b2
        xt = xt + h
        return layernorm(xt, g_norm_out, b_norm_out)

    def _L0_ffn_ref(x, weight, ln_gamma, ln_beta):
        import jax, jax.numpy as jnp
        import numpy as np
        LN_EPS = 0.001
        EPS = 1e-05
        QB = 128.0

        def ste_round(x):
            return x + jax.lax.stop_gradient(jnp.round(x) - x)
        mu = jnp.mean(x, axis=-1, keepdims=True)
        var = jnp.var(x, axis=-1, keepdims=True)
        xn = (x - mu) * jax.lax.rsqrt(var + LN_EPS) * ln_gamma + ln_beta
        beta = jnp.mean(jnp.abs(weight))
        w_q = jnp.clip(ste_round(weight / (beta + EPS)), -1.0, 1.0)
        gamma = jnp.max(jnp.abs(xn))
        xq = jnp.clip(xn * QB / gamma, -QB + EPS, QB - EPS)
        y = jnp.einsum('bsd,du->bsu', xq, w_q)
        return y * (gamma * beta / QB)

    def _L1_xattn_ref(x, latents, mask, ln_x_g, ln_x_b, ln_l_g, ln_l_b, qn_g, kn_g, Wq, Wkv, Wlkv, Wo, bo):
        import jax, jax.numpy as jnp
        import numpy as np
        DIM_IN, DIM_LAT, DIM_HEAD = (96, 128, 64)
        INNER = max(DIM_LAT, DIM_IN)
        HEADS = INNER // DIM_HEAD
        SCALE = DIM_HEAD ** (-0.5)
        RMS_EPS = 1e-08
        LN_EPS = 1e-05

        def layernorm(x, g, b):
            mu = jnp.mean(x, axis=-1, keepdims=True)
            var = jnp.mean((x - mu) ** 2, axis=-1, keepdims=True)
            return (x - mu) * jax.lax.rsqrt(var + LN_EPS) * g + b

        def rmsnorm(x, gamma):
            norm = jnp.sqrt(jnp.sum(x * x, axis=-1, keepdims=True)) * x.shape[-1] ** (-0.5)
            return x / jnp.maximum(norm, RMS_EPS) * gamma
        b, n, _ = x.shape
        m = latents.shape[1]
        xn = layernorm(x, ln_x_g, ln_x_b)
        ln = layernorm(latents, ln_l_g, ln_l_b)
        q = ln @ Wq.T
        kv = jnp.concatenate([xn @ Wkv.T, ln @ Wlkv.T], axis=1)
        k, v = (kv[..., :INNER], kv[..., INNER:])
        split_heads = lambda t: t.reshape(t.shape[0], t.shape[1], HEADS, DIM_HEAD).transpose(0, 2, 1, 3)
        q, k, v = (split_heads(q), split_heads(k), split_heads(v))
        qn = rmsnorm(q, qn_g) * SCALE
        kn = rmsnorm(k, kn_g)
        attn = jnp.einsum('bhid,bhjd->bhij', qn, kn)
        full_mask = jnp.pad(mask, ((0, 0), (0, m)), constant_values=True)
        attn = jnp.where(full_mask[:, None, None, :], attn, -jnp.finfo(attn.dtype).max)
        attn = jax.nn.softmax(attn, axis=-1)
        out = jnp.einsum('bhij,bhjd->bhid', attn, v)
        out = out.transpose(0, 2, 1, 3).reshape(b, m, INNER)
        return out @ Wo.T + bo

    def _L1_ffn_ref(x, router_w, correction_bias, up_w, down_w, shared_up_w, shared_down_w):
        import jax, jax.numpy as jnp
        import numpy as np
        H = 128
        E = 64
        K = 8
        G = 8
        TOPK_GROUP = 4
        I_MOE = 64
        I_SHARED = 256
        SCALE = 2.5

        def relu2(x):
            return jnp.square(jax.nn.relu(x))

        def _route(xf, router_w, correction_bias):
            T = xf.shape[0]
            logits = xf @ router_w.T
            scores = jax.nn.sigmoid(logits)
            sfc = scores + correction_bias[None, :]
            grp = sfc.reshape(T, G, E // G)
            top2, _ = jax.lax.top_k(grp, 2)
            group_scores = top2.sum(-1)
            _, gidx = jax.lax.top_k(group_scores, TOPK_GROUP)
            gmask = jnp.zeros((T, G), sfc.dtype).at[jnp.arange(T)[:, None], gidx].set(1.0)
            emask = jnp.repeat(gmask, E // G, axis=1)
            masked = jnp.where(emask > 0, sfc, 0.0)
            _, tidx = jax.lax.top_k(masked, K)
            tw = jnp.take_along_axis(scores, tidx, axis=1)
            tw = tw / (tw.sum(-1, keepdims=True) + 1e-20)
            return (tidx, tw * SCALE)
        B, S, Hd = x.shape
        xf = x.reshape(-1, Hd)
        T = xf.shape[0]
        tidx, tw = _route(xf.astype(jnp.float32), router_w, correction_bias)
        combine = jnp.zeros((T, E), xf.dtype).at[jnp.arange(T)[:, None], tidx].add(tw.astype(xf.dtype))

        def body(acc, ew):
            wu, wd, c = ew
            return (acc + c[:, None] * (relu2(xf @ wu) @ wd), None)
        routed, _ = jax.lax.scan(body, jnp.zeros_like(xf), (up_w, down_w, combine.T))
        shared = relu2(xf @ shared_up_w) @ shared_down_w
        return (routed + shared).reshape(B, S, Hd)

    def _L2_xattn_ref(x, context, Wq, Wk, Wv, Wo, bo):
        import jax, jax.numpy as jnp
        import numpy as np
        HEADS = 16
        DIM_HEAD = 64
        b, n, _ = x.shape
        h, d = (HEADS, DIM_HEAD)
        scale = d ** (-0.5)
        q = (x @ Wq).reshape(b, n, h, d).transpose(0, 2, 1, 3)
        k = (context @ Wk).reshape(b, -1, h, d).transpose(0, 2, 1, 3)
        v = (context @ Wv).reshape(b, -1, h, d).transpose(0, 2, 1, 3)
        sim = jnp.einsum('bhid,bhjd->bhij', q, k) * scale
        attn = jax.nn.softmax(sim, axis=-1)
        out = jnp.einsum('bhij,bhjd->bhid', attn, v)
        out = out.transpose(0, 2, 1, 3).reshape(b, n, h * d)
        return out @ Wo + bo

    def _L2_ffn_ref(hidden_states, router_w, shared_gate_w, shared_up_w, shared_down_w, expert_gate_k, expert_up_k, expert_down_k):
        import jax, jax.numpy as jnp
        import numpy as np
        B, S, H, I, E, K = (2, 64, 128, 64, 64, 8)
        logits = jnp.einsum('bsh,he->bse', hidden_states.astype(jnp.float32), router_w)
        affinity = jax.nn.sigmoid(logits)
        top_scores, top_idx = jax.lax.top_k(affinity, K)
        top_w = top_scores / (jnp.sum(top_scores, axis=-1, keepdims=True) + 1e-09)
        one_hot = jax.nn.one_hot(top_idx, E, dtype=top_w.dtype)
        router_mask = jnp.einsum('bske,bsk->bse', one_hot, top_w).astype(hidden_states.dtype)
        shared = jnp.einsum('bsi,ih->bsh', jax.nn.silu(hidden_states @ shared_gate_w) * (hidden_states @ shared_up_w), shared_down_w)
        gate_out = jnp.einsum('bsh,ehi->bsei', hidden_states, expert_gate_k)
        up_out = jnp.einsum('bsh,ehi->bsei', hidden_states, expert_up_k)
        expert_act = jax.nn.silu(gate_out) * up_out
        routed = jnp.einsum('bsei,eih->bsh', expert_act * router_mask[..., None], expert_down_k)
        return shared + routed

    def _L3_xattn_ref(x, context, Wq, Wk, Wv, Wout, bout):
        import jax, jax.numpy as jnp
        import numpy as np
        HEADS = 8
        DIM_HEAD = 128
        ATTN_MATRIX_SCALE = 1.5
        SCALE = DIM_HEAD ** (-0.5)

        def _split_heads(t):
            b, n, _ = t.shape
            t = t.reshape(b, n, HEADS, DIM_HEAD)
            return t.transpose(2, 0, 1, 3).reshape(HEADS, b * n, DIM_HEAD)
        b, n, _ = x.shape
        qh = _split_heads(jnp.einsum('bnq,qi->bni', x, Wq))
        kh = _split_heads(jnp.einsum('bmc,ci->bmi', context, Wk))
        vh = _split_heads(jnp.einsum('bmc,ci->bmi', context, Wv))
        sim = jnp.einsum('hid,hjd->hij', qh, kh) * SCALE
        mean = jnp.mean(sim, axis=-1, keepdims=True)
        sim = (sim - mean) * ATTN_MATRIX_SCALE + mean
        attn = jax.nn.softmax(sim, axis=-1)
        out = jnp.einsum('hij,hjd->hid', attn, vh)
        out = out.reshape(HEADS, b, n, DIM_HEAD).transpose(1, 2, 0, 3)
        out = out.reshape(b, n, HEADS * DIM_HEAD)
        return jnp.einsum('bni,iq->bnq', out, Wout) + bout

    def _L3_ffn_ref(x, Wg, bg, W1, b1, W2, b2):
        import jax, jax.numpy as jnp
        import numpy as np
        D_MODEL = 128
        D_FF = 512
        NUM_EXPERTS = 8
        TOP_K = 2
        gate_logits = jnp.einsum('bsd,de->bse', x, Wg) + bg
        gate_probs = jax.nn.softmax(gate_logits, axis=-1)
        topk_probs, topk_idx = jax.lax.top_k(gate_probs, TOP_K)
        topk_probs = topk_probs / jnp.sum(topk_probs, axis=-1, keepdims=True)
        onehot = jax.nn.one_hot(topk_idx, NUM_EXPERTS, dtype=x.dtype)
        weights = jnp.einsum('bske,bsk->bse', onehot, topk_probs)
        h = jnp.einsum('bsd,edf->bsef', x, W1) + b1
        h = jax.nn.gelu(h, approximate=False)
        y = jnp.einsum('bsef,efd->bsed', h, W2) + b2
        return jnp.einsum('bsed,bse->bsd', y, weights)
    x = x + jnp.tanh(g_xattn[0]) * _L0_xattn_ref(_layernorm(x, axis=-1), ctx_768, mask_BxS_bf1, mask_BxS2_bf1, L0_xattn_Wq, L0_xattn_Wk, L0_xattn_Wv, L0_xattn_W_film_in, L0_xattn_b_film_in, L0_xattn_W_film_out, L0_xattn_b_film_out, L0_xattn_g_norm_in, L0_xattn_b_norm_in, L0_xattn_g_norm_out, L0_xattn_b_norm_out, L0_xattn_g_ffn, L0_xattn_b_ffn, L0_xattn_W1, L0_xattn_b1, L0_xattn_W2, L0_xattn_b2, L0_xattn_log_dt, L0_xattn_A_re, L0_xattn_A_im, L0_xattn_C_re, L0_xattn_C_im, L0_xattn_D_skip, L0_xattn_mod_gate)
    x = x + jnp.tanh(g_ffn[0]) * _L0_ffn_ref(_layernorm(x, axis=-1), L0_ffn_weight, L0_ffn_ln_gamma, L0_ffn_ln_beta)
    x = x + jnp.tanh(g_xattn[1]) * _L1_xattn_ref(ctx_768, _layernorm(x, axis=-1), mask_BxS2_bk0, L1_xattn_ln_x_g, L1_xattn_ln_x_b, L1_xattn_ln_l_g, L1_xattn_ln_l_b, L1_xattn_qn_g, L1_xattn_kn_g, L1_xattn_Wq, L1_xattn_Wkv, L1_xattn_Wlkv, L1_xattn_Wo, L1_xattn_bo)
    x = x + jnp.tanh(g_ffn[1]) * _L1_ffn_ref(_layernorm(x, axis=-1), L1_ffn_router_w, L1_ffn_correction_bias, L1_ffn_up_w, L1_ffn_down_w, L1_ffn_shared_up_w, L1_ffn_shared_down_w)
    x = x + jnp.tanh(g_xattn[2]) * _L2_xattn_ref(_layernorm(x, axis=-1), ctx_768, L2_xattn_Wq, L2_xattn_Wk, L2_xattn_Wv, L2_xattn_Wo, L2_xattn_bo)
    x = x + jnp.tanh(g_ffn[2]) * _L2_ffn_ref(_layernorm(x, axis=-1), L2_ffn_router_w, L2_ffn_shared_gate_w, L2_ffn_shared_up_w, L2_ffn_shared_down_w, L2_ffn_expert_gate_k, L2_ffn_expert_up_k, L2_ffn_expert_down_k)
    x = x + jnp.tanh(g_xattn[3]) * _L3_xattn_ref(_layernorm(x, axis=-1), ctx_768, L3_xattn_Wq, L3_xattn_Wk, L3_xattn_Wv, L3_xattn_Wout, L3_xattn_bout)
    x = x + jnp.tanh(g_ffn[3]) * _L3_ffn_ref(_layernorm(x, axis=-1), L3_ffn_Wg, L3_ffn_bg, L3_ffn_W1, L3_ffn_b1, L3_ffn_W2, L3_ffn_b2)
    return x

_drawn_inputs = setup_inputs


def setup_inputs(seed=0):
    import zlib

    import numpy as np

    out = dict(_drawn_inputs(seed))
    spreads = {'L0_xattn_b_film_in': (0.0, 0.1),
     'L0_xattn_b_film_out': (0.0, 0.1),
     'L0_xattn_g_norm_in': (1.0, 0.2),
     'L0_xattn_b_norm_in': (0.0, 0.1),
     'L0_xattn_g_norm_out': (1.0, 0.2),
     'L0_xattn_b_norm_out': (0.0, 0.1),
     'L0_xattn_g_ffn': (1.0, 0.6),
     'L0_xattn_b_ffn': (0.0, 0.8),
     'L0_xattn_b1': (0.0, 0.8),
     'L0_xattn_b2': (0.0, 0.284),
     'L0_xattn_A_re': (-0.5, 0.2),
     'L0_ffn_ln_gamma': (1.0, 0.6),
     'L0_ffn_ln_beta': (0.0, 0.77),
     'L1_xattn_ln_x_g': (1.0, 0.6),
     'L1_xattn_ln_x_b': (0.0, 0.8),
     'L1_xattn_ln_l_g': (1.0, 0.2),
     'L1_xattn_ln_l_b': (0.0, 0.1),
     'L1_xattn_qn_g': (1.0, 0.6),
     'L1_xattn_kn_g': (1.0, 0.6),
     'L1_xattn_bo': (0.0, 0.1),
     'L3_xattn_bout': (0.0, 0.648)}
    factors = {'g_ffn': 8.0,
     'L0_xattn_Wq': 8.0,
     'L0_xattn_Wk': 8.0,
     'L0_xattn_Wv': 5.09,
     'L0_xattn_W_film_in': 5.39,
     'L0_xattn_W_film_out': 8.0,
     'L0_xattn_W1': 3.812,
     'L0_xattn_W2': 3.346,
     'L1_xattn_Wkv': 2.705,
     'L1_ffn_router_w': 8.0,
     'L1_ffn_correction_bias': 8.0,
     'L1_ffn_up_w': 8.0,
     'L1_ffn_down_w': 8.0,
     'L1_ffn_shared_up_w': 5.1,
     'L1_ffn_shared_down_w': 4.667,
     'L2_xattn_bo': 8.0,
     'L2_ffn_router_w': 8.0,
     'L2_ffn_shared_gate_w': 8.0,
     'L2_ffn_shared_up_w': 8.0,
     'L2_ffn_shared_down_w': 8.0,
     'L2_ffn_expert_gate_k': 8.0,
     'L2_ffn_expert_up_k': 8.0,
     'L2_ffn_expert_down_k': 8.0,
     'L3_ffn_bg': 11.909,
     'L3_ffn_b1': 26.223,
     'L3_ffn_b2': 18.816}
    for name, (base, spread) in spreads.items():
        noise = np.random.default_rng([zlib.crc32(name.encode()), seed]).standard_normal(out[name].shape)
        drawn = base * np.exp(spread * noise) if base else spread * noise
        out[name] = jnp.asarray(drawn.astype(out[name].dtype))
    for name, factor in factors.items():
        out[name] = (out[name] * factor).astype(out[name].dtype)
    return out
```

```python
import concourse.bass as bass
from concourse import mybir
from contextlib import ExitStack

FP32 = mybir.dt.float32
BF16 = mybir.dt.bfloat16
U8 = mybir.dt.uint8
ALU = mybir.AluOpType
ACT = mybir.ActivationFunctionType
AX = mybir.AxisListType

BATCH, SEQ, DIM = 4, 512, 128
KEYS, CDIM = 154, 96
PART = 128
TOKENS = BATCH * SEQ
TILES = TOKENS // PART
BLOCKS = TOKENS // 512
BLOCK = 512
PER_BLOCK = BLOCK // PART
ALLKEYS = BATCH * KEYS
HALFKEYS = ALLKEYS // 2
BIG = 1.0e30
LAYERS = 4

COLS = {"ln_l_g": 1, "ln_l_b": 1, "ln_x_g": 1, "ln_x_b": 1, "tern_g": 1, "tern_b": 1, "ffn_g": 1, "ffn_b": 1,
        "b1": 4, "b2": 1, "D_skip": 1}
ROWS = {"qn_g": 64, "kn_g": 64, "L1_bo": 128, "in_g": 128, "in_b": 128, "out_g": 128, "out_b": 128,
        "mod_gate": 1, "log_dt": 128}


class Chain:

    def __init__(self, eng, sem):
        self.eng, self.sem, self.n = eng, sem, 0

    def did(self, ins):
        ins.then_inc(self.sem, 1)
        self.n += 1

    def wait(self):
        if self.n:
            self.eng.wait_ge(self.sem, self.n)

    def wait_for(self, n):
        if n:
            self.eng.wait_ge(self.sem, n)

    def clear(self):
        self.wait()
        self.eng.sem_clear(self.sem)
        self.n = 0


START = 1


def start(eng, *semaphores):
    for s in semaphores:
        eng.sem_inc(s, START)


class Memory:

    def __init__(self, nc, ctx):
        def sb(name, shape, dt=FP32):
            return ctx.enter_context(nc.sbuf_tensor(name, shape, dt))

        self.x = sb("x_tokens", [PART, TILES, DIM])
        self.xn = sb("x_norm", [PART, TILES, DIM])
        self.xt = sb("x_norm_T", [DIM, TOKENS + 2 * PART])
        self.ident = sb("ident", [PART, PART])
        self.ctxT = sb("ctx_T", [CDIM, ALLKEYS])
        self.gate = sb("gate", [PART, 2 * LAYERS])
        self.cols = sb("col_vectors", [PART, sum(COLS.values())])
        self.rows = sb("row_vectors", [PART, sum(ROWS.values())])

        self.semaphores = []

    def semaphore(self, nc, name):
        self.semaphores.append(nc.alloc_semaphore(name=name))
        return self.semaphores[-1]

    def clear_semaphores(self, nc):
        share = lambda n: self.semaphores[n::4]
        with nc.Block() as block:
            @block.scalar
            def _(act):
                for s in share(0):
                    act.sem_clear(s)

            @block.vector
            def _(dve):
                for s in share(1):
                    dve.sem_clear(s)

            @block.tensor
            def _(pe):
                for s in share(2):
                    pe.sem_clear(s)

            @block.gpsimd
            def _(pool):
                for s in share(3):
                    pool.sem_clear(s)
        for s in self.semaphores:
            nc.release_semaphore(s)
        self.semaphores = []

    @staticmethod
    def _at(names, name):
        first = 0
        for n, width in names.items():
            if n == name:
                return slice(first, first + width)
            first += width
        raise KeyError(name)

    def col(self, name):
        return self.cols[:, self._at(COLS, name)]

    def row(self, name):
        return self.rows[:, self._at(ROWS, name)]


def setup(nc, m, a):
    with ExitStack() as ctx:
        sem = lambda n: m.semaphore(nc, n)
        x_in, small_in, g_in = sem("x_in"), sem("small_in"), sem("g_in")
        vectors_in = sem("vectors_in")
        ident_steps, gate_done = sem("ident_steps"), sem("gate_done")
        ctx_sb = ctx.enter_context(nc.sbuf_tensor("ctx_rows", [KEYS // 2, 2 * BATCH, CDIM], FP32))
        graw = ctx.enter_context(nc.sbuf_tensor("gate_raw", [PART, 2 * LAYERS], FP32))
        ctx_ps = ctx.enter_context(nc.psum_tensor("ctx_ps", [PART, 2 * 512], FP32))
        ctx_turned, ctx_kept = sem("ctx_turned"), sem("ctx_kept")
        HK = KEYS // 2
        with nc.Block() as block:
            @block.sync
            def _(sp):
                sp.dma_start(ctx_sb[:], a["ctx_768"].rearrange("b (u k) c -> k (b u) c", k=HK)).then_inc(small_in, 16)
                sp.dma_start(m.x[:], a["x"].rearrange("b (j p) d -> p (b j) d", p=PART)).then_inc(x_in, 16)
                sp.wait_ge(x_in, 16)

            @block.scalar
            def _(act):
                for n, name in enumerate(("g_xattn", "g_ffn")):
                    act.dma_start(graw[:, n * LAYERS:(n + 1) * LAYERS],
                                  a[name].rearrange("(o n) -> o n", o=1).to_broadcast([PART, LAYERS])).then_inc(g_in, 16)
                act.dma_start(m.cols[:], a["columns"]).then_inc(vectors_in, 16)
                act.dma_start(m.rows[:], a["rows"].rearrange("(o n) -> o n", o=1).to_broadcast([PART, sum(ROWS.values())])).then_inc(vectors_in, 16)
                act.wait_ge(vectors_in, 32)
                act.wait_ge(g_in, 32)
                nc.scalar.activation(m.gate[:], graw[:], ACT.Tanh).then_inc(gate_done, 1)

            @block.gpsimd
            def _(pool):
                pool.memset(m.ident[:], 0.0).then_inc(ident_steps, 1)
                pool.wait_ge(ident_steps, 1)
                pool.affine_select(out=m.ident[:], in_=m.ident[:], compare_op=ALU.not_equal, fill=1.0, base=0,
                                   pattern=[[-1, PART]], channel_multiplier=1).then_inc(ident_steps, 1)
                pool.memset(m.xt[:, TOKENS:], 0.0).then_inc(ident_steps, 1)

            @block.tensor
            def _(pe):
                pe.wait_ge(ident_steps, 2)
                pe.wait_ge(small_in, 16)
                for u in range(2 * BATCH):
                    bank, at = divmod(u, 4)
                    pe.transpose(ctx_ps[0:CDIM, bank * 512 + at * HK:bank * 512 + at * HK + HK], ctx_sb[:, u, :],
                                 m.ident[0:HK, 0:HK]).then_inc(ctx_turned, 1)

            @block.vector
            def _(dve):
                for bank in range(2):
                    dve.wait_ge(ctx_turned, 4 * (bank + 1))
                    dve.tensor_copy(m.ctxT[:, bank * HALFKEYS:(bank + 1) * HALFKEYS],
                                    ctx_ps[0:CDIM, bank * 512:bank * 512 + HALFKEYS]).then_inc(ctx_kept, 1)


def norm(nc, m, name, src, eps, dst, turned_to=None, T_scale=None, T_bias=None):
    with ExitStack() as ctx:
        sb = lambda n, s: ctx.enter_context(nc.sbuf_tensor(f"{name}_{n}", s, FP32))
        sem = lambda n: m.semaphore(nc, f"{name}_{n}")
        stats, moments = sb("stats", [PART, TILES, 6]), sb("moments", [PART, TILES, 2])
        var, sd, rstd = sb("var", [PART, TILES]), sb("sd", [PART, TILES]), sb("rstd", [PART, TILES])
        stats_done, moments_done, var_done, sd_done = sem("stats_done"), sem("moments_done"), sem("var_done"), sem("sd_done")
        rstd_done, normed, turned, kept = sem("rstd_done"), sem("normed"), sem("turned"), sem("kept")
        turn = ctx.enter_context(nc.psum_tensor(f"{name}_turn", [PART, BLOCKS, BLOCK], FP32)) if turned_to is not None else None
        with nc.Block() as block:
            @block.vector
            def _(dve):
                for i in range(TILES):
                    dve.bn_stats(stats[:, i, :], src[:, i, :]).then_inc(stats_done, 1)
                for i in range(TILES):
                    dve.wait_ge(stats_done, i + 1)
                    dve.bn_aggr(moments[:, i, :], stats[:, i, :]).then_inc(moments_done, 1)
                dve.wait_ge(moments_done, TILES)
                dve.tensor_scalar(var[:], moments[:, :, 1], eps, None, ALU.add).then_inc(var_done, 1)
                dve.wait_ge(sd_done, 1)
                dve.reciprocal(rstd[:], sd[:]).then_inc(rstd_done, 1)
                dve.wait_ge(rstd_done, 1)
                for i in range(TILES):
                    dve.tensor_scalar(dst[:, i, :], src[:, i, :], moments[:, i, 0:1], rstd[:, i:i + 1],
                                      ALU.subtract, ALU.mult).then_inc(normed, 1)

            @block.scalar
            def _(act):
                act.wait_ge(var_done, 1)
                nc.scalar.activation(sd[:], var[:], ACT.Sqrt).then_inc(sd_done, 1)
                if turned_to is not None:
                    for t in range(BLOCKS):
                        act.wait_ge(turned, PER_BLOCK * (t + 1))
                        nc.scalar.activation(turned_to[:, t * BLOCK:(t + 1) * BLOCK], turn[:, t, :], ACT.Identity,
                                             scale=1.0 if T_scale is None else T_scale,
                                             bias=0.0 if T_bias is None else T_bias).then_inc(kept, 1)

            @block.tensor
            def _(pe):
                if turned_to is not None:
                    for i in range(TILES):
                        pe.wait_ge(normed, i + 1)
                        pe.transpose(turn[:, i // PER_BLOCK, i % PER_BLOCK * PART:(i % PER_BLOCK + 1) * PART],
                                     dst[:, i, :], m.ident[:]).then_inc(turned, 1)


class Mixture:

    def __init__(self, kind, layer, prefix, experts, norm_eps=1e-5):
        self.kind, self.layer, self.prefix, self.experts = kind, layer, prefix, experts
        self.hidden = 4096 // experts


def moe(nc, m, a, mix):
    E, kind, p = mix.experts, mix.kind, mix.prefix
    CHUNKS, SLOTS = 32, 4
    TURNS = CHUNKS // SLOTS
    with ExitStack() as ctx:
        sb = lambda n, s, dt=FP32: ctx.enter_context(nc.sbuf_tensor(f"{p}_{n}", s, dt))
        sem = lambda n: m.semaphore(nc, f"{p}_{n}")
        share_dram = nc.dram_tensor(f"{p}_shares", (E, TOKENS), FP32, kind="Internal").ap()
        shareT = sb("share_T", [E, TOKENS])
        route(nc, m, a, mix, shareT, share_dram)

        share = sb("share", [PART, 1 if kind == "gelu" else 2, TOKENS])
        SHARES = BLOCKS if kind == "gelu" else 2
        share_in = [sem(f"share_in{j}") for j in range(SHARES)]
        up = sb("up", [DIM, SLOTS, PART])
        up2 = sb("up2", [DIM, SLOTS, PART]) if kind == "swiglu" else None
        down = sb("down", [PART, SLOTS, DIM])
        bias = sb("hidden_bias", [PART, CHUNKS + SLOTS]) if kind == "gelu" else None
        bias_now = sb("hidden_bias_now", [PART, SLOTS]) if kind == "gelu" else None
        act_a = sb("act_a", [PART, 2, BLOCK])
        act_b = sb("act_b", [PART, 2, BLOCK])
        hidden = sb("hidden", [PART, 2, BLOCK])
        y = sb("y", [PART, TOKENS])
        ps_acc = ctx.enter_context(nc.psum_tensor(f"{p}_acc", [PART, BLOCKS, BLOCK], FP32))
        ps_h = ctx.enter_context(nc.psum_tensor(f"{p}_h", [PART, 4, BLOCK], FP32))
        w_in, w_used = [sem(f"w_in{j}") for j in range(SLOTS)], sem("w_used")
        h_ready = sem("h_ready")
        act_ready, act2_ready, hid_ready, hid_used = sem("act_ready"), sem("act2_ready"), sem("hid_ready"), sem("hid_used")
        first_h, first_act, first_used = sem("first_h"), sem("first_act"), sem("first_used")
        acc_kept, y_turned, x_added = sem("acc_kept"), sem("y_turned"), sem("x_added")
        first_in = sem("first_in")
        bias_set = sem("bias_set")
        UNITS = SLOTS * BLOCKS
        LOADS = 3 if kind == "swiglu" else 2
        FIRST_LOADS = {"relu2": 2, "swiglu": 3, "gelu": 2}[kind]
        first_relu = sem("first_relu")

        def up_rows(c, turn, j):
            if kind == "relu2":
                return [a[p + "_up_w"][bass.ds(c * 2, 2)].rearrange("e h i -> h e i")]
            if kind == "swiglu":
                return [a[p + "_expert_gate_k"][bass.ds(c * 2, 2)].rearrange("e h i -> h e i"),
                        a[p + "_expert_up_k"][bass.ds(c * 2, 2)].rearrange("e h i -> h e i")]
            return [a[p + "_W1"][bass.ds(turn, 1), :, j * PART:(j + 1) * PART].rearrange("o h i -> h o i")]

        if kind == "relu2":
            down_all = a[p + "_down_w"].rearrange("e i h -> (e i) h")
        elif kind == "swiglu":
            down_all = a[p + "_expert_down_k"].rearrange("e i h -> (e i) h")
        else:
            down_all = a[p + "_W2"].rearrange("e i h -> (e i) h")
        SHARED = {"relu2": [PART, PART], "swiglu": [64], "gelu": []}[kind]
        if SHARED:
            s_up = sb("shared_up", [DIM, len(SHARED), SHARED[0]])
            s_up2 = sb("shared_up2", [DIM, 1, 64]) if kind == "swiglu" else None
            s_down = sb("shared_down", [SHARED[0], len(SHARED), DIM])
        else:
            s_down = sb("bias_down", [8, DIM])

        with nc.Block() as block:
            @block.sync
            def _(sp):
                if kind == "relu2":
                    sp.dma_start(s_up[:], a[p + "_shared_up_w"].rearrange("h (c i) -> h c i", i=PART)).then_inc(first_in, 16)
                    sp.dma_start(s_down[:], a[p + "_shared_down_w"].rearrange("(c i) h -> i c h", i=PART)).then_inc(first_in, 16)
                elif kind == "swiglu":
                    sp.dma_start(s_up[:, 0, :], a[p + "_shared_gate_w"]).then_inc(first_in, 16)
                    sp.dma_start(s_up2[:, 0, :], a[p + "_shared_up_w"]).then_inc(first_in, 16)
                    sp.dma_start(s_down[:, 0, :], a[p + "_shared_down_w"]).then_inc(first_in, 16)
                else:
                    sp.dma_start(s_down[:], a[p + "_b2"]).then_inc(first_in, 16)
                    sp.dma_start(bias[:, 0:CHUNKS], a[p + "_b1"]).then_inc(first_in, 16)

                def load(j, turn):
                    c = turn * SLOTS + j
                    for w, rows in zip((up, up2), up_rows(c, turn, j)):
                        sp.dma_start(w[:, j, :].rearrange("p (e i) -> p e i", e=rows.shape[1]), rows).then_inc(w_in[j], 16)
                    sp.dma_start(down[:, j, :], down_all[bass.ds(c * PART, PART), :]).then_inc(w_in[j], 16)

                def load_share(j, turn):
                    for e in range(2):
                        row = share_dram[bass.ds((turn * SLOTS + j) * 2 + e, 1), :].to_broadcast([64, TOKENS])
                        sp.dma_start(share[e * 64:(e + 1) * 64, j % 2, :], row).then_inc(share_in[j % 2], 16)

                def load_share_block(t, turn):
                    row = share_dram[bass.ds(turn, 1), t * BLOCK:(t + 1) * BLOCK].to_broadcast([PART, BLOCK])
                    sp.dma_start(share[:, 0, t * BLOCK:(t + 1) * BLOCK], row).then_inc(share_in[t], 16)

                for j in range(SLOTS):
                    load(j, 0)
                    if kind == "gelu":
                        load_share_block(j, 0)
                    elif j < 2:
                        load_share(j, 0)
                with sp.Fori(0, TURNS - 1) as it:
                    for j in range(SLOTS):
                        sp.wait_ge(w_used, it * SLOTS + j + 1 + START)
                        load(j, it + 1)
                        if kind == "gelu":
                            if j == SLOTS - 2:
                                for t in range(BLOCKS):
                                    sp.wait_ge(hid_ready, (it + 1) * UNITS - (BLOCKS - 1 - t) + START)
                                    load_share_block(t, it + 1)
                        else:
                            load_share(*((j + 2, it) if j < 2 else (j - 2, it + 1)))
                if kind != "gelu":
                    for j in range(2):
                        sp.wait_ge(w_used, (TURNS - 1) * SLOTS + j + 1 + START)
                        load_share(j + 2, TURNS - 1)
                sp.wait_ge(w_used, (TURNS - 1) * SLOTS + 1 + START)
                load(0, 0)
                sp.wait_ge(w_in[0], 16 * LOADS * (TURNS + 1))


            @block.tensor
            def _(pe):
                start(pe, hid_used, w_used)
                pe.wait_ge(first_in, 16 * FIRST_LOADS)
                if kind == "gelu":
                    for t in range(BLOCKS):
                        pe.matmul(ps_acc[:, t, :], s_down[:], shareT[0:8, t * BLOCK:(t + 1) * BLOCK], start=True, stop=False,
                                  skip_group_check=True)
                else:
                    n = 0
                    for s, width in enumerate(SHARED):
                        for t in range(BLOCKS):
                            if n >= 2 or (kind == "swiglu" and n):
                                pe.wait_ge(first_act, n - 1 if kind == "relu2" else n)
                            rhs = m.xt[:, t * BLOCK:(t + 1) * BLOCK]
                            if kind == "relu2":
                                pe.matmul(ps_h[0:width, n % 2, :], s_up[:, s, :], rhs, start=True, stop=True).then_inc(first_h, 1)
                            else:
                                pe.matmul(ps_h[0:width, 0, :], s_up[:, s, :], rhs, start=True, stop=True)
                                pe.matmul(ps_h[0:width, 1, :], s_up2[:, s, :], rhs, start=True, stop=True).then_inc(first_h, 1)
                            pe.wait_ge(first_act, n + 1)
                            pe.matmul(ps_acc[:, t, :], s_down[0:width, s, :], hidden[0:width, n % 2, :],
                                      start=(s == 0), stop=False, skip_group_check=True).then_inc(first_used, 1)
                            n += 1

                def products(it, k, first=False):
                    j, t = divmod(k, BLOCKS)
                    n = it * UNITS + k
                    rhs = m.xt[:, t * BLOCK:(t + 1) * BLOCK]
                    if t == 0:
                        pe.wait_ge(w_in[j], (it + 1) * (16 * LOADS))
                    if kind == "swiglu":
                        bank = k % 2 * 2
                        if not first:
                            pe.wait_ge(act_ready, n - 1 + START)
                        pe.matmul(ps_h[:, bank, :], up[:, j, :], rhs, start=True, stop=True).then_inc(h_ready, 1)
                        if not first:
                            pe.wait_ge(act2_ready, n - 1 + START)
                        pe.matmul(ps_h[:, bank + 1, :], up2[:, j, :], rhs, start=True, stop=True).then_inc(h_ready, 1)
                    else:
                        if not first:
                            pe.wait_ge(act_ready, n - 1 + START)
                        pe.matmul(ps_h[:, k % 4, :], up[:, j, :], rhs, start=True, stop=True).then_inc(h_ready, 1)

                products(0, 0, first=True)
                products(0, 1, first=True)
                with pe.Fori(0, TURNS) as it:
                    for k in range(UNITS):
                        j, t = divmod(k, BLOCKS)
                        products(it, k + 2) if k + 2 < UNITS else products(it + 1, k + 2 - UNITS)
                        pe.wait_ge(hid_ready, it * UNITS + k + 1 + START)
                        mm = pe.matmul(ps_acc[:, t, :], down[:, j, :], hidden[:, k % 2, :], start=False, stop=False,
                                       skip_group_check=True)
                        mm.then_inc(w_used if t == BLOCKS - 1 else hid_used, 1)
                for t in range(BLOCKS):
                    pe.wait_ge(acc_kept, t + 1)
                    if t >= 2:
                        pe.wait_ge(x_added, t - 1)
                    for at in range(PER_BLOCK):
                        i = t * PER_BLOCK + at
                        mm = pe.transpose(ps_h[:, t % 2, at * PART:(at + 1) * PART], y[:, i * PART:(i + 1) * PART], m.ident[:])
                    mm.then_inc(y_turned, 1)

            @block.scalar
            def _(act):
                start(act, act_ready, *([act2_ready] if kind == "relu2" else []))
                n = 0
                for s, width in enumerate(SHARED):
                    for t in range(BLOCKS):
                        act.wait_ge(first_h, n + 1)
                        if kind == "relu2":
                            nc.scalar.activation(act_a[:, n % 2, :], ps_h[:, n % 2, :], ACT.Relu).then_inc(first_relu, 1)
                            if n >= 2:
                                act.wait_ge(first_used, n - 1)
                            act.wait_ge(first_relu, n + 1)
                            nc.scalar.activation(hidden[:, n % 2, :], act_a[:, n % 2, :], ACT.Square).then_inc(first_act, 1)
                        else:
                            if n:
                                act.wait_ge(first_act, n)
                            nc.scalar.activation(act_a[0:width, 0, :], ps_h[0:width, 0, :], ACT.Silu).then_inc(first_relu, 1)
                        n += 1
                if kind == "relu2":
                    act.wait_ge(first_act, n)
                with act.Fori(0, TURNS) as it:
                    for k in range(UNITS):
                        n = it * UNITS + k
                        if kind == "swiglu":
                            act.wait_ge(h_ready, it * (2 * UNITS) + 2 * k + 1)
                            act.wait_ge(act2_ready, it * UNITS + max(k - 1, 0) + START)
                            nc.scalar.activation(act_a[:, k % 2, :], ps_h[:, k % 2 * 2, :], ACT.Silu).then_inc(act_ready, 1)
                        elif kind == "relu2":
                            act.wait_ge(act2_ready, it * UNITS + max(k - 1, 0) + START)
                            act.wait_ge(h_ready, n + 1)
                            nc.scalar.activation(act_a[:, k % 2, :], ps_h[:, k % 4, :], ACT.Relu).then_inc(act_ready, 1)
                            act.wait_ge(act_ready, n + 1 + START)
                            act.wait_ge(hid_ready, it * UNITS + max(k - 1, 0) + START)
                            nc.scalar.activation(act_b[:, k % 2, :], act_a[:, k % 2, :], ACT.Square).then_inc(act2_ready, 1)
                        else:
                            act.wait_ge(hid_ready, it * UNITS + max(k - 1, 0) + START)
                            act.wait_ge(h_ready, n + 1)
                            j = k // BLOCKS
                            if k % BLOCKS == 0:
                                act.wait_ge(bias_set, it * SLOTS + j + 2)
                            nc.scalar.activation(act_b[:, k % 2, :], ps_h[:, k % 4, :], ACT.Gelu,
                                                 bias=bias_now[:, j:j + 1]).then_inc(act_ready, 1)
                for t in range(BLOCKS):
                    act.wait_ge(w_used, CHUNKS + START)
                    nc.scalar.activation(y[:, t * BLOCK:(t + 1) * BLOCK], ps_acc[:, t, :], ACT.Copy).then_inc(acc_kept, 1)

            @block.vector
            def _(dve):
                start(dve, hid_ready, *([act2_ready] if kind == "swiglu" else []))
                if kind == "swiglu":
                    for n in range(BLOCKS):
                        dve.wait_ge(first_relu, n + 1)
                        if n >= 2:
                            dve.wait_ge(first_used, n - 1)
                        dve.tensor_tensor(hidden[0:64, n % 2, :], act_a[0:64, 0, :], ps_h[0:64, 1, :],
                                          ALU.mult).then_inc(first_act, 1)
                    dve.wait_ge(first_used, BLOCKS)
                elif kind == "relu2":
                    dve.wait_ge(first_used, 2 * BLOCKS)
                if kind == "gelu":
                    dve.memset(bias[:, CHUNKS:], 0.0).then_inc(bias_set, 1)
                    dve.wait_ge(first_in, 16 * FIRST_LOADS)
                    dve.wait_ge(bias_set, 1)
                    for j in range(SLOTS - 1):
                        dve.tensor_copy(bias_now[:, j:j + 1], bias[:, j:j + 1]).then_inc(bias_set, 1)
                    dve.tensor_copy(bias_now[:, SLOTS - 1:], bias[:, SLOTS - 1:SLOTS]).then_inc(bias_set, 1)
                with dve.Fori(0, TURNS) as it:
                    for k in range(UNITS):
                        n = it * UNITS + k
                        if kind == "swiglu":
                            dve.wait_ge(act_ready, n + 1 + START)
                            dve.wait_ge(h_ready, it * (2 * UNITS) + 2 * k + 2)
                            dve.wait_ge(hid_ready, it * UNITS + max(k - 1, 0) + START)
                            dve.tensor_tensor(act_b[:, k % 2, :], act_a[:, k % 2, :], ps_h[:, k % 2 * 2 + 1, :],
                                              ALU.mult).then_inc(act2_ready, 1)
                            dve.wait_ge(act2_ready, n + 1 + START)
                        elif kind == "relu2":
                            dve.wait_ge(act2_ready, n + 1 + START)
                        else:
                            dve.wait_ge(act_ready, n + 1 + START)
                        j, t = divmod(k, BLOCKS)
                        if kind == "gelu":
                            if j == 0:
                                dve.wait_ge(share_in[t], (it + 1) * 16)
                        elif t == 0:
                            dve.wait_ge(share_in[j % 2], (it * 2 + j // 2 + 1) * 32)
                        before = k - 2
                        if before >= 0:
                            tj, tt = divmod(before, BLOCKS)
                            if tt == BLOCKS - 1:
                                dve.wait_ge(w_used, it * SLOTS + tj + 1 + START)
                            else:
                                dve.wait_ge(hid_used, it * (UNITS - SLOTS) + tj * (BLOCKS - 1) + tt + 1 + START)
                        elif k == 0:
                            dve.wait_ge(hid_used, it * (UNITS - SLOTS) + START)
                        else:
                            dve.wait_ge(w_used, it * SLOTS + START)
                        dve.tensor_tensor(hidden[:, k % 2, :], act_b[:, k % 2, :],
                                          share[:, 0 if kind == "gelu" else j % 2, t * BLOCK:(t + 1) * BLOCK],
                                          ALU.mult).then_inc(hid_ready, 1)
                        if kind == "gelu" and k % BLOCKS == BLOCKS - 1:
                            j = k // BLOCKS
                            dve.tensor_scalar(bias_now[:, j:j + 1], bias[:, bass.ds(it * SLOTS + (SLOTS + j), 1)], 1.0, None,
                                              ALU.mult).then_inc(bias_set, 1)
                for t in range(BLOCKS):
                    dve.wait_ge(y_turned, t + 1)
                    rows = m.x[:, t * PER_BLOCK:(t + 1) * PER_BLOCK, :].rearrange("p t d -> p (t d)")
                    dve.scalar_tensor_tensor(rows, ps_h[:, t % 2, :], m.gate[:, LAYERS + mix.layer:LAYERS + mix.layer + 1],
                                             rows, ALU.mult, ALU.add).then_inc(x_added, 1)


def route(nc, m, a, mix, shareT, share_dram):
    E, kind, p = mix.experts, mix.kind, mix.prefix
    with ExitStack() as ctx:
        sb = lambda n, s, dt=FP32: ctx.enter_context(nc.sbuf_tensor(f"{p}_r_{n}", s, dt))
        sem = lambda n: m.semaphore(nc, f"{p}_r_{n}")
        router = sb("router", [DIM, E])
        offset = sb("offset", [PART, E])
        earlier = sb("earlier", [PART, 8, 8])
        score, pick = sb("score", [PART, TILES, E]), sb("pick", [PART, TILES, E])
        work, work2 = sb("work", [PART, TILES, E]), sb("work2", [PART, TILES, E])
        pair, pair2 = sb("pair", [PART, TILES, 64]), sb("pair2", [PART, TILES, 64])
        one, two, three = sb("one", [PART, TILES, 8]), sb("two", [PART, TILES, 8]), sb("three", [PART, TILES, 8])
        top = sb("top", [PART, TILES, 8])
        total = sb("total", [PART, TILES])
        logits = ctx.enter_context(nc.psum_tensor(f"{p}_logits", [PART, TILES, E], FP32))
        turn = ctx.enter_context(nc.psum_tensor(f"{p}_turn", [PART, 4, BLOCK], FP32))
        router_in, offset_in, router_turned, router_kept = sem("router_in"), sem("offset_in"), sem("router_turned"), sem("router_kept")
        logits_ready, score_ready, steps, acts = sem("logits_ready"), sem("score_ready"), sem("steps"), sem("acts")
        shares_ready, turned, kept, built, shares_out = sem("shares_ready"), sem("turned"), sem("kept"), sem("built"), sem("shares_out")
        rowsT = sb("router_rows", [64, DIM]) if kind == "relu2" else None

        with nc.Block() as block:
            @block.sync
            def _(sp):
                if kind == "relu2":
                    sp.dma_start(rowsT[:], a[p + "_router_w"]).then_inc(router_in, 16)
                    sp.dma_start(offset[:], a[p + "_correction_bias"].rearrange("(o e) -> o e", o=1).to_broadcast([PART, E])).then_inc(offset_in, 16)
                elif kind == "swiglu":
                    sp.dma_start(router[:], a[p + "_router_w"]).then_inc(router_in, 16)
                else:
                    sp.dma_start(router[:], a[p + "_Wg"]).then_inc(router_in, 16)
                    sp.dma_start(offset[:], a[p + "_bg"].rearrange("(o e) -> o e", o=1).to_broadcast([PART, E])).then_inc(offset_in, 16)
                sp.wait_ge(router_in, 16)
                for t in range(BLOCKS):
                    sp.wait_ge(kept, t + 1)
                    sp.dma_start(share_dram[:, t * BLOCK:(t + 1) * BLOCK], shareT[:, t * BLOCK:(t + 1) * BLOCK]).then_inc(shares_out, 16)
                sp.wait_ge(shares_out, 16 * BLOCKS)

            @block.gpsimd
            def _(pool):
                made = Chain(pool, built)
                made.did(pool.memset(earlier[:], 1.0))
                made.wait()
                made.did(pool.affine_select(out=earlier[:], in_=earlier[:], compare_op=ALU.is_gt, fill=0.0, base=0,
                                            pattern=[[1, 8], [-1, 8]], channel_multiplier=0))
                made.wait()

            @block.tensor
            def _(pe):
                pe.wait_ge(router_in, 16)
                if kind == "relu2":
                    pe.transpose(turn[:, 0, 0:64], rowsT[:], m.ident[0:64, 0:64]).then_inc(router_turned, 1)
                    pe.wait_ge(router_kept, 1)
                for i in range(TILES):
                    pe.matmul(logits[:, i, :], m.xt[:, i * PART:(i + 1) * PART], router[:], start=True,
                              stop=True).then_inc(logits_ready, 1)
                pe.wait_ge(shares_ready, 1)
                for i in range(TILES):
                    pe.transpose(turn[0:E, i // 4, i % 4 * PART:(i % 4 + 1) * PART], work[:, i, :], m.ident[:]).then_inc(turned, 1)

            @block.scalar
            def _(act):
                if kind != "gelu":
                    act.wait_ge(logits_ready, TILES)
                    nc.scalar.activation(score[:], logits[:], ACT.Sigmoid).then_inc(score_ready, 1)
                else:
                    act.wait_ge(score_ready, 1)
                    nc.scalar.activation(score[:], work[:], ACT.Exp).then_inc(score_ready, 1)
                for t in range(BLOCKS):
                    act.wait_ge(turned, 4 * (t + 1))
                    nc.scalar.activation(shareT[:, t * BLOCK:(t + 1) * BLOCK], turn[0:E, t, :], ACT.Copy).then_inc(kept, 1)

            @block.vector
            def _(dve):
                c = Chain(dve, steps)
                step = lambda ins: (c.did(ins), c.wait())

                def by_pairs(values, rank):
                    mine = values.unsqueeze(3).to_broadcast([PART, TILES, 8, 8])
                    other = values.unsqueeze(2).to_broadcast([PART, TILES, 8, 8])
                    v1 = pair[:].rearrange("p t (i j) -> p t i j", i=8)
                    v2 = pair2[:].rearrange("p t (i j) -> p t i j", i=8)
                    step(dve.tensor_tensor(v1, other, mine, ALU.is_equal))
                    step(dve.tensor_tensor(v1, v1, earlier[:].unsqueeze(1).to_broadcast([PART, TILES, 8, 8]), ALU.mult))
                    step(dve.tensor_tensor(v2, other, mine, ALU.is_gt))
                    step(dve.tensor_tensor(v1, v1, v2, ALU.add))
                    step(dve.tensor_reduce(rank, v1, AX.X, ALU.add))

                def top8():
                    for i in range(TILES):
                        c.did(dve.max(top[:, i, :], work[:, i, :]))
                    c.wait()
                    for i in range(TILES):
                        c.did(dve.match_replace(work2[:, i, :], top[:, i, :], work[:, i, :], -BIG))
                    c.wait()
                    step(dve.tensor_tensor(pick[:], work2[:], work[:], ALU.is_lt))

                if kind == "relu2":
                    dve.wait_ge(router_turned, 1)
                    dve.tensor_copy(router[:], turn[:, 0, 0:64]).then_inc(router_kept, 1)
                    dve.wait_ge(offset_in, 16)
                    dve.wait_ge(score_ready, 1)
                    step(dve.tensor_tensor(work[:], score[:], offset[:].unsqueeze(1).to_broadcast([PART, TILES, E]), ALU.add))
                    grouped = lambda v: v[:].rearrange("p t (g e) -> p t g e", g=8)
                    wide = lambda v: v[:].unsqueeze(3).to_broadcast([PART, TILES, 8, 8])
                    step(dve.tensor_reduce(one[:], grouped(work), AX.X, ALU.max))
                    step(dve.tensor_tensor(grouped(pick), grouped(work), wide(one), ALU.is_equal))
                    step(dve.tensor_reduce(two[:], grouped(pick), AX.X, ALU.add))
                    step(dve.scalar_tensor_tensor(work2[:], pick[:], -BIG, work[:], ALU.mult, ALU.add))
                    step(dve.tensor_reduce(three[:], grouped(work2), AX.X, ALU.max))
                    step(dve.tensor_scalar(two[:], two[:], 1.5, -BIG, ALU.is_lt, ALU.mult))
                    step(dve.tensor_tensor(two[:], two[:], one[:], ALU.add))
                    step(dve.tensor_tensor(three[:], three[:], two[:], ALU.max))
                    step(dve.tensor_tensor(one[:], one[:], three[:], ALU.add))
                    dve.wait_ge(built, 2)
                    by_pairs(one[:], two[:])
                    step(dve.tensor_scalar(two[:], two[:], 3.5, None, ALU.is_lt))
                    step(dve.tensor_tensor(grouped(work), grouped(work), wide(two), ALU.mult))
                    top8()
                    step(dve.tensor_tensor(work[:], score[:], pick[:], ALU.mult))
                    step(dve.tensor_reduce(total[:], work[:], AX.X, ALU.add))
                    step(dve.tensor_scalar(total[:], total[:], 1e-20, None, ALU.add))
                    step(dve.reciprocal(total[:], total[:]))
                    step(dve.tensor_scalar(total[:], total[:], 2.5, None, ALU.mult))
                elif kind == "swiglu":
                    dve.wait_ge(score_ready, 1)
                    step(dve.tensor_copy(work[:], score[:]))
                    top8()
                    step(dve.tensor_tensor(work[:], score[:], pick[:], ALU.mult))
                    step(dve.tensor_reduce(total[:], work[:], AX.X, ALU.add))
                    step(dve.tensor_scalar(total[:], total[:], 1e-9, None, ALU.add))
                    step(dve.reciprocal(total[:], total[:]))
                else:
                    dve.wait_ge(offset_in, 16)
                    dve.wait_ge(logits_ready, TILES)
                    row = lambda: total[:].unsqueeze(2).to_broadcast([PART, TILES, E])
                    step(dve.tensor_tensor(work[:], logits[:], offset[:].unsqueeze(1).to_broadcast([PART, TILES, E]), ALU.add))
                    step(dve.tensor_reduce(total[:], work[:], AX.X, ALU.max))
                    dve.tensor_tensor(work[:], work[:], row(), ALU.subtract).then_inc(score_ready, 1)
                    dve.wait_ge(score_ready, 2)
                    dve.wait_ge(built, 2)
                    step(dve.tensor_reduce(total[:], score[:], AX.X, ALU.add))
                    step(dve.reciprocal(total[:], total[:]))
                    step(dve.tensor_tensor(score[:], score[:], row(), ALU.mult))
                    by_pairs(score[:], work2[:])
                    step(dve.tensor_scalar(pick[:], work2[:], 1.5, None, ALU.is_lt))
                    step(dve.tensor_tensor(work[:], score[:], pick[:], ALU.mult))
                    step(dve.tensor_reduce(total[:], work[:], AX.X, ALU.add))
                    step(dve.reciprocal(total[:], total[:]))
                dve.tensor_tensor(work[:], work[:], total[:].unsqueeze(2).to_broadcast([PART, TILES, E]), ALU.mult).then_inc(shares_ready, 1)



class Attention:

    def __init__(self, layer, prefix, heads, head_dim, heads_in_unit, scale):
        self.layer, self.prefix, self.heads, self.head_dim = layer, prefix, heads, head_dim
        self.G, self.scale = heads_in_unit, scale
        self.units = heads // heads_in_unit if heads_in_unit == 1 else heads // 4
        self.by_batch = heads_in_unit > 1


UNIT = ALLKEYS
UCHUNKS = 5
ULAST = UNIT - 4 * PART


def attention(nc, m, a, at):
    p, H, DH, G, U = at.prefix, at.heads, at.head_dim, at.G, at.units
    with ExitStack() as ctx:
        keysT = ctx.enter_context(nc.sbuf_tensor(f"{p}_keys_T", [DIM, H * ALLKEYS // (1 if G == 1 else 1)], FP32)) \
            if G == 1 else ctx.enter_context(nc.sbuf_tensor(f"{p}_keys_T", [DIM, U * BATCH * UNIT], FP32))
        n_vw = U if G == 1 else U * BATCH
        values = ctx.enter_context(nc.sbuf_tensor(f"{p}_values", [PART, n_vw * UCHUNKS, DIM], FP32))
        attention_tables(nc, m, a, at, keysT, values)
        attention_tokens(nc, m, at, keysT, values)


def attention_tables(nc, m, a, at, keysT, values):
    p, H, DH, G = at.prefix, at.heads, at.head_dim, at.G
    GROUPS = H // 4
    with ExitStack() as ctx:
        sb = lambda n, s: ctx.enter_context(nc.sbuf_tensor(f"{p}_pre_{n}", s, FP32))
        sem = lambda n: m.semaphore(nc, f"{p}_pre_{n}")
        HP = PART // DH
        wq, wk = sb("WqT", [PART, H // HP, DIM]), sb("WkT", [PART, H // HP, CDIM])
        wv, wo = sb("WvT", [PART, H // HP, CDIM]), sb("Wo", [PART, H // HP, DIM])
        head = lambda w, h: w[h % HP * DH:(h % HP + 1) * DH, h // HP, :]
        bias = sb("out_bias", [PART, DIM])
        qk, vo = sb("qk", [CDIM, H, DIM]), sb("vo", [CDIM, H, DIM])
        plain = sb("plain", [PART, 2, BATCH, H, DIM]) if G > 1 else None
        ps_w = ctx.enter_context(nc.psum_tensor(f"{p}_pre_ps_w", [PART, 2, BLOCK], FP32))
        ps_k = ctx.enter_context(nc.psum_tensor(f"{p}_pre_ps_k", [PART, 2, 2, BLOCK], FP32))
        ps_v = ctx.enter_context(nc.psum_tensor(f"{p}_pre_ps_v", [PART, 2, BLOCK], FP32))
        w_in, bias_in, w_ready, qk_kept, vo_kept = (sem(n) for n in ("w_in", "bias_in", "w_ready", "qk_kept", "vo_kept"))
        k_ready, k_kept, v_ready, v_kept, stacked = (sem(n) for n in ("k_ready", "k_kept", "v_ready", "v_kept", "stacked"))
        bias_scaled, bias_added = sem("bias_scaled"), sem("bias_added")
        if HP == 1:
            qk_out = lambda h: ps_w[0:CDIM, 0, h % 4 * DIM:(h % 4 + 1) * DIM]
            vo_out = lambda h: ps_w[0:CDIM, 1, h % 4 * DIM:(h % 4 + 1) * DIM]
            four = lambda n: ps_w[0:CDIM, n, :].rearrange("c (h d) -> c h d", h=4)
        else:
            qk_out = lambda h: ps_w[0:CDIM, h % 2, h % 4 // 2 * DIM:(h % 4 // 2 + 1) * DIM]
            vo_out = lambda h: ps_w[0:CDIM, h % 2, (2 + h % 4 // 2) * DIM:(3 + h % 4 // 2) * DIM]
            four = lambda n: ps_w[0:CDIM, :, 2 * n * DIM:2 * (n + 1) * DIM].rearrange("c s (h d) -> c h s d", h=2)
        if G == 1:
            pieces = [(c * PART, min(PART, ALLKEYS - c * PART)) for c in range(UCHUNKS)]
        else:
            pieces = [(b * KEYS + c * PART, min(PART, KEYS - c * PART)) for b in range(BATCH) for c in range(2)]
        products = [(g, n) for g in range(GROUPS) for n in range(len(pieces))]

        with nc.Block() as block:
            @block.sync
            def _(sp):
                for w, name in ((wk, "WkT"), (wq, "WqT"), (wv, "WvT"), (wo, "Wo")):
                    sp.dma_start(w[:].rearrange("d h c -> d (h c)"), a[f"{p}_{name}"]).then_inc(w_in, 16)
                sp.dma_start(bias[:], a[p + "_bo"].rearrange("(o d) -> o d", o=1).to_broadcast([PART, DIM])).then_inc(bias_in, 16)
                sp.wait_ge(w_in, 64)
                if G > 1:
                    sp.wait_ge(v_kept, len(products))
                    cuts = 0
                    dst = values[:].rearrange("r (q b c) d -> r q b c d", b=BATCH, c=UCHUNKS)
                    for hh in range(4):
                        for c2 in range(2):
                            k0, k1 = c2 * PART, min((c2 + 1) * PART, KEYS)
                            while k0 < k1:
                                r = hh * KEYS + k0
                                n = min(k1 - k0, PART - r % PART)
                                for q in range(GROUPS):
                                    sp.dma_start(dst[r % PART:r % PART + n, q, :, r // PART, :],
                                                 plain[k0 - c2 * PART:k0 - c2 * PART + n, c2, :, q * 4 + hh, :]).then_inc(stacked, 16)
                                    cuts += 1
                                k0 += n
                    sp.wait_ge(stacked, 16 * cuts)

            @block.tensor
            def _(pe):
                pe.wait_ge(w_in, 64)
                n_k = 0
                for g in range(GROUPS):
                    if g:
                        pe.wait_ge(qk_kept, g)
                        pe.wait_ge(vo_kept, g)
                    for w1, w2, out in ((wk, wq, qk_out), (wv, wo, vo_out)):
                        for h in range(4 * g, 4 * g + 4):
                            mm = pe.matmul(out(h), head(w1, h), head(w2, h), start=True, stop=True)
                    mm.then_inc(w_ready, 1)
                    pe.wait_ge(qk_kept, g + 1)
                    for h in range(4 * g, 4 * g + 4):
                        if n_k >= 2:
                            pe.wait_ge(k_kept, n_k - 1)
                        for s in range(2):
                            mm = pe.matmul(ps_k[:, n_k % 2, s, 0:HALFKEYS], qk[:, h, :], m.ctxT[:, s * HALFKEYS:(s + 1) * HALFKEYS],
                                           start=True, stop=True)
                        mm.then_inc(k_ready, 1)
                        n_k += 1
                for n, (g, q) in enumerate(products):
                    first, count = pieces[q]
                    pe.wait_ge(vo_kept, g + 1)
                    if n >= 2:
                        pe.wait_ge(v_kept, n - 1)
                    pe.matmul(ps_v[0:count, n % 2, :], m.ctxT[:, first:first + count],
                              vo[:, 4 * g:4 * g + 4, :].rearrange("c h d -> c (h d)"), start=True, stop=True).then_inc(v_ready, 1)

            @block.scalar
            def _(act):
                def heads4(w, g):
                    v = w[:, 4 * g:4 * g + 4, :]
                    return v if HP == 1 else v.rearrange("c (h s) d -> c h s d", s=2)

                for g in range(GROUPS):
                    act.wait_ge(w_ready, g + 1)
                    nc.scalar.activation(heads4(qk, g), four(0), ACT.Copy,
                                         scale=at.scale).then_inc(qk_kept, 1)
                    nc.scalar.activation(heads4(vo, g), four(1), ACT.Copy).then_inc(vo_kept, 1)
                for n, (g, q) in enumerate(products):
                    first, count = pieces[q]
                    act.wait_ge(v_ready, n + 1)
                    if G == 1:
                        dst = values[0:count, :, :].rearrange("k (h c) d -> k h c d", c=UCHUNKS)[:, 4 * g:4 * g + 4, q, :]
                    else:
                        dst = plain[0:count, q % 2, q // 2, 4 * g:4 * g + 4, :]
                    nc.scalar.activation(dst, ps_v[0:count, n % 2, :].rearrange("k (h d) -> k h d", h=4), ACT.Copy).then_inc(v_kept, 1)

            @block.vector
            def _(dve):
                dve.wait_ge(bias_in, 16)
                dve.tensor_scalar(bias[:], bias[:], m.gate[:, at.layer:at.layer + 1], None, ALU.mult).then_inc(bias_scaled, 1)
                dve.wait_ge(bias_scaled, 1)
                for t in range(BLOCKS):
                    rows = m.x[:, t * PER_BLOCK:(t + 1) * PER_BLOCK, :]
                    dve.tensor_tensor(rows, rows, bias[:].unsqueeze(1).to_broadcast([PART, PER_BLOCK, DIM]), ALU.add).then_inc(bias_added, 1)
                for h in range(H):
                    dve.wait_ge(k_ready, h + 1)
                    src = ps_k[:, h % 2, :, 0:HALFKEYS]
                    if G == 1:
                        dst = keysT[:, h * UNIT:(h + 1) * UNIT].rearrange("p (s k) -> p s k", s=2)
                        dve.tensor_copy(dst, src).then_inc(k_kept, 1)
                    else:
                        dst = keysT[:].rearrange("p (q s v h k) -> p q s v h k", s=2, v=2, h=4, k=KEYS)[:, h // 4, :, :, h % 4, :]
                        dve.tensor_copy(dst, src.rearrange("p s (v k) -> p s v k", v=2)).then_inc(k_kept, 1)


def attention_tokens(nc, m, at, keysT, values):
    p, G, U = at.prefix, at.G, at.units
    TURNS, UNITS = TILES // 2, 2 * U
    WIDTH = UNIT // G
    with ExitStack() as ctx:
        sb = lambda n, s: ctx.enter_context(nc.sbuf_tensor(f"{p}_{n}", s, FP32))
        sem = lambda n: m.semaphore(nc, f"{p}_{n}")
        tile_x = sb("tile_x", [DIM, 2, PART])
        less = sb("less", [PART, 2, G])
        total = sb("total", [PART, 2, G])
        share = sb("share", [PART, 2, G])
        prob = sb("prob", [PART, 2, UNIT])
        scaled = sb("scaled", [PART, 2, UNIT]) if G > 1 else sb("scaled", [PART, 2, PART])
        probT = sb("probT", [PART, 2, UCHUNKS, PART])
        ps_s = ctx.enter_context(nc.psum_tensor(f"{p}_ps_s", [PART, 2, 2 * BLOCK], FP32))
        ps_a = ctx.enter_context(nc.psum_tensor(f"{p}_ps_a", [PART, 2, BLOCK], FP32))
        ps_b = ctx.enter_context(nc.psum_tensor(f"{p}_ps_b", [PART, BLOCK], FP32))
        ps_o = ctx.enter_context(nc.psum_tensor(f"{p}_ps_o", [PART, BLOCK], FP32))
        tile_ready, s_ready, less_ready, prob_ready = sem("tile_ready"), sem("s_ready"), sem("less_ready"), sem("prob_ready")
        share_ready, scaled_ready, t_ready, t_kept = sem("share_ready"), sem("scaled_ready"), sem("t_ready"), sem("t_kept")
        pv_done, x_added = sem("pv_done"), sem("x_added")
        grouped = lambda v: v.rearrange("p (g k) -> p g k", g=G)

        with nc.Block() as block:
            @block.tensor
            def _(pe):
                start(pe, t_ready)
                def scores(turn, k):
                    if k >= UNITS:
                        turn, k = turn + 1, k - UNITS
                    half, u = divmod(k, U)
                    base = u * UNIT if G == 1 else (u * BATCH + turn // 2) * UNIT
                    if u == 0:
                        pe.wait_ge(tile_ready, turn * 2 + half + 1)
                    pe.matmul(ps_s[:, k % 2, 0:BLOCK], tile_x[:, half, :], keysT[:, bass.ds(base, BLOCK)], start=True, stop=True)
                    pe.matmul(ps_s[:, k % 2, BLOCK:UNIT], tile_x[:, half, :], keysT[:, bass.ds(base + BLOCK, UNIT - BLOCK)],
                              start=True, stop=True).then_inc(s_ready, 1)

                scores(0, 0)
                scores(0, 1)
                with pe.Fori(0, TURNS) as it:
                    for k in range(UNITS):
                        n = it * UNITS + k
                        half, u = divmod(k, U)
                        pe.wait_ge(scaled_ready, n + 1 + START)
                        if G == 1:
                            pe.wait_ge(prob_ready, n + 1)
                        for c in range(UCHUNKS):
                            rows = PART if c < 4 else ULAST
                            out = ps_a[:, k % 2, c * PART:(c + 1) * PART] if c < 4 else ps_b[0:ULAST, 0:PART]
                            if G == 1:
                                mm = pe.matmul(out, prob[:, k % 2, c * PART:c * PART + rows], scaled[:, k % 2, :], start=True, stop=True)
                            else:
                                mm = pe.transpose(out, scaled[:, k % 2, c * PART:c * PART + rows], m.ident[:])
                        mm.then_inc(t_ready, 1)
                        pe.wait_ge(prob_ready, n + 1)
                        scores(it, k + 2)
                        pe.wait_ge(t_kept, it * (2 * UNITS) + (2 * k + 2))
                        if u == 0:
                            pe.wait_ge(x_added, it * 2 + half + START)
                        base = u * UCHUNKS if G == 1 else (u * BATCH + it // 2) * UCHUNKS
                        for c in range(UCHUNKS):
                            rows = PART if c < 4 else ULAST
                            v = values[0:rows, bass.ds(base + c, 1), :].rearrange("k o d -> k (o d)")
                            mm = pe.matmul(ps_o[:, 0:DIM], probT[0:rows, k % 2, c, :], v,
                                           start=(u == 0 and c == 0), stop=(u == U - 1 and c == UCHUNKS - 1))
                        mm.then_inc(pv_done, 1)

            @block.scalar
            def _(act):
                with act.Fori(0, TURNS) as it:
                    for k in range(UNITS):
                        n = it * UNITS + k
                        act.wait_ge(less_ready, n + 1)
                        if G == 1:
                            act.wait_ge(t_ready, it * UNITS + max(k - 1, 0) + START)
                        act.wait_ge(scaled_ready, it * UNITS + max(k - 1, 0) + START)
                        for g in range(G):
                            cols = slice(g * WIDTH, (g + 1) * WIDTH)
                            ins = nc.scalar.activation(prob[:, k % 2, cols], ps_s[:, k % 2, cols], ACT.Exp,
                                                       bias=less[:, k % 2, g:g + 1], accum_out=total[:, k % 2, g:g + 1])
                        ins.then_inc(prob_ready, 1)

            @block.vector
            def _(dve):
                start(dve, x_added)
                def fetch(tile, half):
                    dve.tensor_scalar(tile_x[:, half, :], m.xt[:, bass.ds(tile * PART, PART)], 1.0, None,
                                      ALU.mult).then_inc(tile_ready, 1)

                def maxima(n, k):
                    dve.wait_ge(s_ready, n + 1)
                    dve.tensor_reduce(less[:, k % 2, :], grouped(ps_s[:, k % 2, 0:UNIT]), AX.X, ALU.max, negate=True).then_inc(less_ready, 1)

                fetch(0, 0)
                fetch(1, 1)
                maxima(0, 0)
                maxima(1, 1)
                with dve.Fori(0, TURNS) as it:
                    for k in range(UNITS):
                        n = it * UNITS + k
                        half, u = divmod(k, U)
                        dve.wait_ge(prob_ready, n + 1)
                        dve.wait_ge(scaled_ready, it * UNITS + max(k - 1, 0) + START)
                        dve.reciprocal(share[:, k % 2, :], total[:, k % 2, :]).then_inc(share_ready, 1)
                        if u == U - 1:
                            dve.wait_ge(s_ready, n + 1)
                            fetch(it * 2 + 2 + half, half)
                        dve.wait_ge(t_ready, n + 1 + START)
                        dve.tensor_copy(probT[:, k % 2, 0:4, :], ps_a[:, k % 2, :].rearrange("p (c t) -> p c t", c=4)).then_inc(t_kept, 1)
                        dve.tensor_copy(probT[0:ULAST, k % 2, 4, :], ps_b[0:ULAST, 0:PART]).then_inc(t_kept, 1)
                        maxima(n + 2, k)
                        if u == U - 1:
                            dve.wait_ge(pv_done, n + 1)
                            rows = m.x[:, bass.ds(it * 2 + half, 1), :].rearrange("p o d -> p (o d)")
                            dve.scalar_tensor_tensor(rows, ps_o[:, 0:DIM], m.gate[:, at.layer:at.layer + 1], rows,
                                                     ALU.mult, ALU.add).then_inc(x_added, 1)

            @block.gpsimd
            def _(pool):
                start(pool, scaled_ready)
                with pool.Fori(0, TURNS) as it:
                    for k in range(UNITS):
                        n = it * UNITS + k
                        pool.wait_ge(t_ready, it * UNITS + max(k - 1, 0) + START)
                        pool.wait_ge(share_ready, n + 1)
                        if G == 1:
                            pool.tensor_tensor(scaled[:, k % 2, :], m.ident[:], share[:, k % 2, :].to_broadcast([PART, PART]),
                                               ALU.mult).then_inc(scaled_ready, 1)
                        else:
                            pool.tensor_tensor(grouped(scaled[:, k % 2, :]), grouped(prob[:, k % 2, :]),
                                               share[:, k % 2, :].unsqueeze(2).to_broadcast([PART, G, WIDTH]),
                                               ALU.mult).then_inc(scaled_ready, 1)


L2_ATT = Attention(2, "L2_xattn", 16, 64, 4, 64 ** -0.5)
L3_ATT = Attention(3, "L3_xattn", 8, 128, 1, 1.5 * 128 ** -0.5)


LAT_CHUNKS = SEQ // PART
CTX_CHUNK = KEYS // 2
L1_KEYS = SEQ + KEYS
L1_HEADS, L1_DH = 2, 64


def latent_attention(nc, m, a):
    with ExitStack() as ctx:
        sb = lambda n, s: ctx.enter_context(nc.sbuf_tensor(f"lat_{n}", s, FP32))
        kT = sb("kT", [DIM, BATCH + 1, L1_KEYS])
        v = sb("v", [PART, BATCH * 6, DIM])
        qT = sb("qT", [DIM, (TILES + 2) * 2 * PART])
        masked = sb("masked", [PART, ALLKEYS + KEYS])
        latent_context(nc, m, a, kT, v, masked)
        latent_projections(nc, m, a, kT, v, qT, masked)
        latent_tokens(nc, m, kT, v, qT, masked)
    latent_output(nc, m, a)


def latent_context(nc, m, a, kT, v, masked):
    R, N = CTX_CHUNK, 2 * BATCH
    with ExitStack() as ctx:
        sb = lambda n, s, dt=FP32: ctx.enter_context(nc.sbuf_tensor(f"latc_{n}", s, dt))
        sem = lambda n: m.semaphore(nc, f"latc_{n}")
        rows, w = sb("rows", [R, N, CDIM]), sb("w", [CDIM, 2 * DIM])
        mask8, maskf = sb("mask8", [PART, ALLKEYS], U8), sb("maskf", [PART, ALLKEYS])
        stats, moments = sb("stats", [R, N, 6]), sb("moments", [R, N, 2])
        var, sd, rstd = sb("var", [R, N]), sb("sd", [R, N]), sb("rstd", [R, N])
        normT = sb("normT", [CDIM, N, R])
        k, sq = sb("k", [R, N, DIM]), sb("sq", [R, N, DIM])
        ss, rms, inv = sb("ss", [R, 2 * N]), sb("rms", [R, 2 * N]), sb("inv", [R, 2 * N])
        ps_t = ctx.enter_context(nc.psum_tensor("latc_ps_t", [PART, 2, BLOCK], FP32))
        ps_k = ctx.enter_context(nc.psum_tensor("latc_ps_k", [PART, 4, BLOCK], FP32))
        rows_in, w_in, mask_in = sem("rows_in"), sem("w_in"), sem("mask_in")
        steps, var_done, sd_done, normed, turned, turned_kept = (sem(n) for n in ("steps", "var_done", "sd_done", "normed", "turned", "turned_kept"))
        kv_ready, k_kept, v_kept, squares, ss_done, rms_done, k_normed = (sem(n) for n in ("kv_ready", "k_kept", "v_kept", "squares", "ss_done", "rms_done", "k_normed"))
        k_turned, kT_kept = sem("k_turned"), sem("kT_kept")
        with nc.Block() as block:
            @block.sync
            def _(sp):
                sp.dma_start(rows[:], a["ctx_768"].rearrange("b (u k) c -> k (b u) c", k=R)).then_inc(rows_in, 16)
                sp.dma_start(w[:], a["L1_xattn_WkvT"]).then_inc(w_in, 16)
                sp.dma_start(mask8[:], a["mask_BxS2_bk0"].rearrange("(o b) k -> o (b k)", o=1).to_broadcast([PART, ALLKEYS])).then_inc(mask_in, 16)
                sp.wait_ge(w_in, 16)

            @block.vector
            def _(dve):
                c = Chain(dve, steps)
                step = lambda ins: (c.did(ins), c.wait())
                dve.wait_ge(rows_in, 16)
                for i in range(N):
                    c.did(dve.bn_stats(stats[:, i, :], rows[:, i, :]))
                c.wait()
                for i in range(N):
                    c.did(dve.bn_aggr(moments[:, i, :], stats[:, i, :]))
                c.wait()
                dve.tensor_scalar(var[:], moments[:, :, 1], 1e-5, None, ALU.add).then_inc(var_done, 1)
                dve.wait_ge(sd_done, 1)
                step(dve.reciprocal(rstd[:], sd[:]))
                for i in range(N):
                    dve.tensor_scalar(rows[:, i, :], rows[:, i, :], moments[:, i, 0:1], rstd[:, i:i + 1],
                                      ALU.subtract, ALU.mult).then_inc(normed, 1)
                dve.wait_ge(mask_in, 16)
                step(dve.tensor_copy(maskf[:], mask8[:]))
                step(dve.tensor_scalar(masked[:, 0:ALLKEYS], maskf[:], 1.0, BIG, ALU.subtract, ALU.mult))
                dve.wait_ge(squares, 4)
                dve.tensor_reduce(ss[:], sq[:].rearrange("p t (h d) -> p (t h) d", d=L1_DH), AX.X, ALU.add).then_inc(ss_done, 1)
                dve.wait_ge(rms_done, 1)
                step(dve.tensor_scalar(rms[:], rms[:], 1e-8, None, ALU.max))
                step(dve.reciprocal(inv[:], rms[:]))
                dve.wait_ge(k_kept, 4)
                heads = k[:].rearrange("p t (h d) -> p (t h) d", d=L1_DH)
                step(dve.tensor_tensor(heads, heads, inv[:].unsqueeze(2).to_broadcast([R, 2 * N, L1_DH]), ALU.mult))
                dve.tensor_tensor(heads, heads, m.row("kn_g")[0:R].unsqueeze(1).to_broadcast([R, 2 * N, L1_DH]),
                                  ALU.mult).then_inc(k_normed, 1)
                for s in range(2):
                    dve.wait_ge(k_turned, s + 1)
                    dve.tensor_copy(kT[:, 2 * s:2 * s + 2, SEQ:], ps_t[:, s, 0:4 * R].rearrange("p (b k) -> p b k", b=2)).then_inc(kT_kept, 1)

            @block.scalar
            def _(act):
                act.wait_ge(var_done, 1)
                nc.scalar.activation(sd[:], var[:], ACT.Sqrt).then_inc(sd_done, 1)
                for s in range(2):
                    act.wait_ge(turned, s + 1)
                    nc.scalar.activation(normT[:, 4 * s:4 * s + 4, :].rearrange("c t k -> c (t k)"), ps_t[0:CDIM, s, 0:4 * R], ACT.Identity,
                                         scale=m.col("ln_x_g")[0:CDIM], bias=m.col("ln_x_b")[0:CDIM]).then_inc(turned_kept, 1)
                for s in range(4):
                    act.wait_ge(kv_ready, s + 1)
                    bank = ps_k[0:R, s, :].rearrange("p (t n) -> p t n", t=2)
                    nc.scalar.activation(k[:, 2 * s:2 * s + 2, :], bank[:, :, 0:DIM], ACT.Copy).then_inc(k_kept, 1)
                    nc.scalar.activation(sq[:, 2 * s:2 * s + 2, :], bank[:, :, 0:DIM], ACT.Square).then_inc(squares, 1)
                    nc.scalar.activation(v[0:R, s * 6 + 4:s * 6 + 6, :], bank[:, :, DIM:], ACT.Copy).then_inc(v_kept, 1)
                act.wait_ge(ss_done, 1)
                nc.scalar.activation(rms[:], ss[:], ACT.Sqrt, scale=1.0 / L1_DH).then_inc(rms_done, 1)

            @block.tensor
            def _(pe):
                for i in range(N):
                    pe.wait_ge(normed, i + 1)
                    mm = pe.transpose(ps_t[0:CDIM, i // 4, i % 4 * R:(i % 4 + 1) * R], rows[:, i, :], m.ident[0:R, 0:R])
                    if i % 4 == 3:
                        mm.then_inc(turned, 1)
                pe.wait_ge(w_in, 16)
                for i in range(N):
                    pe.wait_ge(turned_kept, i // 4 + 1)
                    mm = pe.matmul(ps_k[0:R, i // 2, i % 2 * 2 * DIM:(i % 2 + 1) * 2 * DIM], normT[:, i, :], w[:], start=True, stop=True)
                    if i % 2:
                        mm.then_inc(kv_ready, 1)
                pe.wait_ge(k_normed, 1)
                for i in range(N):
                    mm = pe.transpose(ps_t[:, i // 4, i % 4 * R:(i % 4 + 1) * R], k[:, i, :], m.ident[0:R, 0:R])
                    if i % 4 == 3:
                        mm.then_inc(k_turned, 1)


def latent_projections(nc, m, a, kT, v, qT, masked):
    with ExitStack() as ctx:
        sb = lambda n, s, dt=FP32: ctx.enter_context(nc.sbuf_tensor(f"latq_{n}", s, dt))
        sem = lambda n: m.semaphore(nc, f"latq_{n}")
        w = sb("w", [DIM, 3 * DIM])
        gain = sb("gain", [PART, 4, L1_DH])
        qk, sq = sb("qk", [PART, 2, 4, 2 * DIM]), sb("sq", [PART, 2, 4, 2 * DIM])
        ss, rms, inv = sb("ss", [PART, 2, 16]), sb("rms", [PART, 2, 16]), sb("inv", [PART, 2, 16])
        ps_p = ctx.enter_context(nc.psum_tensor("latq_ps_p", [PART, 4, BLOCK], FP32))
        ps_t = ctx.enter_context(nc.psum_tensor("latq_ps_t", [PART, 2, BLOCK], FP32))
        names = ("w_in", "zeroed", "gained", "p_ready", "qk_kept", "squares", "v_kept", "ss_done", "rms_done", "steps", "normed", "turned", "q_kept", "k_kept")
        w_in, zeroed, gained, p_ready, qk_kept, squares, v_kept, ss_done, rms_done, steps, normed, turned, q_kept, k_kept = (sem(n) for n in names)
        tiles = qT[:].rearrange("p (i h t) -> p i h t", h=2, t=PART)
        with nc.Block() as block:
            @block.sync
            def _(sp):
                sp.dma_start(w[:], a["L1_xattn_WqkvT"]).then_inc(w_in, 16)
                sp.wait_ge(w_in, 16)

            @block.gpsimd
            def _(pool):
                for n, part in enumerate((kT[:, BATCH, :], masked[:, ALLKEYS:], tiles[64:128, :, 0, :], tiles[0:64, :, 1, :],
                                          tiles[0:64, TILES:, 0, :], tiles[64:128, TILES:, 1, :])):
                    if n:
                        pool.wait_ge(zeroed, n)
                    pool.memset(part, 0.0).then_inc(zeroed, 1)

            @block.tensor
            def _(pe):
                pe.wait_ge(w_in, 16)
                for t in range(BLOCKS):
                    if t:
                        pe.wait_ge(v_kept, t)
                    for j in range(4):
                        i = 4 * t + j
                        mm = pe.matmul(ps_p[:, j, 0:3 * DIM], m.xt[:, i * PART:(i + 1) * PART], w[:], start=True, stop=True)
                    mm.then_inc(p_ready, 1)
                    pe.wait_ge(normed, t + 1)
                    if t:
                        pe.wait_ge(q_kept, 2 * t)
                    for j in range(4):
                        mm = pe.transpose(ps_t[:, 0, j * PART:(j + 1) * PART], qk[:, t % 2, j, 0:DIM], m.ident[:])
                    mm.then_inc(turned, 1)
                    if t:
                        pe.wait_ge(k_kept, t)
                    for j in range(4):
                        mm = pe.transpose(ps_t[:, 1, j * PART:(j + 1) * PART], qk[:, t % 2, j, DIM:], m.ident[:])
                    mm.then_inc(turned, 1)

            @block.scalar
            def _(act):
                for t in range(BLOCKS):
                    act.wait_ge(p_ready, t + 1)
                    if t >= 2:
                        act.wait_ge(turned, 2 * (t - 1))
                    nc.scalar.activation(qk[:, t % 2, :, :], ps_p[:, :, 0:2 * DIM], ACT.Copy).then_inc(qk_kept, 1)
                    nc.scalar.activation(sq[:, t % 2, :, :], ps_p[:, :, 0:2 * DIM], ACT.Square).then_inc(squares, 1)
                    nc.scalar.activation(v[:, t * 6:t * 6 + 4, :], ps_p[:, :, 2 * DIM:3 * DIM], ACT.Copy).then_inc(v_kept, 1)
                    act.wait_ge(ss_done, t + 1)
                    nc.scalar.activation(rms[:, t % 2, :], ss[:, t % 2, :], ACT.Sqrt, scale=1.0 / L1_DH).then_inc(rms_done, 1)
                    act.wait_ge(turned, 2 * t + 2)
                    nc.scalar.activation(kT[:, t, 0:SEQ], ps_t[:, 1, :], ACT.Copy).then_inc(k_kept, 1)

            @block.vector
            def _(dve):
                c = Chain(dve, steps)
                step = lambda ins: (c.did(ins), c.wait())
                step(dve.tensor_scalar(gain[:, 0:2, :], m.row("qn_g").unsqueeze(1).to_broadcast([PART, 2, L1_DH]), L1_DH ** -0.5, None, ALU.mult))
                step(dve.tensor_copy(gain[:, 2:4, :], m.row("kn_g").unsqueeze(1).to_broadcast([PART, 2, L1_DH])))
                dve.wait_ge(zeroed, 6)
                for t in range(BLOCKS):
                    dve.wait_ge(squares, t + 1)
                    heads = qk[:, t % 2, :, :].rearrange("p j (g d) -> p (j g) d", d=L1_DH)
                    dve.tensor_reduce(ss[:, t % 2, :], sq[:, t % 2, :, :].rearrange("p j (g d) -> p (j g) d", d=L1_DH), AX.X,
                                      ALU.add).then_inc(ss_done, 1)
                    dve.wait_ge(rms_done, t + 1)
                    step(dve.tensor_scalar(inv[:, t % 2, :], rms[:, t % 2, :], 1e-8, None, ALU.max))
                    step(dve.reciprocal(inv[:, t % 2, :], inv[:, t % 2, :]))
                    dve.wait_ge(qk_kept, t + 1)
                    step(dve.tensor_tensor(heads, heads, inv[:, t % 2, :].unsqueeze(2).to_broadcast([PART, 16, L1_DH]), ALU.mult))
                    byhead = qk[:, t % 2, :, :].rearrange("p j (g d) -> p j g d", d=L1_DH)
                    dve.tensor_tensor(byhead, byhead, gain[:].unsqueeze(1).to_broadcast([PART, 4, 4, L1_DH]), ALU.mult).then_inc(normed, 1)
                    dve.wait_ge(turned, 2 * t + 1)
                    for h in range(2):
                        part = slice(64 * h, 64 * h + 64)
                        dve.tensor_copy(tiles[part, 4 * t:4 * t + 4, h, :],
                                        ps_t[part, 0, :].rearrange("p (j t) -> p j t", j=4)).then_inc(q_kept, 1)


def latent_tokens(nc, m, kT, v, qT, masked):
    U, TURNS, UNITS = 2, TILES // 2, 4
    keys = kT[:].rearrange("p b k -> p (b k)")
    with ExitStack() as ctx:
        sb = lambda n, s: ctx.enter_context(nc.sbuf_tensor(f"lata_{n}", s, FP32))
        sem = lambda n: m.semaphore(nc, f"lata_{n}")
        tile_q = sb("tile_q", [DIM, 2, 2, PART])
        less, total, share = sb("less", [PART, 2]), sb("total", [PART, 2]), sb("share", [PART, 2])
        prob = sb("prob", [PART, 2, L1_KEYS])
        probT = sb("probT", [PART, 2, 6, PART])
        ps_s = ctx.enter_context(nc.psum_tensor("lata_ps_s", [PART, 2, 2 * BLOCK], FP32))
        ps_a = ctx.enter_context(nc.psum_tensor("lata_ps_a", [PART, 2, BLOCK], FP32))
        ps_b = ctx.enter_context(nc.psum_tensor("lata_ps_b", [PART, BLOCK], FP32))
        ps_o = ctx.enter_context(nc.psum_tensor("lata_ps_o", [PART, BLOCK], FP32))
        names = ("tile_ready", "s_ready", "mask_added", "less_ready", "prob_ready", "share_ready", "t_ready", "t_kept", "pv_done", "o_kept")
        tile_ready, s_ready, mask_added, less_ready, prob_ready, share_ready, t_ready, t_kept, pv_done, o_kept = (sem(n) for n in names)
        CUT = [(c * PART, PART) for c in range(LAT_CHUNKS)] + [(SEQ, CTX_CHUNK), (SEQ + CTX_CHUNK, CTX_CHUNK)]
        with nc.Block() as block:
            @block.tensor
            def _(pe):
                start(pe, t_ready)
                def scores(turn, k):
                    if k >= UNITS:
                        turn, k = turn + 1, k - UNITS
                    half, u = divmod(k, U)
                    if u == 0:
                        pe.wait_ge(tile_ready, turn * 2 + half + 1)
                    base = (turn // 2) * L1_KEYS
                    pe.matmul(ps_s[:, k % 2, 0:BLOCK], tile_q[:, half, u, :], keys[:, bass.ds(base, BLOCK)], start=True, stop=True)
                    pe.matmul(ps_s[:, k % 2, BLOCK:L1_KEYS], tile_q[:, half, u, :], keys[:, bass.ds(base + BLOCK, KEYS)],
                              start=True, stop=True).then_inc(s_ready, 1)

                scores(0, 0)
                scores(0, 1)
                with pe.Fori(0, TURNS) as it:
                    for k in range(UNITS):
                        n = it * UNITS + k
                        half, u = divmod(k, U)
                        pe.wait_ge(prob_ready, n + 1)
                        for c, (at, rows) in enumerate(CUT):
                            out = ps_a[:, k % 2, c * PART:(c + 1) * PART] if c < 4 else ps_b[0:rows, (c - 4) * PART:(c - 3) * PART]
                            mm = pe.transpose(out, prob[:, k % 2, at:at + rows], m.ident[:])
                        mm.then_inc(t_ready, 1)
                        scores(it, k + 2)
                        pe.wait_ge(t_kept, it * (2 * UNITS) + (2 * k + 2))
                        if u == 0:
                            pe.wait_ge(o_kept, it * 4 + 2 * half + START)
                        for c, (at, rows) in enumerate(CUT):
                            values = v[0:rows, bass.ds((it // 2) * 6 + c, 1), u * 64:(u + 1) * 64].rearrange("k o d -> k (o d)")
                            mm = pe.matmul(ps_o[:, u * 64:(u + 1) * 64], probT[0:rows, k % 2, c, :], values, start=(c == 0), stop=(c == 5))
                        mm.then_inc(pv_done, 1)

            @block.scalar
            def _(act):
                with act.Fori(0, TURNS) as it:
                    for k in range(UNITS):
                        n = it * UNITS + k
                        act.wait_ge(less_ready, n + 1)
                        act.wait_ge(t_ready, it * UNITS + max(k - 1, 0) + START)
                        act.wait_ge(share_ready, it * UNITS + max(k - 1, 0) + START)
                        nc.scalar.activation(prob[:, k % 2, :], ps_s[:, k % 2, 0:L1_KEYS], ACT.Exp, bias=less[:, k % 2:k % 2 + 1],
                                             accum_out=total[:, k % 2:k % 2 + 1]).then_inc(prob_ready, 1)

            @block.vector
            def _(dve):
                start(dve, o_kept, share_ready)
                def fetch(tile, half):
                    dve.tensor_scalar(tile_q[:, half, :, :].rearrange("p h t -> p (h t)"), qT[:, bass.ds(tile * (2 * PART), 2 * PART)],
                                      1.0, None, ALU.mult).then_inc(tile_ready, 1)

                def maxima(n, k, turn):
                    dve.wait_ge(s_ready, n + 1)
                    part = ps_s[:, k % 2, SEQ:L1_KEYS]
                    dve.tensor_tensor(part, part, masked[:, bass.ds((turn // 2) * KEYS, KEYS)], ALU.add).then_inc(mask_added, 1)
                    dve.wait_ge(mask_added, n + 1)
                    dve.tensor_reduce(less[:, k % 2:k % 2 + 1], ps_s[:, k % 2, 0:L1_KEYS], AX.X, ALU.max, negate=True).then_inc(less_ready, 1)

                fetch(0, 0)
                fetch(1, 1)
                maxima(0, 0, 0)
                maxima(1, 1, 0)
                with dve.Fori(0, TURNS) as it:
                    for k in range(UNITS):
                        n = it * UNITS + k
                        half, u = divmod(k, U)
                        dve.wait_ge(prob_ready, n + 1)
                        if u == 0:
                            dve.wait_ge(o_kept, it * 4 + 2 * half + START)
                        dve.reciprocal(share[:, k % 2:k % 2 + 1], total[:, k % 2:k % 2 + 1]).then_inc(share_ready, 1)
                        if u == U - 1:
                            dve.wait_ge(s_ready, n + 1)
                            fetch(it * 2 + 2 + half, half)
                        dve.wait_ge(t_ready, n + 1 + START)
                        dve.tensor_copy(probT[:, k % 2, 0:4, :], ps_a[:, k % 2, :].rearrange("p (c t) -> p c t", c=4)).then_inc(t_kept, 1)
                        dve.tensor_copy(probT[0:CTX_CHUNK, k % 2, 4:6, :], ps_b[0:CTX_CHUNK, 0:2 * PART].rearrange("p (c t) -> p c t", c=2)).then_inc(t_kept, 1)
                        maxima(n + 2, k, it if k < 2 else it + 1)
                        if u == U - 1:
                            dve.wait_ge(pv_done, n + 1)
                            dve.wait_ge(share_ready, n + 1 + START)
                            for h in range(2):
                                out = m.xn[:, bass.ds(it * 2 + half, 1), h * 64:(h + 1) * 64].rearrange("p o d -> p (o d)")
                                dve.tensor_scalar(out, ps_o[:, h * 64:(h + 1) * 64], share[:, h:h + 1], None, ALU.mult).then_inc(o_kept, 1)


def latent_output(nc, m, a):
    with ExitStack() as ctx:
        sb = lambda n, s: ctx.enter_context(nc.sbuf_tensor(f"lato_{n}", s, FP32))
        sem = lambda n: m.semaphore(nc, f"lato_{n}")
        w, bias = sb("w", [DIM, DIM]), sb("bias", [PART, DIM])
        w_in, steps, turned, kept, y_ready, x_added = (sem(n) for n in ("w_in", "steps", "turned", "kept", "y_ready", "x_added"))
        ps_t = ctx.enter_context(nc.psum_tensor("lato_ps_t", [PART, 4, BLOCK], FP32))
        ps_y = ctx.enter_context(nc.psum_tensor("lato_ps_y", [PART, 4, BLOCK], FP32))
        gate = m.gate[:, 1:2]
        with nc.Block() as block:
            @block.sync
            def _(sp):
                sp.dma_start(w[:], a["L1_xattn_WoT"]).then_inc(w_in, 16)
                sp.wait_ge(w_in, 16)

            @block.tensor
            def _(pe):
                for t in range(BLOCKS):
                    for j in range(4):
                        mm = pe.transpose(ps_t[:, t, j * PART:(j + 1) * PART], m.xn[:, 4 * t + j, :], m.ident[:])
                    mm.then_inc(turned, 1)
                pe.wait_ge(w_in, 16)
                for t in range(BLOCKS):
                    pe.wait_ge(kept, t + 1)
                    for j in range(4):
                        i = 4 * t + j
                        mm = pe.matmul(ps_y[:, t, j * PART:(j + 1) * PART], m.xt[:, i * PART:(i + 1) * PART], w[:], start=True, stop=True)
                    mm.then_inc(y_ready, 1)

            @block.scalar
            def _(act):
                for t in range(BLOCKS):
                    act.wait_ge(turned, t + 1)
                    nc.scalar.activation(m.xt[:, t * BLOCK:(t + 1) * BLOCK], ps_t[:, t, :], ACT.Copy).then_inc(kept, 1)

            @block.vector
            def _(dve):
                c = Chain(dve, steps)
                c.did(dve.tensor_scalar(bias[:], m.row("L1_bo"), gate, None, ALU.mult))
                c.wait()
                for t in range(BLOCKS):
                    rows = m.x[:, 4 * t:4 * t + 4, :]
                    c.did(dve.tensor_tensor(rows, rows, bias[:].unsqueeze(1).to_broadcast([PART, 4, DIM]), ALU.add))
                c.wait()
                for t in range(BLOCKS):
                    rows = m.x[:, 4 * t:4 * t + 4, :].rearrange("p t d -> p (t d)")
                    dve.wait_ge(y_ready, t + 1)
                    dve.scalar_tensor_tensor(rows, ps_y[:, t, :], gate, rows, ALU.mult, ALU.add).then_inc(x_added, 1)


def ternary(nc, m, a):
    QB, EPS, ROUND = 128.0, 1e-5, 1.5 * 2.0 ** 23
    with ExitStack() as ctx:
        sb = lambda n, s: ctx.enter_context(nc.sbuf_tensor(f"tern_{n}", s, FP32))
        sem = lambda n: m.semaphore(nc, f"tern_{n}")
        w, wq = sb("w", [DIM, DIM]), sb("wq", [DIM, DIM])
        w_row, w_sum, x_row, x_max = sb("w_row", [PART, 1]), sb("w_sum", [PART, 1]), sb("x_row", [PART, 1]), sb("x_max", [PART, 1])
        beta, w_inv, x_inv, factor = sb("beta", [PART, 1]), sb("w_inv", [PART, 1]), sb("x_inv", [PART, 1]), sb("factor", [PART, 1])
        w_in, steps, rows_done, all_done, w_ready, x_ready, y_ready, x_added = (sem(n) for n in ("w_in", "steps", "rows_done", "all_done", "w_ready", "x_ready", "y_ready", "x_added"))
        ps_y = ctx.enter_context(nc.psum_tensor("tern_ps_y", [PART, 4, BLOCK], FP32))
        with nc.Block() as block:
            @block.sync
            def _(sp):
                sp.dma_start(w[:], a["L0_ffn_weight"]).then_inc(w_in, 16)
                sp.wait_ge(w_in, 16)

            @block.gpsimd
            def _(pool):
                pool.wait_ge(rows_done, 1)
                pool.partition_all_reduce(w_sum[:], w_row[:], PART, bass.bass_isa.ReduceOp.add).then_inc(all_done, 1)
                pool.wait_ge(rows_done, 2)
                pool.partition_all_reduce(x_max[:], x_row[:], PART, bass.bass_isa.ReduceOp.max).then_inc(all_done, 1)

            @block.vector
            def _(dve):
                c = Chain(dve, steps)
                step = lambda ins: (c.did(ins), c.wait())
                dve.wait_ge(w_in, 16)
                dve.tensor_reduce(w_row[:], w[:], AX.X, ALU.add, apply_absolute_value=True).then_inc(rows_done, 1)
                dve.tensor_reduce(x_row[:], m.xt[:, 0:TOKENS], AX.X, ALU.max, apply_absolute_value=True).then_inc(rows_done, 1)
                dve.wait_ge(all_done, 1)
                step(dve.tensor_scalar(beta[:], w_sum[:], 1.0 / (DIM * DIM), None, ALU.mult))
                step(dve.tensor_scalar(w_inv[:], beta[:], EPS, None, ALU.add))
                step(dve.reciprocal(w_inv[:], w_inv[:]))
                step(dve.tensor_scalar(wq[:], w[:], w_inv[:], None, ALU.mult))
                step(dve.tensor_scalar(wq[:], wq[:], ROUND, ROUND, ALU.add, ALU.subtract))
                dve.tensor_scalar(wq[:], wq[:], -1.0, 1.0, ALU.max, ALU.min).then_inc(w_ready, 1)
                dve.wait_ge(all_done, 2)
                step(dve.reciprocal(x_inv[:], x_max[:]))
                step(dve.tensor_scalar(factor[:], x_max[:], beta[:], 1.0 / QB, ALU.mult, ALU.mult))
                step(dve.tensor_scalar(factor[:], factor[:], m.gate[:, LAYERS:LAYERS + 1], None, ALU.mult))
                for t in range(BLOCKS):
                    xt = m.xt[:, t * BLOCK:(t + 1) * BLOCK]
                    step(dve.tensor_scalar(xt, xt, QB, x_inv[:], ALU.mult, ALU.mult))
                    dve.tensor_scalar(xt, xt, -QB + EPS, QB - EPS, ALU.max, ALU.min).then_inc(x_ready, 1)
                for t in range(BLOCKS):
                    rows = m.x[:, 4 * t:4 * t + 4, :].rearrange("p t d -> p (t d)")
                    dve.wait_ge(y_ready, t + 1)
                    dve.scalar_tensor_tensor(rows, ps_y[:, t, :], factor[:], rows, ALU.mult, ALU.add).then_inc(x_added, 1)

            @block.tensor
            def _(pe):
                pe.wait_ge(w_ready, 1)
                for t in range(BLOCKS):
                    pe.wait_ge(x_ready, t + 1)
                    for j in range(4):
                        i = 4 * t + j
                        mm = pe.matmul(ps_y[:, t, j * PART:(j + 1) * PART], m.xt[:, i * PART:(i + 1) * PART], wq[:], start=True, stop=True)
                    mm.then_inc(y_ready, 1)


L0_HEADS, L0_DH, TOP = 4, 32, 32
L0_SCALE = 1.0 / 32 ** 0.5
STATES = 64
FINE, COARSE = 32, 16
ROUND = 1.5 * 2.0 ** 23
TWO_PI = 6.2831845
LOG2_E = 1.4426950408889634
LN2_HIGH = 0.693359375
LN2_LOW = -2.12194440e-4
EXP_SERIES = (1 / 5040, 1 / 720, 1 / 120, 1 / 24, 1 / 6, 1 / 2, 1.0)
FREQ = 4


def film(nc, m, a, mod):
    with ExitStack() as ctx:
        sb = lambda n, s, dt=FP32: ctx.enter_context(nc.sbuf_tensor(f"film_{n}", s, dt))
        keysT = sb("keysT", [DIM, BATCH + 1, L0_HEADS * KEYS])
        values = sb("values", [CTX_CHUNK + 1, BATCH * 2, 4 * DIM])
        masked = sb("masked", [PART, BATCH + 1, KEYS])
        weight = sb("weight", [PART, TILES + 1])
        film_tables(nc, m, a, keysT, values, masked, weight)
        film_tokens(nc, m, keysT, values, masked, weight, mod)


def film_tables(nc, m, a, keysT, values, masked, weight):
    H = L0_HEADS
    with ExitStack() as ctx:
        sb = lambda n, s, dt=FP32: ctx.enter_context(nc.sbuf_tensor(f"filmt_{n}", s, dt))
        sem = lambda n: m.semaphore(nc, f"filmt_{n}")
        wq, wk = sb("wq", [DIM, DIM]), sb("wk", [DIM, CDIM])
        wv, wf = sb("wv", [DIM, CDIM]), sb("wf", [DIM, 4 * DIM])
        qk, vf = sb("qk", [CDIM, H, DIM]), sb("vf", [CDIM, 4 * DIM])
        mask8, maskf = sb("mask8", [PART, ALLKEYS], U8), sb("maskf", [PART, ALLKEYS])
        text8 = sb("text8", [PART, TILES], U8)
        bias = sb("bias", [1, 4 * DIM])
        ps_w = ctx.enter_context(nc.psum_tensor("filmt_ps_w", [PART, 4, BLOCK], FP32))
        ps_k = ctx.enter_context(nc.psum_tensor("filmt_ps_k", [PART, 2, 2, BLOCK], FP32))
        names = ("w_in", "masks_in", "bias_in", "steps", "qk_ready", "qk_kept", "vf_ready", "vf_kept", "k_ready", "k_kept", "v_ready", "v_kept", "bias_ready", "bias_laid", "zeroed")
        w_in, masks_in, bias_in, steps, qk_ready, qk_kept, vf_ready, vf_kept, k_ready, k_kept, v_ready, v_kept, bias_ready, bias_laid, zeroed = (sem(n) for n in names)
        with nc.Block() as block:
            @block.sync
            def _(sp):
                sp.dma_start(wq[:], a["L0_xattn_WqT"]).then_inc(w_in, 16)
                sp.dma_start(wk[:], a["L0_xattn_WkT"]).then_inc(w_in, 16)
                sp.dma_start(wv[:], a["L0_xattn_WvT"]).then_inc(w_in, 16)
                sp.dma_start(wf[:], a["L0_xattn_Wfilm"]).then_inc(w_in, 16)
                sp.dma_start(bias[:], a["L0_xattn_bfilm"].rearrange("(o n) -> o n", o=1)).then_inc(bias_in, 16)
                sp.dma_start(mask8[:], a["mask_BxS2_bf1"].rearrange("(o b) k -> o (b k)", o=1).to_broadcast([PART, ALLKEYS])).then_inc(masks_in, 16)
                sp.dma_start(text8[:], a["mask_BxS_bf1"]).then_inc(masks_in, 16)
                sp.wait_ge(bias_ready, 1)
                for n in range(BATCH * 2):
                    sp.dma_start(values[CTX_CHUNK:CTX_CHUNK + 1, n, :], bias[:]).then_inc(bias_laid, 16)
                sp.wait_ge(bias_laid, 16 * BATCH * 2)

            @block.gpsimd
            def _(pool):
                pool.memset(keysT[:, BATCH, :], 0.0).then_inc(zeroed, 1)
                pool.wait_ge(zeroed, 1)
                pool.memset(masked[:, BATCH, :], 0.0).then_inc(zeroed, 1)

            @block.tensor
            def _(pe):
                pe.wait_ge(w_in, 64)
                for h in range(H):
                    part = slice(h * L0_DH, (h + 1) * L0_DH)
                    mm = pe.matmul(ps_w[0:CDIM, h, 0:DIM], wk[part, :], wq[part, :], start=True, stop=True)
                mm.then_inc(qk_ready, 1)
                for h in range(H):
                    pe.wait_ge(qk_kept, 1)
                    if h >= 2:
                        pe.wait_ge(k_kept, h - 1)
                    for s in range(2):
                        mm = pe.matmul(ps_k[:, h % 2, s, 0:HALFKEYS], qk[:, h, :], m.ctxT[:, s * HALFKEYS:(s + 1) * HALFKEYS], start=True, stop=True)
                    mm.then_inc(k_ready, 1)
                pe.matmul(ps_w[0:CDIM, 0, :], wv[:], wf[:], start=True, stop=True).then_inc(vf_ready, 1)
                pe.wait_ge(vf_kept, 1)
                for n in range(BATCH * 2):
                    if n >= 3:
                        pe.wait_ge(v_kept, n - 2)
                    pe.matmul(ps_w[0:CTX_CHUNK, 1 + n % 3, :], m.ctxT[:, n * CTX_CHUNK:(n + 1) * CTX_CHUNK], vf[:], start=True,
                              stop=True).then_inc(v_ready, 1)

            @block.scalar
            def _(act):
                act.wait_ge(qk_ready, 1)
                nc.scalar.activation(qk[:], ps_w[0:CDIM, :, 0:DIM], ACT.Copy).then_inc(qk_kept, 1)
                act.wait_ge(vf_ready, 1)
                nc.scalar.activation(vf[:], ps_w[0:CDIM, 0, :], ACT.Copy, scale=m.row("mod_gate")[0:CDIM]).then_inc(vf_kept, 1)
                for n in range(BATCH * 2):
                    act.wait_ge(v_ready, n + 1)
                    nc.scalar.activation(values[0:CTX_CHUNK, n, :], ps_w[0:CTX_CHUNK, 1 + n % 3, :], ACT.Copy).then_inc(v_kept, 1)

            @block.vector
            def _(dve):
                c = Chain(dve, steps)
                step = lambda ins: (c.did(ins), c.wait())
                dve.wait_ge(bias_in, 16)
                step(dve.tensor_scalar(bias[:], bias[:], m.row("mod_gate")[0:1], None, ALU.mult))
                scales = bias[:].rearrange("o (n s d) -> o n s d", n=2, s=2)[:, :, 0, :]
                dve.tensor_scalar(scales, scales, 1.0, None, ALU.add).then_inc(bias_ready, 1)
                dve.wait_ge(masks_in, 32)
                step(dve.memset(weight[:], 0.0))
                step(dve.tensor_copy(weight[:, 1:TILES + 1], text8[:]))
                step(dve.tensor_scalar(weight[:], weight[:], 1.0 / H, None, ALU.mult))
                step(dve.tensor_copy(maskf[:], mask8[:]))
                step(dve.tensor_scalar(masked[:, 0:BATCH, :].rearrange("p b k -> p (b k)"), maskf[:], 1.0, BIG, ALU.subtract, ALU.mult))
                for h in range(H):
                    dve.wait_ge(k_ready, h + 1)
                    dst = keysT[:, 0:BATCH, h * KEYS:(h + 1) * KEYS]
                    dve.tensor_copy(dst, ps_k[:, h % 2, :, 0:HALFKEYS].rearrange("p s (v k) -> p s v k", v=2)).then_inc(k_kept, 1)


def film_tokens(nc, m, keysT, values, masked, weight, mod):
    H, W = L0_HEADS, L0_HEADS * KEYS
    keys = keysT[:].rearrange("p b k -> p (b k)")
    with ExitStack() as ctx:
        sb = lambda n, s: ctx.enter_context(nc.sbuf_tensor(f"filma_{n}", s, FP32))
        sem = lambda n: m.semaphore(nc, f"filma_{n}")
        tile_x = sb("tile_x", [DIM, 2, PART])
        score, rest = sb("score", [PART, 2, W]), sb("rest", [PART, 2, W])
        top = sb("top", [PART, 2, H, TOP])
        less, total, share = sb("less", [PART, 2, H]), sb("total", [PART, 2, H]), sb("share", [PART, 2, H])
        e_all, e_rest, e_top = sb("e_all", [PART, 2, W]), sb("e_rest", [PART, 2, W]), sb("e_top", [PART, H, TOP])
        prob = sb("prob", [PART, 2, W])
        probT = sb("probT", [CTX_CHUNK + 1, 2, PART])
        ps_s = ctx.enter_context(nc.psum_tensor("filma_ps_s", [PART, 2, 2 * BLOCK], FP32))
        ps_t = ctx.enter_context(nc.psum_tensor("filma_ps_t", [PART, BLOCK], FP32))
        ps_f = ctx.enter_context(nc.psum_tensor("filma_ps_f", [PART, BLOCK], FP32))
        names = ("tile_ready", "s_ready", "s_kept", "steps", "top_ready", "e_ready", "share_ready", "left_ready", "prob_ready", "t_ready", "t_kept", "f_ready", "f_kept", "zeroed")
        tile_ready, s_ready, s_kept, steps, top_ready, e_ready, share_ready, left_ready, prob_ready, t_ready, t_kept, f_ready, f_kept, zeroed = (sem(n) for n in names)
        with nc.Block() as block:
            @block.tensor
            def _(pe):
                start(pe, f_ready, f_ready, t_ready)
                def scores(turn, h):
                    if h >= 2:
                        turn, h = turn + 1, h - 2
                    n = turn * 2 + h
                    pe.wait_ge(tile_ready, n + 1)
                    base = (turn // 2) * W
                    pe.matmul(ps_s[:, h, 0:BLOCK], tile_x[:, h, :], keys[:, bass.ds(base, BLOCK)], start=True, stop=True)
                    pe.matmul(ps_s[:, h, BLOCK:W], tile_x[:, h, :], keys[:, bass.ds(base + BLOCK, W - BLOCK)], start=True, stop=True).then_inc(s_ready, 1)

                scores(0, 0)
                scores(0, 1)
                with pe.Fori(0, TILES // 2) as it:
                    for h in range(2):
                        n = it * 2 + h
                        pe.wait_ge(s_kept, n + 1 + START)
                        scores(it, h + 2)
                        pe.wait_ge(prob_ready, n + 2 + START)
                        pe.wait_ge(t_kept, n + START)
                        for c in range(2):
                            for g in range(H):
                                cols = slice(g * KEYS + c * CTX_CHUNK, g * KEYS + (c + 1) * CTX_CHUNK)
                                mm = pe.matmul(ps_t[0:CTX_CHUNK, c * PART:(c + 1) * PART], prob[:, h, cols], m.ident[:],
                                               start=(g == 0), stop=(g == H - 1))
                        mm.then_inc(t_ready, 1)
                        pe.wait_ge(t_kept, n + 1 + START)
                        pe.wait_ge(f_kept, n + 2 + START)
                        for c in range(2):
                            v = values[:, bass.ds((it // 2) * 2 + c, 1), :].rearrange("k o n -> k (o n)")
                            rows = CTX_CHUNK + 1 - c
                            mm = pe.matmul(ps_f[:], probT[0:rows, c, :], v[0:rows], start=(c == 0), stop=(c == 1))
                        mm.then_inc(f_ready, 1)

            @block.scalar
            def _(act):
                start(act, t_kept, e_ready)
                act.wait_ge(zeroed, 2)
                nc.scalar.activation(e_top[:, 0, 0:1], total[:, 0, 0:1], ACT.Exp).then_inc(e_ready, 1)
                with act.Fori(0, TILES // 2) as it:
                    for h in range(2):
                        n = it * 2 + h
                        act.wait_ge(top_ready, n + 1)
                        act.wait_ge(prob_ready, n + START)
                        act.wait_ge(share_ready, n + START)
                        act.wait_ge(e_ready, n + 1 + START)
                        for g in range(H):
                            cols = slice(g * KEYS, (g + 1) * KEYS)
                            bias = less[:, h, g:g + 1]
                            nc.scalar.activation(e_all[:, h, cols], score[:, h, cols], ACT.Exp, scale=L0_SCALE, bias=bias)
                            nc.scalar.activation(e_rest[:, h, cols], rest[:, h, cols], ACT.Exp, scale=L0_SCALE, bias=bias)
                            ins = nc.scalar.activation(e_top[:, g, :], top[:, h, g, :], ACT.Exp, scale=L0_SCALE, bias=bias,
                                                       accum_out=total[:, h, g:g + 1])
                        ins.then_inc(e_ready, 1)
                        act.wait_ge(t_ready, n + 1 + START)
                        act.wait_ge(f_ready, n + 2 * START)
                        nc.scalar.activation(probT[0:CTX_CHUNK, :, :].rearrange("k c t -> k (c t)"), ps_t[0:CTX_CHUNK, 0:2 * PART],
                                             ACT.Copy).then_inc(t_kept, 1)

            @block.gpsimd
            def _(pool):
                start(pool, prob_ready)
                pool.memset(probT[:], 1.0).then_inc(prob_ready, 1)
                with pool.Fori(0, TILES // 2) as it:
                    for h in range(2):
                        n = it * 2 + h
                        pool.wait_ge(t_ready, it * 2 + START)
                        pool.wait_ge(e_ready, n + 2 + START)
                        pool.tensor_tensor(prob[:, h, :], e_all[:, h, :], e_rest[:, h, :], ALU.subtract).then_inc(left_ready, 1)
                        pool.wait_ge(left_ready, n + 1)
                        pool.wait_ge(share_ready, n + 2 + START)
                        p3 = prob[:, h, :].rearrange("p (g k) -> p g k", g=H)
                        pool.tensor_tensor(p3, p3, share[:, h, :].unsqueeze(2).to_broadcast([PART, H, KEYS]), ALU.mult).then_inc(prob_ready, 1)

            @block.vector
            def _(dve):
                start(dve, s_kept, share_ready, f_kept)
                def fetch(tile, half):
                    dve.tensor_scalar(tile_x[:, half, :], m.xt[:, bass.ds(tile * PART, PART)], 1.0, None, ALU.mult).then_inc(tile_ready, 1)

                def use_sums(n, h):
                    dve.wait_ge(e_ready, n + 1 + START)
                    dve.wait_ge(prob_ready, n + START)
                    c.did(dve.reciprocal(share[:, h, :], total[:, h, :]))
                    c.wait()
                    dve.tensor_tensor(share[:, h, :], share[:, h, :], weight[:, bass.ds(n, 1)].to_broadcast([PART, H]),
                                      ALU.mult).then_inc(share_ready, 1)

                def store(n):
                    dve.wait_ge(f_ready, n - 1 + 2 * START)
                    dve.tensor_scalar(mod[:, bass.ds(n, 1), :].rearrange("p o n -> p (o n)"), ps_f[:], 1.0, None,
                                      ALU.mult).then_inc(f_kept, 1)

                dve.memset(total[:], 1.0).then_inc(zeroed, 1)
                dve.memset(ps_f[:], 0.0).then_inc(zeroed, 1)
                dve.wait_ge(zeroed, 2)
                c = Chain(dve, steps)
                fetch(0, 0)
                fetch(1, 1)
                with dve.Fori(0, TILES // 2) as it:
                    for h in range(2):
                        n = it * 2 + h
                        dve.wait_ge(s_ready, n + 1)
                        dve.wait_ge(e_ready, n + START)
                        s3 = score[:, h, :].rearrange("p (g k) -> p g k", g=H)
                        dve.tensor_tensor(s3, ps_s[:, h, 0:W].rearrange("p (g k) -> p g k", g=H),
                                          masked[:, bass.ds(it // 2, 1), :].to_broadcast([PART, H, KEYS]), ALU.add).then_inc(s_kept, 1)
                        dve.wait_ge(s_kept, n + 1 + START)
                        fetch(n + 2, h)
                        found = [0] * H
                        for r in range(TOP // 8):
                            src = score if r == 0 else rest
                            for g in range(H):
                                cols = slice(g * KEYS, (g + 1) * KEYS)
                                c.wait_for(found[g])
                                c.did(dve.max(top[:, h, g, 8 * r:8 * r + 8], src[:, h, cols]))
                                found[g] = c.n
                            for g in range(H):
                                cols = slice(g * KEYS, (g + 1) * KEYS)
                                c.wait_for(found[g])
                                c.did(dve.match_replace(rest[:, h, cols], top[:, h, g, 8 * r:8 * r + 8], src[:, h, cols], -BIG))
                                found[g] = c.n
                            if r == 0:
                                store(n)
                            if r == 1:
                                use_sums(n, 1 - h)
                        c.wait()
                        dve.tensor_scalar(less[:, h, :], top[:, h, :, 0], -L0_SCALE, None, ALU.mult).then_inc(top_ready, 1)
                    c.clear()
                store(TILES)
                use_sums(TILES, 1)
                store(TILES + 1)


def state_kernel(nc, m, a, kernel_dram):
    S = STATES
    with ExitStack() as ctx:
        sb = lambda n, s, dt=FP32: ctx.enter_context(nc.sbuf_tensor(f"ssmk_{n}", s, dt))
        sem = lambda n: m.semaphore(nc, f"ssmk_{n}")
        params = sb("params", [PART, 4, DIM])
        consts = sb("consts", [PART, 3 + FINE + COARSE])
        dt_row = sb("dt", [PART, DIM])
        two_n = sb("two_n", [PART, DIM], mybir.dt.int32)
        x, turns, tmp = sb("x", [PART, DIM]), sb("turns", [PART, DIM]), sb("tmp", [PART, DIM])
        ang_c, ang_s = sb("ang_c", [PART, DIM]), sb("ang_s", [PART, DIM])
        cosy, siny, half, th = sb("cosy", [PART, DIM]), sb("siny", [PART, DIM]), sb("half", [PART, DIM]), sb("th", [PART, DIM])
        wr, wi, qr, qi = sb("wr", [PART, DIM]), sb("wi", [PART, DIM]), sb("qr", [PART, DIM]), sb("qi", [PART, DIM])
        den, c1, c2 = sb("den", [PART, DIM]), sb("c1", [PART, DIM]), sb("c2", [PART, DIM])
        fine, mag, angle = sb("fine", [PART, DIM, FINE]), sb("mag", [PART, DIM, FINE]), sb("angle", [PART, DIM, FINE])
        cmag, cang = sb("cmag", [PART, DIM, COARSE]), sb("cang", [PART, DIM, COARSE])
        ccos, csin, coarse = sb("ccos", [PART, DIM, COARSE]), sb("csin", [PART, DIM, COARSE]), sb("coarse", [PART, DIM, COARSE])
        rows = sb("rows", [COARSE, DIM * FINE])
        ps_k = ctx.enter_context(nc.psum_tensor("ssm_ps_k", [PART, 8, BLOCK], FP32))
        names = ("params_in", "steps", "dve_ready", "act_done", "mags_ready", "k_ready", "k_kept", "k_out", "pool_steps")
        params_in, steps, dve_ready, act_done, mags_ready, k_ready, k_kept, k_out, pool_steps = (sem(n) for n in names)
        off_part, off_part_rad, quarter_rad = consts[:, 0:1], consts[:, 1:2], consts[:, 2:3]
        fine_l, coarse_l = consts[:, 3:3 + FINE], consts[:, 3 + FINE:3 + FINE + COARSE]
        across = lambda v, n: v.unsqueeze(2).to_broadcast([PART, DIM, n])
        along = lambda v, n: v.unsqueeze(1).to_broadcast([PART, DIM, n])
        with nc.Block() as block:
            @block.sync
            def _(sp):
                sp.dma_start(params[:], a["L0_xattn_AC"]).then_inc(params_in, 16)
                sp.dma_start(consts[:], a["ssm_consts"]).then_inc(params_in, 16)
                for half_rows in range(2):
                    sp.wait_ge(k_kept, 8)
                    part = slice(half_rows * 8, half_rows * 8 + 8)
                    sp.dma_start(kernel_dram[:, part, :].rearrange("d a b -> a d b"),
                                 rows[part, :].rearrange("a (d b) -> a d b", b=FINE)).then_inc(k_out, 16)
                sp.wait_ge(k_out, 32)

            @block.gpsimd
            def _(pool):
                pool.wait_ge(dve_ready, 1)
                pool.tensor_tensor(mag[:], across(x[:], FINE), along(fine_l, FINE), ALU.mult).then_inc(mags_ready, 1)
                pool.tensor_tensor(cmag[:], across(x[:], COARSE), along(coarse_l, COARSE), ALU.mult).then_inc(mags_ready, 1)

            @block.scalar
            def _(act):
                act.wait_ge(dve_ready, 1)
                nc.scalar.activation(th[:], x[:], ACT.Tanh, scale=0.5).then_inc(act_done, 1)
                act.wait_ge(mags_ready, 2)
                nc.scalar.activation(mag[:], mag[:], ACT.Exp).then_inc(act_done, 1)
                nc.scalar.activation(cmag[:], cmag[:], ACT.Exp).then_inc(act_done, 1)
                act.wait_ge(dve_ready, 2)
                nc.scalar.activation(cosy[:], ang_c[:], ACT.Sin, scale=-TWO_PI, bias=quarter_rad).then_inc(act_done, 1)
                nc.scalar.activation(siny[:], turns[:], ACT.Sin, scale=TWO_PI).then_inc(act_done, 1)
                nc.scalar.activation(half[:], turns[:], ACT.Sin, scale=TWO_PI / 2).then_inc(act_done, 1)
                act.wait_ge(dve_ready, 3)
                nc.scalar.activation(csin[:], csin[:], ACT.Sin, scale=-TWO_PI).then_inc(act_done, 1)
                nc.scalar.activation(ccos[:], ccos[:], ACT.Sin, scale=-TWO_PI, bias=quarter_rad).then_inc(act_done, 1)
                act.wait_ge(dve_ready, 4)
                nc.scalar.activation(fine[:], fine[:], ACT.Sin, scale=-TWO_PI, bias=off_part_rad).then_inc(act_done, 1)
                for g in range(8):
                    act.wait_ge(k_ready, g + 1)
                    nc.scalar.activation(rows[:, g * BLOCK:(g + 1) * BLOCK], ps_k[0:COARSE, g, :], ACT.Copy).then_inc(k_kept, 1)

            @block.vector
            def _(dve):
                c = Chain(dve, steps)
                step = lambda ins: (c.did(ins), c.wait())
                tt = lambda out, a0, a1, op: step(dve.tensor_tensor(out, a0, a1, op))
                ar, ai, cr, ci = (params[:, n, :] for n in range(4))

                def reduced(out, work, src, offset):
                    step(dve.tensor_scalar(work, src, offset, ROUND, ALU.add, ALU.add))
                    return dve.scalar_tensor_tensor(out, work, ROUND, src, ALU.subtract, ALU.subtract)

                log_dt = m.row("log_dt")
                step(dve.tensor_scalar(tmp[:], log_dt, LOG2_E, ROUND, ALU.mult, ALU.add))
                step(dve.tensor_scalar(tmp[:], tmp[:], ROUND, None, ALU.subtract))
                step(dve.scalar_tensor_tensor(x[:], tmp[:], -LN2_HIGH, log_dt, ALU.mult, ALU.add))
                step(dve.scalar_tensor_tensor(x[:], tmp[:], -LN2_LOW, x[:], ALU.mult, ALU.add))
                step(dve.tensor_scalar(two_n[:], tmp[:], 127.0, None, ALU.add))
                step(dve.tensor_scalar(two_n[:], two_n[:], 23, None, ALU.logical_shift_left))
                step(dve.tensor_scalar(dt_row[:], x[:], EXP_SERIES[0], None, ALU.mult))
                for factor in EXP_SERIES[1:]:
                    step(dve.scalar_tensor_tensor(dt_row[:], dt_row[:], factor, x[:], ALU.add, ALU.mult))
                step(dve.tensor_scalar(dt_row[:], dt_row[:], 1.0, None, ALU.add))
                tt(dt_row[:], dt_row[:], two_n[:].bitcast(FP32), ALU.mult)
                dve.wait_ge(params_in, 32)
                step(dve.tensor_scalar(turns[:], ai, 1.0 / (2 * 3.141592653589793), None, ALU.mult))
                tt(turns[:], turns[:], dt_row[:], ALU.mult)
                dve.tensor_tensor(x[:], ar, dt_row[:], ALU.mult).then_inc(dve_ready, 1)
                step(reduced(tmp[:], ang_s[:], turns[:], 0.0))
                step(dve.tensor_scalar(turns[:], tmp[:], -1.0, None, ALU.mult))
                reduced(ang_c[:], ang_s[:], turns[:], 0.25).then_inc(dve_ready, 1)
                tt(cang[:], across(turns[:], COARSE), along(coarse_l, COARSE), ALU.mult)
                step(reduced(csin[:], coarse[:], cang[:], 0.0))
                reduced(ccos[:], coarse[:], cang[:], 0.25).then_inc(dve_ready, 1)
                tt(angle[:], across(turns[:], FINE), along(fine_l, FINE), ALU.mult)
                step(dve.tensor_scalar(fine[:], angle[:], off_part, ROUND, ALU.add, ALU.add))
                dve.scalar_tensor_tensor(fine[:], fine[:], ROUND, angle[:], ALU.subtract, ALU.subtract).then_inc(dve_ready, 1)
                dve.wait_ge(act_done, 6)
                step(dve.tensor_scalar(tmp[:], th[:], -1.0, 1.0, ALU.mult, ALU.add))
                step(dve.reciprocal(tmp[:], tmp[:]))
                tt(th[:], th[:], tmp[:], ALU.mult)
                step(dve.tensor_scalar(th[:], th[:], 2.0, None, ALU.mult))
                tt(wr[:], th[:], cosy[:], ALU.mult)
                tt(half[:], half[:], half[:], ALU.mult)
                step(dve.scalar_tensor_tensor(wr[:], half[:], -2.0, wr[:], ALU.mult, ALU.add))
                step(dve.scalar_tensor_tensor(wi[:], th[:], 1.0, siny[:], ALU.add, ALU.mult))
                tt(den[:], ar, ar, ALU.mult)
                tt(tmp[:], ai, ai, ALU.mult)
                tt(den[:], den[:], tmp[:], ALU.add)
                step(dve.reciprocal(den[:], den[:]))
                tt(qr[:], wr[:], ar, ALU.mult)
                tt(tmp[:], wi[:], ai, ALU.mult)
                tt(qr[:], qr[:], tmp[:], ALU.add)
                tt(qr[:], qr[:], den[:], ALU.mult)
                tt(qi[:], wi[:], ar, ALU.mult)
                tt(tmp[:], wr[:], ai, ALU.mult)
                tt(qi[:], qi[:], tmp[:], ALU.subtract)
                tt(qi[:], qi[:], den[:], ALU.mult)
                tt(wr[:], cr, qr[:], ALU.mult)
                tt(tmp[:], ci, qi[:], ALU.mult)
                tt(wr[:], wr[:], tmp[:], ALU.subtract)
                tt(wi[:], cr, qi[:], ALU.mult)
                tt(tmp[:], ci, qr[:], ALU.mult)
                tt(wi[:], wi[:], tmp[:], ALU.add)
                top, low = slice(0, S), slice(S, 2 * S)
                step(dve.tensor_scalar(c1[top], wr[top], 2.0, None, ALU.mult))
                step(dve.tensor_scalar(c1[low], wi[low], -2.0, None, ALU.mult))
                step(dve.tensor_scalar(c2[top], wi[top], -2.0, None, ALU.mult))
                step(dve.tensor_scalar(c2[low], wr[low], -2.0, None, ALU.mult))
                dve.wait_ge(act_done, 8)
                tt(ccos[:], ccos[:], across(c1[:], COARSE), ALU.mult)
                tt(csin[:], csin[:], across(c2[:], COARSE), ALU.mult)
                tt(ccos[:], ccos[:], csin[:], ALU.add)
                tt(coarse[:], ccos[:], cmag[:], ALU.mult)
                dve.wait_ge(act_done, 9)
                dve.tensor_tensor(fine[:], fine[:], mag[:], ALU.mult).then_inc(dve_ready, 1)

            @block.tensor
            def _(pe):
                pe.wait_ge(dve_ready, 5)
                for d in range(DIM):
                    g, at = divmod(d, BLOCK // FINE)
                    mm = pe.matmul(ps_k[0:COARSE, g, at * FINE:(at + 1) * FINE], coarse[:, d, :], fine[:, d, :], start=True, stop=True)
                    if at == BLOCK // FINE - 1:
                        mm.then_inc(k_ready, 1)


def state_space(nc, m, a, kernel_dram, u, mod, z):
    with ExitStack() as ctx:
        sb = lambda n, s, dt=FP32: ctx.enter_context(nc.sbuf_tensor(f"conv_{n}", s, dt))
        sem = lambda n: m.semaphore(nc, f"conv_{n}")
        cos, sin = sb("cos", [PART, FREQ, SEQ]), sb("sin", [PART, FREQ, SEQ])
        turn = sb("turn", [PART, FREQ, 2])
        kern, kernT = sb("kern", [DIM, SEQ]), sb("kernT", [PART, FREQ, DIM])
        kr, ki, tmp = sb("kr", [PART, FREQ, DIM]), sb("ki", [PART, FREQ, DIM]), sb("tmp", [PART, DIM])
        kcs = sb("kcs", [PART, 2, DIM])
        p1, p2 = sb("p1", [PART, 2, BLOCK]), sb("p2", [PART, 2, BLOCK])
        yr, yi = sb("yr", [PART, FREQ, BLOCK]), sb("yi", [PART, FREQ, BLOCK])
        ps_t = ctx.enter_context(nc.psum_tensor("conv_ps_t", [PART, BLOCK], FP32))
        ps_k = ctx.enter_context(nc.psum_tensor("conv_ps_k", [PART, BLOCK], FP32))
        ps_x = ctx.enter_context(nc.psum_tensor("conv_ps_x", [PART, 2, 2, BLOCK], FP32))
        ps_y = ctx.enter_context(nc.psum_tensor("conv_ps_y", [PART, 2, BLOCK], FP32))
        names = ("tables_in", "kern_in", "steps", "u_ready", "kern_ready", "kern_turned", "kernT_kept", "k_ready", "k_kept", "x_ready", "products_ready", "yr_ready", "y_ready", "y_kept")
        tables_in, kern_in, steps, u_ready, kern_ready, kern_turned, kernT_kept, k_ready, k_kept, x_ready, products_ready, yr_ready, y_ready, y_kept = (sem(n) for n in names)
        wide = lambda v: v.unsqueeze(1).to_broadcast([PART, BATCH, DIM])
        four = lambda v: v.rearrange("p (b d) -> p b d", b=BATCH)
        with nc.Block() as block:
            @block.sync
            def _(sp):
                sp.dma_start(kern[:], kernel_dram.rearrange("d a b -> d (a b)")).then_inc(kern_in, 16)
                sp.dma_start(turn[:], a["half_turn"]).then_inc(tables_in, 16)
                sp.dma_start(cos[:], a["dft_cos"].rearrange("(c p) f -> p c f", p=PART)).then_inc(tables_in, 16)
                sp.dma_start(sin[:], a["dft_sin"].rearrange("(c p) f -> p c f", p=PART)).then_inc(tables_in, 16)
                sp.wait_ge(tables_in, 48)

            @block.vector
            def _(dve):
                c = Chain(dve, steps)
                step = lambda ins: (c.did(ins), c.wait())
                dve.wait_ge(kern_in, 16)
                dve.tensor_scalar(kern[:, 0:1], kern[:, 0:1], m.col("D_skip"), None, ALU.add).then_inc(kern_ready, 1)
                for t in range(BLOCKS):
                    rows = u[:, 4 * t:4 * t + 4, :]
                    part = mod[:, 4 * t + 2:4 * t + 6, :]
                    every = lambda name: m.row(name).unsqueeze(1).to_broadcast([PART, 4, DIM])
                    step(dve.tensor_tensor(rows, rows, every("in_g"), ALU.mult))
                    step(dve.tensor_tensor(rows, rows, every("in_b"), ALU.add))
                    step(dve.tensor_tensor(rows, rows, part[:, :, 0:DIM], ALU.mult))
                    dve.tensor_tensor(rows, rows, part[:, :, DIM:2 * DIM], ALU.add).then_inc(u_ready, 1)
                dve.wait_ge(tables_in, 48)
                for f in range(FREQ):
                    dve.wait_ge(k_ready, f + 1)
                    step(dve.tensor_copy(kcs[:], ps_k[:, 0:2 * DIM].rearrange("p (s d) -> p s d", s=2)))
                    kc, ks = kcs[:, 0, :], kcs[:, 1, :]
                    co, si = turn[:, f, 0:1], turn[:, f, 1:2]
                    step(dve.tensor_scalar(tmp[:], ks, si, None, ALU.mult))
                    step(dve.scalar_tensor_tensor(kr[:, f, :], kc, co, tmp[:], ALU.mult, ALU.add))
                    step(dve.tensor_scalar(tmp[:], ks, co, None, ALU.mult))
                    dve.scalar_tensor_tensor(ki[:, f, :], kc, si, tmp[:], ALU.mult, ALU.subtract).then_inc(k_kept, 1)
                for f in range(FREQ):
                    dve.wait_ge(k_kept, f + 1)
                    dve.wait_ge(x_ready, f + 1)
                    if f:
                        dve.wait_ge(yr_ready, 2 * f)
                    xc, xs = four(ps_x[:, f % 2, 0, :]), four(ps_x[:, f % 2, 1, :])
                    k_r, k_i = wide(kr[:, f, :]), wide(ki[:, f, :])
                    c.did(dve.tensor_tensor(four(p1[:, 0, :]), xc, k_r, ALU.mult))
                    c.did(dve.tensor_tensor(four(p1[:, 1, :]), xs, k_i, ALU.mult))
                    c.did(dve.tensor_tensor(four(p2[:, 0, :]), xs, k_r, ALU.mult))
                    c.wait()
                    dve.tensor_tensor(four(p2[:, 1, :]), xc, k_i, ALU.mult).then_inc(products_ready, 1)
                for l in range(FREQ):
                    dve.wait_ge(y_ready, l + 1)
                    rows = z[:].rearrange("p (b l) d -> p b l d", b=BATCH)[:, :, l, :]
                    part = mod[:, 2:TILES + 2, :].rearrange("p (b l) n -> p b l n", b=BATCH)[:, :, l, :]
                    base = m.xn[:].rearrange("p (b l) d -> p b l d", b=BATCH)[:, :, l, :]
                    dve.tensor_tensor(rows, four(ps_y[:, l % 2, :]), part[:, :, 2 * DIM:3 * DIM], ALU.mult).then_inc(y_kept, 1)
                    dve.wait_ge(y_kept, l + 1)
                    step(dve.tensor_tensor(rows, rows, part[:, :, 3 * DIM:4 * DIM], ALU.add))
                    step(dve.tensor_tensor(rows, rows, base, ALU.add))

            @block.gpsimd
            def _(pool):
                for f in range(FREQ):
                    pool.wait_ge(products_ready, f + 1)
                    pool.tensor_tensor(yr[:, f, :], p1[:, 0, :], p1[:, 1, :], ALU.add).then_inc(yr_ready, 1)
                    pool.tensor_tensor(yi[:, f, :], p2[:, 0, :], p2[:, 1, :], ALU.subtract).then_inc(yr_ready, 1)

            @block.scalar
            def _(act):
                act.wait_ge(kern_turned, 1)
                nc.scalar.activation(kernT[:].rearrange("l c d -> l (c d)"), ps_t[:], ACT.Copy).then_inc(kernT_kept, 1)

            @block.tensor
            def _(pe):
                pe.wait_ge(kern_ready, 1)
                for l in range(FREQ):
                    mm = pe.transpose(ps_t[:, l * PART:(l + 1) * PART], kern[:, l * PART:(l + 1) * PART], m.ident[:])
                mm.then_inc(kern_turned, 1)
                pe.wait_ge(tables_in, 48)
                pe.wait_ge(kernT_kept, 1)
                for f in range(FREQ):
                    if f:
                        pe.wait_ge(k_kept, f)
                    for s, table in enumerate((cos, sin)):
                        for l in range(FREQ):
                            mm = pe.matmul(ps_k[:, s * DIM:(s + 1) * DIM], table[:, l, f * PART:(f + 1) * PART], kernT[:, l, :],
                                           start=(l == 0), stop=(l == FREQ - 1))
                    mm.then_inc(k_ready, 1)
                pe.wait_ge(u_ready, BLOCKS)
                for f in range(FREQ):
                    if f >= 2:
                        pe.wait_ge(products_ready, f - 1)
                    for s, table in enumerate((cos, sin)):
                        for l in range(FREQ):
                            mm = pe.matmul(ps_x[:, f % 2, s, :], table[:, l, f * PART:(f + 1) * PART],
                                           u[:].rearrange("p (b l) d -> p b l d", b=BATCH)[:, :, l, :], start=(l == 0), stop=(l == FREQ - 1))
                    mm.then_inc(x_ready, 1)
                pe.wait_ge(yr_ready, 2 * FREQ)
                for l in range(FREQ):
                    if l >= 2:
                        pe.wait_ge(y_kept, l - 1)
                    for s, (table, y) in enumerate(((cos, yr), (sin, yi))):
                        for f in range(FREQ):
                            mm = pe.matmul(ps_y[:, l % 2, :], table[:, f, l * PART:(l + 1) * PART], y[:, f, :],
                                           start=(s == 0 and f == 0), stop=(s == 1 and f == FREQ - 1))
                    mm.then_inc(y_ready, 1)


def feed_forward(nc, m, a, z):
    CH = 4
    with ExitStack() as ctx:
        sb = lambda n, s, dt=FP32: ctx.enter_context(nc.sbuf_tensor(f"ff_{n}", s, dt))
        sem = lambda n: m.semaphore(nc, f"ff_{n}")
        w1, w2 = sb("w1", [DIM, CH * PART]), sb("w2", [PART, CH, DIM])
        hidden, y = sb("hidden", [PART, 3, BLOCK]), sb("y", [PART, TOKENS])
        ps_h = ctx.enter_context(nc.psum_tensor("ff_ps_h", [PART, 2, BLOCK], FP32))
        ps_a = ctx.enter_context(nc.psum_tensor("ff_ps_a", [PART, 2, BLOCK], FP32))
        ps_t = ctx.enter_context(nc.psum_tensor("ff_ps_t", [PART, 2, BLOCK], FP32))
        w_in, h_ready, hidden_ready, a_ready, y_kept, turned, z_added = (sem(n) for n in ("w_in", "h_ready", "hidden_ready", "a_ready", "y_kept", "turned", "z_added"))
        UNITS = BLOCKS * CH
        with nc.Block() as block:
            @block.sync
            def _(sp):
                sp.dma_start(w1[:], a["L0_xattn_W1"]).then_inc(w_in, 16)
                sp.dma_start(w2[:], a["L0_xattn_W2"].rearrange("(c p) d -> p c d", p=PART)).then_inc(w_in, 16)
                sp.wait_ge(w_in, 32)

            @block.tensor
            def _(pe):
                def up(n):
                    t, c = divmod(n, CH)
                    if n >= 2:
                        pe.wait_ge(hidden_ready, n - 1)
                    pe.matmul(ps_h[:, n % 2, :], w1[:, c * PART:(c + 1) * PART], m.xt[:, t * BLOCK:(t + 1) * BLOCK], start=True,
                              stop=True).then_inc(h_ready, 1)

                pe.wait_ge(w_in, 32)
                up(0)
                for n in range(UNITS):
                    t, c = divmod(n, CH)
                    if n + 1 < UNITS:
                        up(n + 1)
                    pe.wait_ge(hidden_ready, n + 1)
                    if c == 0 and t >= 2:
                        pe.wait_ge(y_kept, t - 1)
                    pe.matmul(ps_a[:, t % 2, :], w2[:, c, :], hidden[:, n % 3, :], start=(c == 0), stop=(c == CH - 1)).then_inc(a_ready, 1)
                for t in range(BLOCKS):
                    pe.wait_ge(y_kept, t + 1)
                    if t >= 2:
                        pe.wait_ge(z_added, t - 1)
                    for j in range(4):
                        i = 4 * t + j
                        mm = pe.transpose(ps_t[:, t % 2, j * PART:(j + 1) * PART], y[:, i * PART:(i + 1) * PART], m.ident[:])
                    mm.then_inc(turned, 1)

            @block.scalar
            def _(act):
                for n in range(UNITS):
                    t, c = divmod(n, CH)
                    act.wait_ge(h_ready, n + 1)
                    if n >= 3:
                        act.wait_ge(a_ready, n - 2)
                    nc.scalar.activation(hidden[:, n % 3, :], ps_h[:, n % 2, :], ACT.Gelu, bias=m.col("b1")[:, c:c + 1]).then_inc(hidden_ready, 1)

            @block.vector
            def _(dve):
                for t in range(BLOCKS):
                    dve.wait_ge(a_ready, CH * (t + 1))
                    dve.tensor_scalar(y[:, t * BLOCK:(t + 1) * BLOCK], ps_a[:, t % 2, :], m.col("b2"), None, ALU.add).then_inc(y_kept, 1)
                for t in range(BLOCKS):
                    rows = z[:, 4 * t:4 * t + 4, :].rearrange("p t d -> p (t d)")
                    dve.wait_ge(turned, t + 1)
                    dve.tensor_tensor(rows, rows, ps_t[:, t % 2, :], ALU.add).then_inc(z_added, 1)


def add_out(nc, m, z):
    with ExitStack() as ctx:
        steps = m.semaphore(nc, "addout_steps")
        gain = ctx.enter_context(nc.sbuf_tensor("addout_gain", [PART, 2, DIM], FP32))
        with nc.Block() as block:
            @block.vector
            def _(dve):
                c = Chain(dve, steps)
                c.did(dve.tensor_scalar(gain[:, 0, :], m.row("out_g"), m.gate[:, 0:1], None, ALU.mult))
                c.did(dve.tensor_scalar(gain[:, 1, :], m.row("out_b"), m.gate[:, 0:1], None, ALU.mult))
                every = lambda n: gain[:, n, :].unsqueeze(1).to_broadcast([PART, TILES, DIM])
                c.wait()
                c.did(dve.tensor_tensor(z[:], z[:], every(0), ALU.mult))
                c.wait()
                c.did(dve.tensor_tensor(m.x[:], m.x[:], every(1), ALU.add))
                c.wait()
                c.did(dve.tensor_tensor(m.x[:], m.x[:], z[:], ALU.add))
                c.wait()


def layer0_attention(nc, m, a):
    with ExitStack() as ctx:
        sb = lambda n, s: ctx.enter_context(nc.sbuf_tensor(f"l0_{n}", s, FP32))
        kernel_dram = nc.dram_tensor("state_kernel", (DIM, COARSE, FINE), FP32, kind="Internal").ap()
        state_kernel(nc, m, a, kernel_dram)
        z = sb("z", [PART, TILES, DIM])
        with ExitStack() as inner:
            mod = inner.enter_context(nc.sbuf_tensor("l0_mod", [PART, TILES + 2, 4 * DIM], FP32))
            film(nc, m, a, mod)
            u = inner.enter_context(nc.sbuf_tensor("l0_u", [PART, TILES, DIM], FP32))
            norm(nc, m, "l0_in", m.xn, 1e-5, u)
            state_space(nc, m, a, kernel_dram, u, mod, z)
        norm(nc, m, "l0_ffn", z, 1e-5, m.xn, m.xt, m.col("ffn_g"), m.col("ffn_b"))
        feed_forward(nc, m, a, z)
        norm(nc, m, "l0_out", z, 1e-5, z)
        add_out(nc, m, z)


def store(nc, m, out):
    with nc.semaphore("out_done") as out_done, nc.Block() as block:
        @block.sync
        def _(sp):
            sp.dma_start(out.rearrange("b (j p) d -> p (b j) d", p=PART), m.x[:]).then_inc(out_done, 16)
            sp.wait_ge(out_done, 16)


L1_FFN = Mixture("relu2", 1, "L1_ffn", 64)
L2_FFN = Mixture("swiglu", 2, "L2_ffn", 64)
L3_FFN = Mixture("gelu", 3, "L3_ffn", 8)


def norm_x(nc, m, name):
    norm(nc, m, name, m.x, 1e-5, m.xn, m.xt)


def norm_norm_x(nc, m, name, eps, gain, shift):
    norm_x(nc, m, f"{name}_x")
    norm(nc, m, name, m.xn, eps, m.xn, m.xt, m.col(gain), m.col(shift))


def layers(nc, m, a):
    norm_x(nc, m, "n0_att")
    layer0_attention(nc, m, a)
    norm_norm_x(nc, m, "n0_ffn", 1e-3, "tern_g", "tern_b")
    ternary(nc, m, a)
    m.clear_semaphores(nc)
    norm_norm_x(nc, m, "n1_att", 1e-5, "ln_l_g", "ln_l_b")
    latent_attention(nc, m, a)
    norm_x(nc, m, "n1_ffn")
    moe(nc, m, a, L1_FFN)
    m.clear_semaphores(nc)
    norm_x(nc, m, "n2_att")
    attention(nc, m, a, L2_ATT)
    norm_x(nc, m, "n2_ffn")
    moe(nc, m, a, L2_FFN)
    m.clear_semaphores(nc)
    norm_x(nc, m, "n3_att")
    attention(nc, m, a, L3_ATT)
    norm_x(nc, m, "n3_ffn")
    moe(nc, m, a, L3_FFN)


def program(nc, a, out, stages=layers):
    with ExitStack() as ctx:
        m = Memory(nc, ctx)
        setup(nc, m, a)
        stages(nc, m, a)
        store(nc, m, out)


def arrange(inputs):
    import numpy as np
    v = {k: np.asarray(x) for k, x in inputs.items()}
    v["L3_ffn_b1"] = v["L3_ffn_b1"].reshape(32, PART).T
    for p, heads, wo in (("L2_xattn", 16, "Wo"), ("L3_xattn", 8, "Wout")):
        hp = PART * heads // v[f"{p}_Wq"].shape[1]
        for w in ("Wq", "Wk", "Wv"):
            x = v.pop(f"{p}_{w}")
            v[f"{p}_{w}T"] = x.reshape(x.shape[0], heads // hp, PART).transpose(2, 1, 0).reshape(PART, -1)
        x = v.pop(f"{p}_{wo}")
        v[f"{p}_Wo"] = x.reshape(heads // hp, PART, DIM).transpose(1, 0, 2).reshape(PART, -1)
    column = lambda name: np.pad(v[name].reshape(-1, min(PART, v[name].size)).T, ((0, PART - min(PART, v[name].size)), (0, 0)))
    v["columns"] = np.concatenate([column(n) for n in (
        "L1_xattn_ln_l_g", "L1_xattn_ln_l_b", "L1_xattn_ln_x_g", "L1_xattn_ln_x_b", "L0_ffn_ln_gamma", "L0_ffn_ln_beta",
        "L0_xattn_g_ffn", "L0_xattn_b_ffn", "L0_xattn_b1", "L0_xattn_b2", "L0_xattn_D_skip")], axis=1)
    v["rows"] = np.concatenate([v[n].reshape(-1) for n in (
        "L1_xattn_qn_g", "L1_xattn_kn_g", "L1_xattn_bo", "L0_xattn_g_norm_in", "L0_xattn_b_norm_in", "L0_xattn_g_norm_out",
        "L0_xattn_b_norm_out", "L0_xattn_mod_gate", "L0_xattn_log_dt")])
    v["L1_xattn_WkvT"] = v["L1_xattn_Wkv"].T
    v["L1_xattn_WqkvT"] = np.concatenate([v["L1_xattn_Wq"], v["L1_xattn_Wlkv"]]).T
    v["L1_xattn_WoT"] = v["L1_xattn_Wo"].T
    for w in ("Wq", "Wk", "Wv"):
        v[f"L0_xattn_{w}T"] = v.pop(f"L0_xattn_{w}").T
    v["L0_xattn_Wfilm"] = np.concatenate([v.pop("L0_xattn_W_film_in"), v.pop("L0_xattn_W_film_out")], axis=1)
    v["L0_xattn_bfilm"] = np.concatenate([v.pop("L0_xattn_b_film_in"), v.pop("L0_xattn_b_film_out")])
    v["mask_BxS_bf1"] = v["mask_BxS_bf1"].reshape(TILES, PART).T
    v["L0_xattn_AC"] = np.stack([np.concatenate([v[f"L0_xattn_{n}"].T] * 2) for n in ("A_re", "A_im", "C_re", "C_im")], axis=1)
    consts = np.zeros((PART, 3 + FINE + COARSE), np.float32)
    consts[:STATES, 0] = 0.25
    consts[:STATES, 1] = TWO_PI / 4
    consts[:, 2] = TWO_PI / 4
    consts[:, 3:3 + FINE] = np.arange(FINE)
    consts[:, 3 + FINE:] = FINE * np.arange(COARSE)
    v["ssm_consts"] = consts
    half = np.arange(SEQ) + 0.5
    angle = 2 * np.pi / (2 * SEQ) * np.outer(half, half)
    v["dft_cos"], v["dft_sin"] = np.cos(angle).astype(np.float32), np.sin(angle).astype(np.float32)
    omega = (np.pi / (2 * SEQ) * half).reshape(FREQ, PART).T
    v["half_turn"] = (np.stack([np.cos(omega), np.sin(omega)], axis=2) / SEQ).astype(np.float32)
    v["L3_xattn_bo"] = v.pop("L3_xattn_bout")
    return {k: np.ascontiguousarray(x) for k, x in v.items()}


def kernel(**inputs):
    import concourse.bacc as _bacc
    from concourse import mybir as _mybir
    from concourse.bass_utils import run_bass_kernel_spmd as _run

    nc = _bacc.Bacc("TRN2", target_bir_lowering=False, num_devices=1)
    arrays = arrange(inputs)
    a = {n: nc.dram_tensor(n, v.shape, _mybir.dt.from_np(v.dtype), kind="ExternalInput").ap() for n, v in arrays.items()}
    out = nc.dram_tensor("out", (BATCH, SEQ, DIM), FP32, kind="ExternalOutput").ap()
    program(nc, a, out)
    return _run(nc, [arrays], core_ids=[0]).results[0]["out"]
```

```python
import concourse.bass as bass
from concourse import mybir
from contextlib import ExitStack

FP32 = mybir.dt.float32
BF16 = mybir.dt.bfloat16
U8 = mybir.dt.uint8
ALU = mybir.AluOpType
ACT = mybir.ActivationFunctionType
AX = mybir.AxisListType
FP32R = mybir.dt.float32r

BATCH, SEQ, DIM = 4, 512, 128
KEYS, CDIM = 154, 96
PART = 128
TOKENS = BATCH * SEQ
TILES = TOKENS // PART
BLOCKS = TOKENS // 512
BLOCK = 512
PER_BLOCK = BLOCK // PART
ALLKEYS = BATCH * KEYS
HALFKEYS = ALLKEYS // 2
BIG = 1.0e30
LAYERS = 4

COLS = {"ln_l_g": 1, "ln_l_b": 1, "ln_x_g": 1, "ln_x_b": 1, "tern_g": 1, "tern_b": 1, "ffn_g": 1, "ffn_b": 1,
        "b1": 4, "b2": 1, "D_skip": 1}
ROWS = {"qn_g": 64, "kn_g": 64, "L1_bo": 128, "in_g": 128, "in_b": 128, "out_g": 128, "out_b": 128,
        "mod_gate": 1, "log_dt": 128}


class Chain:

    def __init__(self, eng, sem):
        self.eng, self.sem, self.n = eng, sem, 0

    def did(self, ins):
        ins.then_inc(self.sem, 1)
        self.n += 1

    def wait(self):
        if self.n:
            self.eng.wait_ge(self.sem, self.n)

    def wait_for(self, n):
        if n:
            self.eng.wait_ge(self.sem, n)

    def clear(self):
        self.wait()
        self.eng.sem_clear(self.sem)
        self.n = 0


START = 3


def start(eng, *semaphores):
    for s in semaphores:
        eng.sem_inc(s, START)


class Memory:

    def __init__(self, nc, ctx):
        def sb(name, shape, dt=FP32):
            return ctx.enter_context(nc.sbuf_tensor(name, shape, dt))

        self.x = sb("x_tokens", [PART, TILES, DIM])
        self.xn = sb("x_norm", [PART, TILES, DIM])
        self.xt = sb("x_norm_T", [DIM, TOKENS + 2 * PART])
        self.ident = sb("ident", [PART, PART])
        self.ctxT = sb("ctx_T", [CDIM, ALLKEYS])
        self.gate = sb("gate", [PART, 2 * LAYERS])
        self.cols = sb("col_vectors", [PART, sum(COLS.values())])
        self.rows = sb("row_vectors", [PART, sum(ROWS.values())])

        self.semaphores = []

    def semaphore(self, nc, name):
        self.semaphores.append(nc.alloc_semaphore(name=name))
        return self.semaphores[-1]

    def clear_semaphores(self, nc):
        share = lambda n: self.semaphores[n::4]
        with nc.Block() as block:
            @block.scalar
            def _(act):
                for s in share(0):
                    act.sem_clear(s)

            @block.vector
            def _(dve):
                for s in share(1):
                    dve.sem_clear(s)

            @block.tensor
            def _(pe):
                for s in share(2):
                    pe.sem_clear(s)

            @block.gpsimd
            def _(pool):
                for s in share(3):
                    pool.sem_clear(s)
        for s in self.semaphores:
            nc.release_semaphore(s)
        self.semaphores = []

    @staticmethod
    def _at(names, name):
        first = 0
        for n, width in names.items():
            if n == name:
                return slice(first, first + width)
            first += width
        raise KeyError(name)

    def col(self, name):
        return self.cols[:, self._at(COLS, name)]

    def row(self, name):
        return self.rows[:, self._at(ROWS, name)]


def setup(nc, m, a):
    with ExitStack() as ctx:
        sem = lambda n: m.semaphore(nc, n)
        x_in, small_in, g_in = sem("x_in"), sem("small_in"), sem("g_in")
        vectors_in = sem("vectors_in")
        ident_steps, gate_done = sem("ident_steps"), sem("gate_done")
        ctx_sb = ctx.enter_context(nc.sbuf_tensor("ctx_rows", [KEYS // 2, 2 * BATCH, CDIM], FP32))
        graw = ctx.enter_context(nc.sbuf_tensor("gate_raw", [PART, 2 * LAYERS], FP32))
        ctx_ps = ctx.enter_context(nc.psum_tensor("ctx_ps", [PART, 2 * 512], FP32))
        ctx_turned, ctx_kept = sem("ctx_turned"), sem("ctx_kept")
        HK = KEYS // 2
        with nc.Block() as block:
            @block.sync
            def _(sp):
                sp.dma_start(ctx_sb[:], a["ctx_768"].rearrange("b (u k) c -> k (b u) c", k=HK)).then_inc(small_in, 16)
                sp.dma_start(m.x[:], a["x"].rearrange("b (j p) d -> p (b j) d", p=PART)).then_inc(x_in, 16)
                sp.wait_ge(x_in, 16)

            @block.scalar
            def _(act):
                for n, name in enumerate(("g_xattn", "g_ffn")):
                    act.dma_start(graw[:, n * LAYERS:(n + 1) * LAYERS],
                                  a[name].rearrange("(o n) -> o n", o=1).to_broadcast([PART, LAYERS])).then_inc(g_in, 16)
                act.dma_start(m.cols[:], a["columns"]).then_inc(vectors_in, 16)
                act.dma_start(m.rows[:], a["rows"].rearrange("(o n) -> o n", o=1).to_broadcast([PART, sum(ROWS.values())])).then_inc(vectors_in, 16)
                act.wait_ge(vectors_in, 32)
                act.wait_ge(g_in, 32)
                nc.scalar.activation(m.gate[:], graw[:], ACT.Tanh).then_inc(gate_done, 1)

            @block.gpsimd
            def _(pool):
                pool.memset(m.ident[:], 0.0).then_inc(ident_steps, 1)
                pool.wait_ge(ident_steps, 1)
                pool.affine_select(out=m.ident[:], in_=m.ident[:], compare_op=ALU.not_equal, fill=1.0, base=0,
                                   pattern=[[-1, PART]], channel_multiplier=1).then_inc(ident_steps, 1)
                pool.memset(m.xt[:, TOKENS:], 0.0).then_inc(ident_steps, 1)

            @block.tensor
            def _(pe):
                pe.wait_ge(ident_steps, 2)
                pe.wait_ge(small_in, 16)
                for u in range(2 * BATCH):
                    bank, at = divmod(u, 4)
                    pe.transpose(ctx_ps[0:CDIM, bank * 512 + at * HK:bank * 512 + at * HK + HK], ctx_sb[:, u, :],
                                 m.ident[0:HK, 0:HK]).then_inc(ctx_turned, 1)

            @block.vector
            def _(dve):
                for bank in range(2):
                    dve.wait_ge(ctx_turned, 4 * (bank + 1))
                    dve.tensor_copy(m.ctxT[:, bank * HALFKEYS:(bank + 1) * HALFKEYS],
                                    ctx_ps[0:CDIM, bank * 512:bank * 512 + HALFKEYS]).then_inc(ctx_kept, 1)


def norm(nc, m, name, src, eps, dst, turned_to=None, T_scale=None, T_bias=None):
    with ExitStack() as ctx:
        sb = lambda n, s: ctx.enter_context(nc.sbuf_tensor(f"{name}_{n}", s, FP32))
        sem = lambda n: m.semaphore(nc, f"{name}_{n}")
        stats, moments = sb("stats", [PART, TILES, 6]), sb("moments", [PART, TILES, 2])
        var, sd, rstd = sb("var", [PART, TILES]), sb("sd", [PART, TILES]), sb("rstd", [PART, TILES])
        stats_done, moments_done, var_done, sd_done = sem("stats_done"), sem("moments_done"), sem("var_done"), sem("sd_done")
        rstd_done, normed, turned, kept = sem("rstd_done"), sem("normed"), sem("turned"), sem("kept")
        turn = ctx.enter_context(nc.psum_tensor(f"{name}_turn", [PART, BLOCKS, BLOCK], FP32)) if turned_to is not None else None
        with nc.Block() as block:
            @block.vector
            def _(dve):
                for i in range(TILES):
                    dve.bn_stats(stats[:, i, :], src[:, i, :]).then_inc(stats_done, 1)
                for i in range(TILES):
                    dve.wait_ge(stats_done, i + 1)
                    dve.bn_aggr(moments[:, i, :], stats[:, i, :]).then_inc(moments_done, 1)
                dve.wait_ge(moments_done, TILES)
                dve.tensor_scalar(var[:], moments[:, :, 1], eps, None, ALU.add).then_inc(var_done, 1)
                dve.wait_ge(sd_done, 1)
                dve.reciprocal(rstd[:], sd[:]).then_inc(rstd_done, 1)
                dve.wait_ge(rstd_done, 1)
                for i in range(TILES):
                    dve.tensor_scalar(dst[:, i, :], src[:, i, :], moments[:, i, 0:1], rstd[:, i:i + 1],
                                      ALU.subtract, ALU.mult).then_inc(normed, 1)

            @block.scalar
            def _(act):
                act.wait_ge(var_done, 1)
                nc.scalar.activation(sd[:], var[:], ACT.Sqrt).then_inc(sd_done, 1)
                if turned_to is not None:
                    for t in range(BLOCKS):
                        act.wait_ge(turned, PER_BLOCK * (t + 1))
                        nc.scalar.activation(turned_to[:, t * BLOCK:(t + 1) * BLOCK], turn[:, t, :], ACT.Identity,
                                             scale=1.0 if T_scale is None else T_scale,
                                             bias=0.0 if T_bias is None else T_bias).then_inc(kept, 1)

            @block.tensor
            def _(pe):
                if turned_to is not None:
                    for i in range(TILES):
                        pe.wait_ge(normed, i + 1)
                        pe.transpose(turn[:, i // PER_BLOCK, i % PER_BLOCK * PART:(i % PER_BLOCK + 1) * PART],
                                     dst[:, i, :], m.ident[:]).then_inc(turned, 1)


def product3(pe, out, w, x):
    (w_high, w_low), (x_high, x_low) = w, x
    pe.matmul(out, w_high, x_high, start=True, stop=False)
    pe.matmul(out, w_high, x_low, start=False, stop=False)
    return pe.matmul(out, w_low, x_high, start=False, stop=True)


class Mixture:

    def __init__(self, kind, layer, prefix, experts, norm_eps=1e-5):
        self.kind, self.layer, self.prefix, self.experts = kind, layer, prefix, experts
        self.hidden = 4096 // experts


def moe(nc, m, a, mix):
    E, kind, p = mix.experts, mix.kind, mix.prefix
    CHUNKS, SLOTS = 32, 4
    TURNS = CHUNKS // SLOTS
    with ExitStack() as ctx:
        sb = lambda n, s, dt=FP32: ctx.enter_context(nc.sbuf_tensor(f"{p}_{n}", s, dt))
        sem = lambda n: m.semaphore(nc, f"{p}_{n}")
        share_dram = nc.dram_tensor(f"{p}_shares", (E, TOKENS), FP32, kind="Internal").ap()
        shareT = sb("share_T", [E, TOKENS])
        share = sb("share", [PART, 1 if kind == "gelu" else SLOTS, TOKENS])
        SHARES = BLOCKS if kind == "gelu" else SLOTS
        share_in = [sem(f"share_in{j}") for j in range(SHARES)]
        UPS = 2 if kind == "swiglu" else 1
        up = sb("up", [DIM, SLOTS, UPS, PART])
        up_high, up_low = sb("up_high", [DIM, SLOTS, UPS, PART], FP32R), sb("up_low", [DIM, SLOTS, UPS, PART], FP32R)
        x_high, x_low = sb("x_high", [DIM, TOKENS], FP32R), sb("x_low", [DIM, TOKENS], FP32R)
        down = sb("down", [PART, SLOTS, DIM])
        bias = sb("hidden_bias", [PART, CHUNKS + SLOTS]) if kind == "gelu" else None
        bias_now = sb("hidden_bias_now", [PART, SLOTS]) if kind == "gelu" else None
        act_a = sb("act_a", [PART, 4, BLOCK])
        act_b = sb("act_b", [PART, 2, BLOCK])
        hidden = sb("hidden", [PART, 2, BLOCK])
        y = sb("y", [PART, TOKENS])
        up_in, down_in = [sem(f"up_in{j}") for j in range(SLOTS)], [sem(f"down_in{j}") for j in range(SLOTS)]
        up_masked, up_split, x_masked, x_split, w_used = sem("up_masked"), sem("up_split"), sem("x_masked"), sem("x_split"), sem("w_used")
        h_ready = sem("h_ready")
        act_ready, act2_ready, hid_ready, hid_used = sem("act_ready"), sem("act2_ready"), sem("hid_ready"), sem("hid_used")
        first_h, first_act, first_used = sem("first_h"), sem("first_act"), sem("first_used")
        acc_kept, y_turned, x_added = sem("acc_kept"), sem("y_turned"), sem("x_added")
        first_in = sem("first_in")
        bias_set = sem("bias_set")
        AHEAD = 3 if kind == "relu2" else 2
        UNITS = SLOTS * BLOCKS
        FIRST_LOADS = {"relu2": 2, "swiglu": 3, "gelu": 2}[kind]
        first_relu = sem("first_relu")

        def up_rows(c, turn, j):
            if kind == "relu2":
                return [a[p + "_up_w"][bass.ds(c * 2, 2)].rearrange("e h i -> h e i")]
            if kind == "swiglu":
                return [a[p + "_expert_gate_k"][bass.ds(c * 2, 2)].rearrange("e h i -> h e i"),
                        a[p + "_expert_up_k"][bass.ds(c * 2, 2)].rearrange("e h i -> h e i")]
            return [a[p + "_W1"][bass.ds(turn, 1), :, j * PART:(j + 1) * PART].rearrange("o h i -> h o i")]

        if kind == "relu2":
            down_all = a[p + "_down_w"].rearrange("e i h -> (e i) h")
        elif kind == "swiglu":
            down_all = a[p + "_expert_down_k"].rearrange("e i h -> (e i) h")
        else:
            down_all = a[p + "_W2"].rearrange("e i h -> (e i) h")
        SHARED = {"relu2": [PART, PART], "swiglu": [64], "gelu": []}[kind]
        if SHARED:
            s_up = sb("shared_up", [DIM, len(SHARED), SHARED[0]])
            s_up2 = sb("shared_up2", [DIM, 1, 64]) if kind == "swiglu" else None
            s_down = sb("shared_down", [SHARED[0], len(SHARED), DIM])
        else:
            s_down = sb("bias_down", [8, DIM])

        def load_up(sp, j, turn):
            for n, rows in enumerate(up_rows(turn * SLOTS + j, turn, j)):
                sp.dma_start(up[:, j, n, :].rearrange("p (e i) -> p e i", e=rows.shape[1]), rows).then_inc(up_in[j], 16)

        def load_down(sp, j, turn):
            sp.dma_start(down[:, j, :], down_all[bass.ds((turn * SLOTS + j) * PART, PART), :]).then_inc(down_in[j], 16)

        def first_loads(sp):
            if kind == "relu2":
                sp.dma_start(s_up[:], a[p + "_shared_up_w"].rearrange("h (c i) -> h c i", i=PART)).then_inc(first_in, 16)
                sp.dma_start(s_down[:], a[p + "_shared_down_w"].rearrange("(c i) h -> i c h", i=PART)).then_inc(first_in, 16)
            elif kind == "swiglu":
                sp.dma_start(s_up[:, 0, :], a[p + "_shared_gate_w"]).then_inc(first_in, 16)
                sp.dma_start(s_up2[:, 0, :], a[p + "_shared_up_w"]).then_inc(first_in, 16)
                sp.dma_start(s_down[:, 0, :], a[p + "_shared_down_w"]).then_inc(first_in, 16)
            else:
                sp.dma_start(s_down[:], a[p + "_b2"]).then_inc(first_in, 16)
                sp.dma_start(bias[:, 0:CHUNKS], a[p + "_b1"]).then_inc(first_in, 16)
            for j in range(SLOTS):
                load_up(sp, j, 0)
                load_down(sp, j, 0)

        def split_x(pool):
            for t in range(BLOCKS):
                cols = slice(t * BLOCK, (t + 1) * BLOCK)
                pool.tensor_copy(x_high[:, cols], m.xt[:, cols]).then_inc(x_masked, 1)
                pool.wait_ge(x_masked, t + 1)
                pool.tensor_tensor(x_low[:, cols], m.xt[:, cols], x_high[:, cols], ALU.subtract).then_inc(x_split, 1)

        route(nc, m, a, mix, shareT, share_dram, first_loads, split_x)
        ps_acc = ctx.enter_context(nc.psum_tensor(f"{p}_acc", [PART, BLOCKS, BLOCK], FP32))
        ps_h = ctx.enter_context(nc.psum_tensor(f"{p}_h", [PART, 4, BLOCK], FP32))

        with nc.Block() as block:
            @block.sync
            def _(sp):
                def load_share(j, turn):
                    for e in range(2):
                        row = share_dram[bass.ds((turn * SLOTS + j) * 2 + e, 1), :].to_broadcast([64, TOKENS])
                        sp.dma_start(share[e * 64:(e + 1) * 64, j, :], row).then_inc(share_in[j], 16)

                def load_share_block(t, turn):
                    row = share_dram[bass.ds(turn, 1), t * BLOCK:(t + 1) * BLOCK].to_broadcast([PART, BLOCK])
                    sp.dma_start(share[:, 0, t * BLOCK:(t + 1) * BLOCK], row).then_inc(share_in[t], 16)

                for j in range(SLOTS):
                    if kind == "gelu":
                        load_share_block(j, 0)
                    else:
                        load_share(j, 0)
                with sp.Fori(0, TURNS - 1) as it:
                    for j in range(SLOTS):
                        sp.wait_ge(up_split, it * SLOTS + j + 1)
                        load_up(sp, j, it + 1)
                        sp.wait_ge(w_used, it * SLOTS + j + 1 + START)
                        load_down(sp, j, it + 1)
                        if kind == "gelu":
                            if j == SLOTS - 2:
                                for t in range(BLOCKS):
                                    sp.wait_ge(hid_ready, (it + 1) * UNITS - (BLOCKS - 1 - t) + START)
                                    load_share_block(t, it + 1)
                        else:
                            load_share(j, it + 1)
                for j in range(SLOTS):
                    sp.wait_ge(up_split, (TURNS - 1) * SLOTS + j + 1)
                    load_up(sp, j, 0)
                for j in range(SLOTS):
                    sp.wait_ge(up_in[j], 16 * UPS * (TURNS + 1))

            @block.gpsimd
            def _(pool):
                def low_part(turn, j):
                    pool.wait_ge(up_masked, turn * SLOTS + j + 1)
                    pool.tensor_tensor(up_low[:, j], up[:, j], up_high[:, j], ALU.subtract).then_inc(up_split, 1)

                for j in range(SLOTS):
                    low_part(0, j)
                with pool.Fori(0, TURNS) as it:
                    for j in range(SLOTS):
                        low_part(it + 1, j)

            @block.tensor
            def _(pe):
                start(pe, hid_used, w_used)
                pe.wait_ge(first_in, 16 * FIRST_LOADS)
                if kind == "gelu":
                    for t in range(BLOCKS):
                        pe.matmul(ps_acc[:, t, :], s_down[:], shareT[0:8, t * BLOCK:(t + 1) * BLOCK], start=True, stop=False,
                                  skip_group_check=True)
                else:
                    n = 0
                    for s, width in enumerate(SHARED):
                        for t in range(BLOCKS):
                            if n >= 2 or (kind == "swiglu" and n):
                                pe.wait_ge(first_act, n - 1 if kind == "relu2" else n)
                            rhs = m.xt[:, t * BLOCK:(t + 1) * BLOCK]
                            if kind == "relu2":
                                pe.matmul(ps_h[0:width, n % 2, :], s_up[:, s, :], rhs, start=True, stop=True).then_inc(first_h, 1)
                            else:
                                pe.matmul(ps_h[0:width, 0, :], s_up[:, s, :], rhs, start=True, stop=True)
                                pe.matmul(ps_h[0:width, 1, :], s_up2[:, s, :], rhs, start=True, stop=True).then_inc(first_h, 1)
                            pe.wait_ge(first_act, n + 1)
                            pe.matmul(ps_acc[:, t, :], s_down[0:width, s, :], hidden[0:width, n % 2, :],
                                      start=(s == 0), stop=False, skip_group_check=True).then_inc(first_used, 1)
                            n += 1

                def products(it, k, first=False):
                    j, t = divmod(k, BLOCKS)
                    n = it * UNITS + k
                    x = [v[:, t * BLOCK:(t + 1) * BLOCK] for v in (x_high, x_low)]
                    if t == 0:
                        pe.wait_ge(up_split, it * SLOTS + j + 1)
                    if not first:
                        pe.wait_ge(act_ready, n - (3 if AHEAD == 3 else 1) + START)
                    for u in range(UPS):
                        if u and not first:
                            pe.wait_ge(act2_ready, n - 1 + START)
                        bank = k % 2 * 2 + u if UPS == 2 else k % 4
                        product3(pe, ps_h[:, bank, :], (up_high[:, j, u, :], up_low[:, j, u, :]), x).then_inc(h_ready, 1)

                pe.wait_ge(x_split, BLOCKS)
                for k in range(AHEAD):
                    products(0, k, first=True)
                with pe.Fori(0, TURNS) as it:
                    for k in range(UNITS):
                        j, t = divmod(k, BLOCKS)
                        if t == 0:
                            pe.wait_ge(down_in[j], (it + 1) * 16)
                        products(it, k + AHEAD) if k + AHEAD < UNITS else products(it + 1, k + AHEAD - UNITS)
                        pe.wait_ge(hid_ready, it * UNITS + k + 1 + START)
                        mm = pe.matmul(ps_acc[:, t, :], down[:, j, :], hidden[:, k % 2, :], start=False, stop=False,
                                       skip_group_check=True)
                        mm.then_inc(w_used if t == BLOCKS - 1 else hid_used, 1)
                for t in range(BLOCKS):
                    pe.wait_ge(acc_kept, t + 1)
                    if t >= 2:
                        pe.wait_ge(x_added, t - 1)
                    for at in range(PER_BLOCK):
                        i = t * PER_BLOCK + at
                        mm = pe.transpose(ps_h[:, t % 2, at * PART:(at + 1) * PART], y[:, i * PART:(i + 1) * PART], m.ident[:])
                    mm.then_inc(y_turned, 1)

            @block.scalar
            def _(act):
                start(act, act_ready, *([act2_ready] if kind == "relu2" else []))
                n = 0
                for s, width in enumerate(SHARED):
                    for t in range(BLOCKS):
                        act.wait_ge(first_h, n + 1)
                        if kind == "relu2":
                            nc.scalar.activation(act_a[:, n % 2, :], ps_h[:, n % 2, :], ACT.Relu).then_inc(first_relu, 1)
                            if n >= 2:
                                act.wait_ge(first_used, n - 1)
                            act.wait_ge(first_relu, n + 1)
                            nc.scalar.activation(hidden[:, n % 2, :], act_a[:, n % 2, :], ACT.Square).then_inc(first_act, 1)
                        else:
                            if n:
                                act.wait_ge(first_act, n)
                            nc.scalar.activation(act_a[0:width, 0, :], ps_h[0:width, 0, :], ACT.Silu).then_inc(first_relu, 1)
                        n += 1
                if kind == "relu2":
                    act.wait_ge(first_act, n)

                def relu(n, k):
                    act.wait_ge(h_ready, n + 1)
                    nc.scalar.activation(act_a[:, k % 4, :], ps_h[:, k % 4, :], ACT.Relu).then_inc(act_ready, 1)

                if kind == "relu2":
                    relu(0, 0)
                with act.Fori(0, TURNS) as it:
                    for k in range(UNITS):
                        n = it * UNITS + k
                        if kind == "swiglu":
                            act.wait_ge(h_ready, it * (2 * UNITS) + 2 * k + 1)
                            act.wait_ge(act2_ready, it * UNITS + max(k - 1, 0) + START)
                            nc.scalar.activation(act_a[:, k % 2, :], ps_h[:, k % 2 * 2, :], ACT.Silu).then_inc(act_ready, 1)
                        elif kind == "relu2":
                            act.wait_ge(act2_ready, it * UNITS + max(k - 1, 0) + START)
                            relu(n + 1, k + 1)
                            act.wait_ge(act_ready, n + 1 + START)
                            act.wait_ge(hid_ready, it * UNITS + max(k - 1, 0) + START)
                            nc.scalar.activation(act_b[:, k % 2, :], act_a[:, k % 4, :], ACT.Square).then_inc(act2_ready, 1)
                        else:
                            act.wait_ge(hid_ready, it * UNITS + max(k - 1, 0) + START)
                            act.wait_ge(h_ready, n + 1)
                            j = k // BLOCKS
                            if k % BLOCKS == 0:
                                act.wait_ge(bias_set, it * SLOTS + j + 2)
                            nc.scalar.activation(act_b[:, k % 2, :], ps_h[:, k % 4, :], ACT.Gelu,
                                                 bias=bias_now[:, j:j + 1]).then_inc(act_ready, 1)
                for t in range(BLOCKS):
                    act.wait_ge(w_used, CHUNKS + START)
                    nc.scalar.activation(y[:, t * BLOCK:(t + 1) * BLOCK], ps_acc[:, t, :], ACT.Copy).then_inc(acc_kept, 1)

            @block.vector
            def _(dve):
                def mask_up(turn, j):
                    dve.wait_ge(up_in[j], (turn + 1) * (16 * UPS))
                    dve.tensor_copy(up_high[:, j], up[:, j]).then_inc(up_masked, 1)

                for j in range(SLOTS):
                    mask_up(0, j)
                start(dve, hid_ready, *([act2_ready] if kind == "swiglu" else []))
                if kind == "swiglu":
                    for n in range(BLOCKS):
                        dve.wait_ge(first_relu, n + 1)
                        if n >= 2:
                            dve.wait_ge(first_used, n - 1)
                        dve.tensor_tensor(hidden[0:64, n % 2, :], act_a[0:64, 0, :], ps_h[0:64, 1, :],
                                          ALU.mult).then_inc(first_act, 1)
                    dve.wait_ge(first_used, BLOCKS)
                elif kind == "relu2":
                    dve.wait_ge(first_used, 2 * BLOCKS)
                if kind == "gelu":
                    dve.memset(bias[:, CHUNKS:], 0.0).then_inc(bias_set, 1)
                    dve.wait_ge(first_in, 16 * FIRST_LOADS)
                    dve.wait_ge(bias_set, 1)
                    for j in range(SLOTS - 1):
                        dve.tensor_copy(bias_now[:, j:j + 1], bias[:, j:j + 1]).then_inc(bias_set, 1)
                    dve.tensor_copy(bias_now[:, SLOTS - 1:], bias[:, SLOTS - 1:SLOTS]).then_inc(bias_set, 1)
                with dve.Fori(0, TURNS) as it:
                    for k in range(UNITS):
                        n = it * UNITS + k
                        if kind == "swiglu":
                            dve.wait_ge(act_ready, n + 1 + START)
                            dve.wait_ge(h_ready, it * (2 * UNITS) + 2 * k + 2)
                            dve.wait_ge(hid_ready, it * UNITS + max(k - 1, 0) + START)
                            dve.tensor_tensor(act_b[:, k % 2, :], act_a[:, k % 2, :], ps_h[:, k % 2 * 2 + 1, :],
                                              ALU.mult).then_inc(act2_ready, 1)
                            dve.wait_ge(act2_ready, n + 1 + START)
                        elif kind == "relu2":
                            dve.wait_ge(act2_ready, n + 1 + START)
                        else:
                            dve.wait_ge(act_ready, n + 1 + START)
                        j, t = divmod(k, BLOCKS)
                        if kind == "gelu":
                            if j == 0:
                                dve.wait_ge(share_in[t], (it + 1) * 16)
                        elif t == 0:
                            dve.wait_ge(share_in[j], (it + 1) * 32)
                        before = k - 2
                        if before >= 0:
                            tj, tt = divmod(before, BLOCKS)
                            if tt == BLOCKS - 1:
                                dve.wait_ge(w_used, it * SLOTS + tj + 1 + START)
                            else:
                                dve.wait_ge(hid_used, it * (UNITS - SLOTS) + tj * (BLOCKS - 1) + tt + 1 + START)
                        elif k == 0:
                            dve.wait_ge(hid_used, it * (UNITS - SLOTS) + START)
                        else:
                            dve.wait_ge(w_used, it * SLOTS + START)
                        dve.tensor_tensor(hidden[:, k % 2, :], act_b[:, k % 2, :],
                                          share[:, 0 if kind == "gelu" else j, t * BLOCK:(t + 1) * BLOCK],
                                          ALU.mult).then_inc(hid_ready, 1)
                        if t == BLOCKS - 1:
                            dve.wait_ge(h_ready, (it * UNITS + (j + 1) * BLOCKS) * UPS)
                            mask_up(it + 1, j)
                        if kind == "gelu" and k % BLOCKS == BLOCKS - 1:
                            j = k // BLOCKS
                            dve.tensor_scalar(bias_now[:, j:j + 1], bias[:, bass.ds(it * SLOTS + (SLOTS + j), 1)], 1.0, None,
                                              ALU.mult).then_inc(bias_set, 1)
                for t in range(BLOCKS):
                    dve.wait_ge(y_turned, t + 1)
                    rows = m.x[:, t * PER_BLOCK:(t + 1) * PER_BLOCK, :].rearrange("p t d -> p (t d)")
                    dve.scalar_tensor_tensor(rows, ps_h[:, t % 2, :], m.gate[:, LAYERS + mix.layer:LAYERS + mix.layer + 1],
                                             rows, ALU.mult, ALU.add).then_inc(x_added, 1)


def route(nc, m, a, mix, shareT, share_dram, first_loads, split_x):
    E, kind, p = mix.experts, mix.kind, mix.prefix
    with ExitStack() as ctx:
        sb = lambda n, s, dt=FP32: ctx.enter_context(nc.sbuf_tensor(f"{p}_r_{n}", s, dt))
        sem = lambda n: m.semaphore(nc, f"{p}_r_{n}")
        router = sb("router", [DIM, E])
        offset = sb("offset", [PART, E])
        earlier = sb("earlier", [PART, 8, 8])
        score, pick = sb("score", [PART, TILES, E]), sb("pick", [PART, TILES, E])
        work, work2 = sb("work", [PART, TILES, E]), sb("work2", [PART, TILES, E])
        pair, pair2 = sb("pair", [PART, TILES, 64]), sb("pair2", [PART, TILES, 64])
        one, two, three = sb("one", [PART, TILES, 8]), sb("two", [PART, TILES, 8]), sb("three", [PART, TILES, 8])
        top = sb("top", [PART, TILES, 8])
        total = sb("total", [PART, TILES])
        logits = ctx.enter_context(nc.psum_tensor(f"{p}_logits", [PART, TILES, E], FP32))
        turn = ctx.enter_context(nc.psum_tensor(f"{p}_turn", [PART, 4, BLOCK], FP32))
        router_in, offset_in, router_turned, router_kept = sem("router_in"), sem("offset_in"), sem("router_turned"), sem("router_kept")
        logits_ready, score_ready, steps, acts = sem("logits_ready"), sem("score_ready"), sem("steps"), sem("acts")
        shares_ready, turned, kept, built, shares_out = sem("shares_ready"), sem("turned"), sem("kept"), sem("built"), sem("shares_out")
        rowsT = sb("router_rows", [64, DIM]) if kind == "relu2" else None

        with nc.Block() as block:
            @block.sync
            def _(sp):
                if kind == "relu2":
                    sp.dma_start(rowsT[:], a[p + "_router_w"]).then_inc(router_in, 16)
                    sp.dma_start(offset[:], a[p + "_correction_bias"].rearrange("(o e) -> o e", o=1).to_broadcast([PART, E])).then_inc(offset_in, 16)
                elif kind == "swiglu":
                    sp.dma_start(router[:], a[p + "_router_w"]).then_inc(router_in, 16)
                else:
                    sp.dma_start(router[:], a[p + "_Wg"]).then_inc(router_in, 16)
                    sp.dma_start(offset[:], a[p + "_bg"].rearrange("(o e) -> o e", o=1).to_broadcast([PART, E])).then_inc(offset_in, 16)
                first_loads(sp)
                sp.wait_ge(router_in, 16)
                for t in range(BLOCKS):
                    sp.wait_ge(kept, t + 1)
                    sp.dma_start(share_dram[:, t * BLOCK:(t + 1) * BLOCK], shareT[:, t * BLOCK:(t + 1) * BLOCK]).then_inc(shares_out, 16)
                sp.wait_ge(shares_out, 16 * BLOCKS)

            @block.gpsimd
            def _(pool):
                made = Chain(pool, built)
                made.did(pool.memset(earlier[:], 1.0))
                made.wait()
                made.did(pool.affine_select(out=earlier[:], in_=earlier[:], compare_op=ALU.is_gt, fill=0.0, base=0,
                                            pattern=[[1, 8], [-1, 8]], channel_multiplier=0))
                made.wait()
                split_x(pool)

            @block.tensor
            def _(pe):
                pe.wait_ge(router_in, 16)
                if kind == "relu2":
                    pe.transpose(turn[:, 0, 0:64], rowsT[:], m.ident[0:64, 0:64]).then_inc(router_turned, 1)
                    pe.wait_ge(router_kept, 1)
                for i in range(TILES):
                    pe.matmul(logits[:, i, :], m.xt[:, i * PART:(i + 1) * PART], router[:], start=True,
                              stop=True).then_inc(logits_ready, 1)
                pe.wait_ge(shares_ready, 1)
                for i in range(TILES):
                    pe.transpose(turn[0:E, i // 4, i % 4 * PART:(i % 4 + 1) * PART], work[:, i, :], m.ident[:]).then_inc(turned, 1)

            @block.scalar
            def _(act):
                if kind != "gelu":
                    act.wait_ge(logits_ready, TILES)
                    nc.scalar.activation(score[:], logits[:], ACT.Sigmoid).then_inc(score_ready, 1)
                else:
                    act.wait_ge(score_ready, 1)
                    nc.scalar.activation(score[:], work[:], ACT.Exp).then_inc(score_ready, 1)
                for t in range(BLOCKS):
                    act.wait_ge(turned, 4 * (t + 1))
                    nc.scalar.activation(shareT[:, t * BLOCK:(t + 1) * BLOCK], turn[0:E, t, :], ACT.Copy).then_inc(kept, 1)

            @block.vector
            def _(dve):
                c = Chain(dve, steps)
                step = lambda ins: (c.did(ins), c.wait())

                def by_pairs(values, rank):
                    mine = values.unsqueeze(3).to_broadcast([PART, TILES, 8, 8])
                    other = values.unsqueeze(2).to_broadcast([PART, TILES, 8, 8])
                    v1 = pair[:].rearrange("p t (i j) -> p t i j", i=8)
                    v2 = pair2[:].rearrange("p t (i j) -> p t i j", i=8)
                    step(dve.tensor_tensor(v1, other, mine, ALU.is_equal))
                    step(dve.tensor_tensor(v1, v1, earlier[:].unsqueeze(1).to_broadcast([PART, TILES, 8, 8]), ALU.mult))
                    step(dve.tensor_tensor(v2, other, mine, ALU.is_gt))
                    step(dve.tensor_tensor(v1, v1, v2, ALU.add))
                    step(dve.tensor_reduce(rank, v1, AX.X, ALU.add))

                def top8():
                    for i in range(TILES):
                        c.did(dve.max(top[:, i, :], work[:, i, :]))
                    c.wait()
                    for i in range(TILES):
                        c.did(dve.match_replace(work2[:, i, :], top[:, i, :], work[:, i, :], -BIG))
                    c.wait()
                    step(dve.tensor_tensor(pick[:], work2[:], work[:], ALU.is_lt))

                if kind == "relu2":
                    dve.wait_ge(router_turned, 1)
                    dve.tensor_copy(router[:], turn[:, 0, 0:64]).then_inc(router_kept, 1)
                    dve.wait_ge(offset_in, 16)
                    dve.wait_ge(score_ready, 1)
                    step(dve.tensor_tensor(work[:], score[:], offset[:].unsqueeze(1).to_broadcast([PART, TILES, E]), ALU.add))
                    grouped = lambda v: v[:].rearrange("p t (g e) -> p t g e", g=8)
                    wide = lambda v: v[:].unsqueeze(3).to_broadcast([PART, TILES, 8, 8])
                    step(dve.tensor_reduce(one[:], grouped(work), AX.X, ALU.max))
                    step(dve.tensor_tensor(grouped(pick), grouped(work), wide(one), ALU.is_equal))
                    step(dve.tensor_reduce(two[:], grouped(pick), AX.X, ALU.add))
                    step(dve.scalar_tensor_tensor(work2[:], pick[:], -BIG, work[:], ALU.mult, ALU.add))
                    step(dve.tensor_reduce(three[:], grouped(work2), AX.X, ALU.max))
                    step(dve.tensor_scalar(two[:], two[:], 1.5, -BIG, ALU.is_lt, ALU.mult))
                    step(dve.tensor_tensor(two[:], two[:], one[:], ALU.add))
                    step(dve.tensor_tensor(three[:], three[:], two[:], ALU.max))
                    step(dve.tensor_tensor(one[:], one[:], three[:], ALU.add))
                    dve.wait_ge(built, 2)
                    by_pairs(one[:], two[:])
                    step(dve.tensor_scalar(two[:], two[:], 3.5, None, ALU.is_lt))
                    step(dve.tensor_tensor(grouped(work), grouped(work), wide(two), ALU.mult))
                    top8()
                    step(dve.tensor_tensor(work[:], score[:], pick[:], ALU.mult))
                    step(dve.tensor_reduce(total[:], work[:], AX.X, ALU.add))
                    step(dve.tensor_scalar(total[:], total[:], 1e-20, None, ALU.add))
                    step(dve.reciprocal(total[:], total[:]))
                    step(dve.tensor_scalar(total[:], total[:], 2.5, None, ALU.mult))
                elif kind == "swiglu":
                    dve.wait_ge(score_ready, 1)
                    step(dve.tensor_copy(work[:], score[:]))
                    top8()
                    step(dve.tensor_tensor(work[:], score[:], pick[:], ALU.mult))
                    step(dve.tensor_reduce(total[:], work[:], AX.X, ALU.add))
                    step(dve.tensor_scalar(total[:], total[:], 1e-9, None, ALU.add))
                    step(dve.reciprocal(total[:], total[:]))
                else:
                    dve.wait_ge(offset_in, 16)
                    dve.wait_ge(logits_ready, TILES)
                    row = lambda: total[:].unsqueeze(2).to_broadcast([PART, TILES, E])
                    step(dve.tensor_tensor(work[:], logits[:], offset[:].unsqueeze(1).to_broadcast([PART, TILES, E]), ALU.add))
                    step(dve.tensor_reduce(total[:], work[:], AX.X, ALU.max))
                    dve.tensor_tensor(work[:], work[:], row(), ALU.subtract).then_inc(score_ready, 1)
                    dve.wait_ge(score_ready, 2)
                    dve.wait_ge(built, 2)
                    step(dve.tensor_reduce(total[:], score[:], AX.X, ALU.add))
                    step(dve.reciprocal(total[:], total[:]))
                    step(dve.tensor_tensor(score[:], score[:], row(), ALU.mult))
                    by_pairs(score[:], work2[:])
                    step(dve.tensor_scalar(pick[:], work2[:], 1.5, None, ALU.is_lt))
                    step(dve.tensor_tensor(work[:], score[:], pick[:], ALU.mult))
                    step(dve.tensor_reduce(total[:], work[:], AX.X, ALU.add))
                    step(dve.reciprocal(total[:], total[:]))
                dve.tensor_tensor(work[:], work[:], total[:].unsqueeze(2).to_broadcast([PART, TILES, E]), ALU.mult).then_inc(shares_ready, 1)



class Attention:

    def __init__(self, layer, prefix, heads, head_dim, heads_in_unit, scale):
        self.layer, self.prefix, self.heads, self.head_dim = layer, prefix, heads, head_dim
        self.G, self.scale = heads_in_unit, scale
        self.units = heads // heads_in_unit if heads_in_unit == 1 else heads // 4
        self.by_batch = heads_in_unit > 1


UNIT = ALLKEYS
UCHUNKS = 5
ULAST = UNIT - 4 * PART


def attention(nc, m, a, at):
    p, H, DH, G, U = at.prefix, at.heads, at.head_dim, at.G, at.units
    with ExitStack() as ctx:
        keysT = [ctx.enter_context(nc.sbuf_tensor(f"{p}_keys_T_{part}", [DIM, U * UNIT * (1 if G == 1 else BATCH)], FP32R)) for part in ("high", "low")]
        n_vw = U if G == 1 else U * BATCH
        values = ctx.enter_context(nc.sbuf_tensor(f"{p}_values", [PART, n_vw * UCHUNKS, DIM], FP32))
        attention_tables(nc, m, a, at, keysT, values)
        attention_tokens(nc, m, at, keysT, values)


def attention_tables(nc, m, a, at, keysT, values):
    p, H, DH, G = at.prefix, at.heads, at.head_dim, at.G
    GROUPS = H // 4
    with ExitStack() as ctx:
        sb = lambda n, s: ctx.enter_context(nc.sbuf_tensor(f"{p}_pre_{n}", s, FP32))
        sem = lambda n: m.semaphore(nc, f"{p}_pre_{n}")
        HP = PART // DH
        wq, wk = sb("WqT", [PART, H // HP, DIM]), sb("WkT", [PART, H // HP, CDIM])
        wv, wo = sb("WvT", [PART, H // HP, CDIM]), sb("Wo", [PART, H // HP, DIM])
        head = lambda w, h: w[h % HP * DH:(h % HP + 1) * DH, h // HP, :]
        bias = sb("out_bias", [PART, DIM])
        qk, vo = sb("qk", [CDIM, 8, DIM]), sb("vo", [CDIM, H, DIM])
        plain = sb("plain", [PART, 2, 2, BATCH, 4, DIM]) if G > 1 else None
        ps_w = ctx.enter_context(nc.psum_tensor(f"{p}_pre_ps_w", [PART, 2, BLOCK], FP32))
        ps_k = ctx.enter_context(nc.psum_tensor(f"{p}_pre_ps_k", [PART, 2, 2, BLOCK], FP32))
        ps_v = ctx.enter_context(nc.psum_tensor(f"{p}_pre_ps_v", [PART, 2, BLOCK], FP32))
        w_in, bias_in, w_ready, qk_kept, vo_kept = (sem(n) for n in ("w_in", "bias_in", "w_ready", "qk_kept", "vo_kept"))
        k_ready, k_kept, v_ready, v_kept = (sem(n) for n in ("k_ready", "k_kept", "v_ready", "v_kept"))
        stacked = [sem(f"stacked{n}") for n in range(2)]
        bias_scaled, bias_added, k_high = sem("bias_scaled"), sem("bias_added"), sem("k_high")
        if HP == 1:
            qk_out = lambda h: ps_w[0:CDIM, 0, h % 4 * DIM:(h % 4 + 1) * DIM]
            vo_out = lambda h: ps_w[0:CDIM, 1, h % 4 * DIM:(h % 4 + 1) * DIM]
            four = lambda n: ps_w[0:CDIM, n, :].rearrange("c (h d) -> c h d", h=4)
        else:
            qk_out = lambda h: ps_w[0:CDIM, h % 2, h % 4 // 2 * DIM:(h % 4 // 2 + 1) * DIM]
            vo_out = lambda h: ps_w[0:CDIM, h % 2, (2 + h % 4 // 2) * DIM:(3 + h % 4 // 2) * DIM]
            four = lambda n: ps_w[0:CDIM, :, 2 * n * DIM:2 * (n + 1) * DIM].rearrange("c s (h d) -> c h s d", h=2)
        if G == 1:
            pieces = [(c * PART, min(PART, ALLKEYS - c * PART)) for c in range(UCHUNKS)]
        else:
            pieces = [(b * KEYS + c * PART, min(PART, KEYS - c * PART)) for b in range(BATCH) for c in range(2)]
        CUTS = sum(len({0, PART} | {r - hh * KEYS for r in range(0, UNIT, PART) if hh * KEYS < r < (hh + 1) * KEYS}) for hh in range(4))
        products = [(g, n) for g in range(GROUPS) for n in range(len(pieces))]

        def of_head(src, h):
            if G == 1:
                return (src,) + tuple(v[:, h * UNIT:(h + 1) * UNIT].rearrange("p (s k) -> p s k", s=2) for v in keysT)
            return (src.rearrange("p s (v k) -> p s v k", v=2),) + tuple(
                v[:].rearrange("p (q s v h k) -> p q s v h k", s=2, v=2, h=4, k=KEYS)[:, h // 4, :, :, h % 4, :] for v in keysT)

        with nc.Block() as block:
            @block.sync
            def _(sp):
                for w, name in ((wk, "WkT"), (wq, "WqT"), (wv, "WvT"), (wo, "Wo")):
                    sp.dma_start(w[:].rearrange("d h c -> d (h c)"), a[f"{p}_{name}"]).then_inc(w_in, 16)
                sp.dma_start(bias[:], a[p + "_bo"].rearrange("(o d) -> o d", o=1).to_broadcast([PART, DIM])).then_inc(bias_in, 16)
                sp.wait_ge(w_in, 64)
                if G > 1:
                    dst = values[:].rearrange("r (q b c) d -> r q b c d", b=BATCH, c=UCHUNKS)
                    for q in range(GROUPS):
                        sp.wait_ge(v_kept, len(pieces) * (q + 1))
                        for hh in range(4):
                            for c2 in range(2):
                                k0, k1 = c2 * PART, min((c2 + 1) * PART, KEYS)
                                while k0 < k1:
                                    r = hh * KEYS + k0
                                    n = min(k1 - k0, PART - r % PART)
                                    sp.dma_start(dst[r % PART:r % PART + n, q, :, r // PART, :],
                                                 plain[k0 - c2 * PART:k0 - c2 * PART + n, q % 2, c2, :, hh, :]).then_inc(stacked[q % 2], 16)
                                    k0 += n
                    for n in range(2):
                        sp.wait_ge(stacked[n], 16 * CUTS * GROUPS // 2)

            @block.tensor
            def _(pe):
                pe.wait_ge(w_in, 64)
                n_k = 0
                for g in range(GROUPS):
                    if g:
                        pe.wait_ge(qk_kept, g)
                        pe.wait_ge(vo_kept, g)
                    for w1, w2, out in ((wk, wq, qk_out), (wv, wo, vo_out)):
                        for h in range(4 * g, 4 * g + 4):
                            mm = pe.matmul(out(h), head(w1, h), head(w2, h), start=True, stop=True)
                    mm.then_inc(w_ready, 1)
                    pe.wait_ge(qk_kept, g + 1)
                    for h in range(4 * g, 4 * g + 4):
                        if n_k >= 2:
                            pe.wait_ge(k_kept, n_k - 1)
                        for s in range(2):
                            mm = pe.matmul(ps_k[:, n_k % 2, s, 0:HALFKEYS], qk[:, h % 8, :], m.ctxT[:, s * HALFKEYS:(s + 1) * HALFKEYS],
                                           start=True, stop=True)
                        mm.then_inc(k_ready, 1)
                        n_k += 1
                for n, (g, q) in enumerate(products):
                    first, count = pieces[q]
                    pe.wait_ge(vo_kept, g + 1)
                    if n >= 2:
                        pe.wait_ge(v_kept, n - 1)
                    pe.matmul(ps_v[0:count, n % 2, :], m.ctxT[:, first:first + count],
                              vo[:, 4 * g:4 * g + 4, :].rearrange("c h d -> c (h d)"), start=True, stop=True).then_inc(v_ready, 1)

            @block.scalar
            def _(act):
                def heads4(w, g):
                    v = w[:, 4 * g:4 * g + 4, :]
                    return v if HP == 1 else v.rearrange("c (h s) d -> c h s d", s=2)

                for g in range(GROUPS):
                    act.wait_ge(w_ready, g + 1)
                    nc.scalar.activation(heads4(qk, g % 2), four(0), ACT.Copy,
                                         scale=at.scale).then_inc(qk_kept, 1)
                    nc.scalar.activation(heads4(vo, g), four(1), ACT.Copy,
                                         scale=m.gate[0:CDIM, at.layer:at.layer + 1]).then_inc(vo_kept, 1)
                for n, (g, q) in enumerate(products):
                    first, count = pieces[q]
                    act.wait_ge(v_ready, n + 1)
                    if G == 1:
                        dst = values[0:count, :, :].rearrange("k (h c) d -> k h c d", c=UCHUNKS)[:, 4 * g:4 * g + 4, q, :]
                    else:
                        dst = plain[0:count, g % 2, q % 2, q // 2, :, :]
                        if g >= 2 and q == 0:
                            act.wait_ge(stacked[g % 2], 16 * CUTS * (g // 2))
                    nc.scalar.activation(dst, ps_v[0:count, n % 2, :].rearrange("k (h d) -> k h d", h=4), ACT.Copy).then_inc(v_kept, 1)

            @block.vector
            def _(dve):
                dve.wait_ge(bias_in, 16)
                dve.tensor_scalar(bias[:], bias[:], m.gate[:, at.layer:at.layer + 1], None, ALU.mult).then_inc(bias_scaled, 1)
                dve.wait_ge(bias_scaled, 1)
                for t in range(BLOCKS):
                    rows = m.x[:, t * PER_BLOCK:(t + 1) * PER_BLOCK, :]
                    dve.tensor_tensor(rows, rows, bias[:].unsqueeze(1).to_broadcast([PART, PER_BLOCK, DIM]), ALU.add).then_inc(bias_added, 1)
                for h in range(H):
                    dve.wait_ge(k_ready, h + 1)
                    src, high, low = of_head(ps_k[:, h % 2, :, 0:HALFKEYS], h)
                    dve.tensor_copy(high, src).then_inc(k_high, 1)
                    dve.wait_ge(k_high, h + 1)
                    dve.tensor_tensor(low, src, high, ALU.subtract).then_inc(k_kept, 1)


def attention_tokens(nc, m, at, keysT, values):
    p, G, U = at.prefix, at.G, at.units
    TURNS, UNITS = TILES // 2, 2 * U
    WIDTH = UNIT // G
    with ExitStack() as ctx:
        sb = lambda n, s: ctx.enter_context(nc.sbuf_tensor(f"{p}_{n}", s, FP32))
        sem = lambda n: m.semaphore(nc, f"{p}_{n}")
        tile_x = sb("tile_x", [DIM, 2, PART])
        x_high, x_low = (ctx.enter_context(nc.sbuf_tensor(f"{p}_{n}", [DIM, 2, PART], FP32R)) for n in ("x_high", "x_low"))
        fetched, high_ready = sem("fetched"), sem("high_ready")
        less = sb("less", [PART, 2, G])
        total = sb("total", [PART, 2, G])
        share = sb("share", [PART, 4, G])
        prob = sb("prob", [PART, 2, UNIT])
        scaled = sb("scaled", [PART, 2, UNIT]) if G > 1 else None
        probT = sb("probT", [PART, 2, UCHUNKS, PART])
        ps_s = ctx.enter_context(nc.psum_tensor(f"{p}_ps_s", [PART, 2, 2, BLOCK], FP32))
        ps_a = ctx.enter_context(nc.psum_tensor(f"{p}_ps_a", [PART, 2, BLOCK], FP32))
        ps_b = ctx.enter_context(nc.psum_tensor(f"{p}_ps_b", [PART, BLOCK], FP32))
        ps_o = ctx.enter_context(nc.psum_tensor(f"{p}_ps_o", [PART, BLOCK], FP32))
        tile_ready, s_ready, less_ready, prob_ready = sem("tile_ready"), sem("s_ready"), sem("less_ready"), sem("prob_ready")
        share_ready, scaled_ready, t_ready, t_kept = sem("share_ready"), sem("scaled_ready"), sem("t_ready"), sem("t_kept")
        pv_done, x_added = sem("pv_done"), sem("x_added")
        grouped = lambda v: v.rearrange("p (g k) -> p g k", g=G)

        with nc.Block() as block:
            @block.tensor
            def _(pe):
                start(pe, t_ready, pv_done)

                def scores(turn, k):
                    if k >= UNITS:
                        turn, k = turn + 1, k - UNITS
                    half, u = divmod(k, U)
                    base = u * UNIT if G == 1 else (u * BATCH + turn // 2) * UNIT
                    if u == 0:
                        pe.wait_ge(tile_ready, turn * 2 + half + 1)
                    for s in range(2):
                        keys = [v[:, bass.ds(base + s * HALFKEYS, HALFKEYS)] for v in keysT]
                        mm = product3(pe, ps_s[:, k % 2, s, 0:HALFKEYS], (x_high[:, half, :], x_low[:, half, :]), keys)
                    mm.then_inc(s_ready, 1)

                def turned(turn, k, first=False):
                    if k >= UNITS:
                        turn, k = turn + 1, k - UNITS
                    n = turn * UNITS + k
                    if G == 1:
                        pe.wait_ge(prob_ready, n + 1)
                    else:
                        pe.wait_ge(scaled_ready, n + 1 + START)
                    if not first:
                        pe.wait_ge(t_kept, 2 * n)
                    for c in range(UCHUNKS):
                        rows = PART if c < 4 else ULAST
                        out = ps_a[:, k % 2, c * PART:(c + 1) * PART] if c < 4 else ps_b[0:ULAST, 0:PART]
                        mm = pe.transpose(out, (prob if G == 1 else scaled)[:, k % 2, c * PART:c * PART + rows], m.ident[:])
                    mm.then_inc(t_ready, 1)

                def weighted(turn, k):
                    half, u = divmod(k, U)
                    pe.wait_ge(t_kept, turn * (2 * UNITS) + (2 * k + 2))
                    if G == 1:
                        pe.wait_ge(x_added, turn * UNITS + k + START)
                    elif u == 0:
                        pe.wait_ge(x_added, turn * 2 + half + START)
                    base = u * UCHUNKS if G == 1 else (u * BATCH + turn // 2) * UCHUNKS
                    for c in range(UCHUNKS):
                        rows = PART if c < 4 else ULAST
                        v = values[0:rows, bass.ds(base + c, 1), :].rearrange("k o d -> k (o d)")
                        mm = pe.matmul(ps_o[:, 0:DIM], probT[0:rows, k % 2, c, :], v,
                                       start=(G == 1 or u == 0) and c == 0, stop=(G == 1 or u == U - 1) and c == UCHUNKS - 1)
                    mm.then_inc(pv_done, 1)

                scores(0, 0)
                scores(0, 1)
                pe.wait_ge(prob_ready, 1)
                scores(0, 2)
                turned(0, 0, first=True)
                with pe.Fori(0, TURNS) as it:
                    for k in range(UNITS):
                        pe.wait_ge(prob_ready, it * UNITS + k + 2)
                        scores(it, k + 3)
                        turned(it, k + 1)
                        weighted(it, k)

            @block.scalar
            def _(act):
                def exponentials(turn, k, first=False):
                    if k >= UNITS:
                        turn, k = turn + 1, k - UNITS
                    n = turn * UNITS + k
                    act.wait_ge(less_ready, n + 1)
                    if G == 1 and not first:
                        act.wait_ge(t_ready, n - 1 + START)
                        act.wait_ge(share_ready, n - 1 + START)
                    elif not first:
                        act.wait_ge(scaled_ready, n - 1 + START)
                    for g in range(G):
                        out = prob[:, k % 2, g * WIDTH:(g + 1) * WIDTH]
                        if G == 1:
                            out, scores = out.rearrange("p (s k) -> p s k", s=2), ps_s[:, k % 2, :, 0:HALFKEYS]
                        else:
                            scores = ps_s[:, k % 2, g // 2, g % 2 * KEYS:(g % 2 + 1) * KEYS]
                        ins = nc.scalar.activation(out, scores, ACT.Exp,
                                                   bias=less[:, k % 2, g:g + 1], accum_out=total[:, k % 2, g:g + 1])
                    ins.then_inc(prob_ready, 1)

                exponentials(0, 0, first=True)
                exponentials(0, 1)
                with act.Fori(0, TURNS) as it:
                    for k in range(UNITS):
                        exponentials(it, k + 2)

            @block.vector
            def _(dve):
                start(dve, x_added, share_ready)

                def fetch(tile, half):
                    dve.tensor_scalar(tile_x[:, half, :], m.xt[:, bass.ds(tile * PART, PART)], 1.0, None, ALU.mult).then_inc(fetched, 1)
                    dve.wait_ge(fetched, tile + 1)
                    dve.tensor_copy(x_high[:, half, :], tile_x[:, half, :]).then_inc(high_ready, 1)
                    dve.wait_ge(high_ready, tile + 1)
                    dve.tensor_tensor(x_low[:, half, :], tile_x[:, half, :], x_high[:, half, :], ALU.subtract).then_inc(tile_ready, 1)

                def maxima(turn, k):
                    if k >= UNITS:
                        turn, k = turn + 1, k - UNITS
                    dve.wait_ge(s_ready, turn * UNITS + k + 1)
                    if G == 1:
                        out, scores, axes = less[:, k % 2, :], ps_s[:, k % 2, :, 0:HALFKEYS], AX.XY
                    else:
                        out, axes = less[:, k % 2, :].rearrange("p (s v) -> p s v", s=2), AX.X
                        scores = ps_s[:, k % 2, :, 0:HALFKEYS].rearrange("p s (v k) -> p s v k", v=2)
                    dve.tensor_reduce(out, scores, axes, ALU.max, negate=True).then_inc(less_ready, 1)

                def over_sum(turn, k, first=False):
                    if k >= UNITS:
                        turn, k = turn + 1, k - UNITS
                    n = turn * UNITS + k
                    dve.wait_ge(prob_ready, n + 1)
                    if G == 1 and not first:
                        dve.wait_ge(x_added, n - 3 + START)
                    elif not first:
                        dve.wait_ge(scaled_ready, n - 3 + START)
                    dve.reciprocal(share[:, k % 4, :], total[:, k % 2, :]).then_inc(share_ready, 1)

                def keep(turn, k, first=False):
                    if k >= UNITS:
                        turn, k = turn + 1, k - UNITS
                    n = turn * UNITS + k
                    dve.wait_ge(t_ready, n + 1 + START)
                    if not first:
                        dve.wait_ge(pv_done, n - 1 + START)
                    dve.tensor_copy(probT[:, k % 2, 0:4, :], ps_a[:, k % 2, :].rearrange("p (c t) -> p c t", c=4)).then_inc(t_kept, 1)
                    dve.tensor_copy(probT[0:ULAST, k % 2, 4, :], ps_b[0:ULAST, 0:PART]).then_inc(t_kept, 1)

                fetch(0, 0)
                fetch(1, 1)
                maxima(0, 0)
                over_sum(0, 0, first=True)
                maxima(0, 1)
                maxima(0, 2)
                over_sum(0, 1)
                keep(0, 0, first=True)
                with dve.Fori(0, TURNS) as it:
                    for k in range(UNITS):
                        half, u = divmod(k, U)
                        maxima(it, k + 3)
                        over_sum(it, k + 2)
                        if u == U - 4:
                            fetch(it * 2 + 2 + half, half)
                        keep(it, k + 1)
                        if G == 1 or u == U - 1:
                            dve.wait_ge(pv_done, it * UNITS + k + 1 + START)
                            rows = m.x[:, bass.ds(it * 2 + half, 1), :].rearrange("p o d -> p (o d)")
                            if G == 1:
                                dve.wait_ge(x_added, it * UNITS + k + START)
                                dve.wait_ge(share_ready, it * UNITS + k + 1 + START)
                                dve.scalar_tensor_tensor(rows, ps_o[:, 0:DIM], share[:, k % 4, :], rows, ALU.mult, ALU.add).then_inc(x_added, 1)
                            else:
                                dve.tensor_tensor(rows, ps_o[:, 0:DIM], rows, ALU.add).then_inc(x_added, 1)

            @block.gpsimd
            def _(pool):
                def scale(turn, k, first=False):
                    if k >= UNITS:
                        turn, k = turn + 1, k - UNITS
                    n = turn * UNITS + k
                    if not first:
                        pool.wait_ge(t_ready, n - 1 + START)
                    pool.wait_ge(share_ready, n + 1 + START)
                    pool.tensor_tensor(grouped(scaled[:, k % 2, :]), grouped(prob[:, k % 2, :]),
                                       share[:, k % 4, :].unsqueeze(2).to_broadcast([PART, G, WIDTH]),
                                       ALU.mult).then_inc(scaled_ready, 1)

                if G > 1:
                    start(pool, scaled_ready)
                    scale(0, 0, first=True)
                    with pool.Fori(0, TURNS) as it:
                        for k in range(UNITS):
                            scale(it, k + 1)


L2_ATT = Attention(2, "L2_xattn", 16, 64, 4, 64 ** -0.5)
L3_ATT = Attention(3, "L3_xattn", 8, 128, 1, 1.5 * 128 ** -0.5)


LAT_CHUNKS = SEQ // PART
CTX_CHUNK = KEYS // 2
L1_KEYS = SEQ + KEYS
L1_HEADS, L1_DH = 2, 64


def latent_attention(nc, m, a):
    with ExitStack() as ctx:
        sb = lambda n, s: ctx.enter_context(nc.sbuf_tensor(f"lat_{n}", s, FP32))
        kT = sb("kT", [DIM, BATCH + 1, L1_KEYS])
        v = sb("v", [PART, BATCH * 6, DIM])
        qT = sb("qT", [DIM, (TILES + 2) * 2 * PART])
        masked = sb("masked", [PART, ALLKEYS + KEYS])
        latent_context(nc, m, a, kT, v, masked)
        latent_projections(nc, m, a, kT, v, qT, masked)
        latent_tokens(nc, m, kT, v, qT, masked)
    latent_output(nc, m, a)


def latent_context(nc, m, a, kT, v, masked):
    R, N = CTX_CHUNK, 2 * BATCH
    with ExitStack() as ctx:
        sb = lambda n, s, dt=FP32: ctx.enter_context(nc.sbuf_tensor(f"latc_{n}", s, dt))
        sem = lambda n: m.semaphore(nc, f"latc_{n}")
        rows, w = sb("rows", [R, N, CDIM]), sb("w", [CDIM, 2 * DIM])
        mask8, maskf = sb("mask8", [PART, ALLKEYS], U8), sb("maskf", [PART, ALLKEYS])
        stats, moments = sb("stats", [R, N, 6]), sb("moments", [R, N, 2])
        var, sd, rstd = sb("var", [R, N]), sb("sd", [R, N]), sb("rstd", [R, N])
        normT = sb("normT", [CDIM, N, R])
        k, sq = sb("k", [R, N, DIM]), sb("sq", [R, N, DIM])
        ss, rms, inv = sb("ss", [R, 2 * N]), sb("rms", [R, 2 * N]), sb("inv", [R, 2 * N])
        ps_t = ctx.enter_context(nc.psum_tensor("latc_ps_t", [PART, 2, BLOCK], FP32))
        ps_k = ctx.enter_context(nc.psum_tensor("latc_ps_k", [PART, 4, BLOCK], FP32))
        rows_in, w_in, mask_in = sem("rows_in"), sem("w_in"), sem("mask_in")
        steps, var_done, sd_done, normed, turned, turned_kept = (sem(n) for n in ("steps", "var_done", "sd_done", "normed", "turned", "turned_kept"))
        kv_ready, k_kept, v_kept, squares, ss_done, rms_done, k_normed = (sem(n) for n in ("kv_ready", "k_kept", "v_kept", "squares", "ss_done", "rms_done", "k_normed"))
        k_turned, kT_kept = sem("k_turned"), sem("kT_kept")
        with nc.Block() as block:
            @block.sync
            def _(sp):
                sp.dma_start(rows[:], a["ctx_768"].rearrange("b (u k) c -> k (b u) c", k=R)).then_inc(rows_in, 16)
                sp.dma_start(w[:], a["L1_xattn_WkvT"]).then_inc(w_in, 16)
                sp.dma_start(mask8[:], a["mask_BxS2_bk0"].rearrange("(o b) k -> o (b k)", o=1).to_broadcast([PART, ALLKEYS])).then_inc(mask_in, 16)
                sp.wait_ge(w_in, 16)

            @block.vector
            def _(dve):
                c = Chain(dve, steps)
                step = lambda ins: (c.did(ins), c.wait())
                dve.wait_ge(rows_in, 16)
                for i in range(N):
                    c.did(dve.bn_stats(stats[:, i, :], rows[:, i, :]))
                c.wait()
                for i in range(N):
                    c.did(dve.bn_aggr(moments[:, i, :], stats[:, i, :]))
                c.wait()
                dve.tensor_scalar(var[:], moments[:, :, 1], 1e-5, None, ALU.add).then_inc(var_done, 1)
                dve.wait_ge(sd_done, 1)
                step(dve.reciprocal(rstd[:], sd[:]))
                for i in range(N):
                    dve.tensor_scalar(rows[:, i, :], rows[:, i, :], moments[:, i, 0:1], rstd[:, i:i + 1],
                                      ALU.subtract, ALU.mult).then_inc(normed, 1)
                dve.wait_ge(mask_in, 16)
                step(dve.tensor_copy(maskf[:], mask8[:]))
                step(dve.tensor_scalar(masked[:, 0:ALLKEYS], maskf[:], 1.0, BIG, ALU.subtract, ALU.mult))
                dve.wait_ge(squares, 4)
                dve.tensor_reduce(ss[:], sq[:].rearrange("p t (h d) -> p (t h) d", d=L1_DH), AX.X, ALU.add).then_inc(ss_done, 1)
                dve.wait_ge(rms_done, 1)
                step(dve.tensor_scalar(rms[:], rms[:], 1e-8, None, ALU.max))
                step(dve.reciprocal(inv[:], rms[:]))
                dve.wait_ge(k_kept, 4)
                heads = k[:].rearrange("p t (h d) -> p (t h) d", d=L1_DH)
                step(dve.tensor_tensor(heads, heads, inv[:].unsqueeze(2).to_broadcast([R, 2 * N, L1_DH]), ALU.mult))
                dve.tensor_tensor(heads, heads, m.row("kn_g")[0:R].unsqueeze(1).to_broadcast([R, 2 * N, L1_DH]),
                                  ALU.mult).then_inc(k_normed, 1)
                for s in range(2):
                    dve.wait_ge(k_turned, s + 1)
                    dve.tensor_copy(kT[:, 2 * s:2 * s + 2, SEQ:], ps_t[:, s, 0:4 * R].rearrange("p (b k) -> p b k", b=2)).then_inc(kT_kept, 1)

            @block.scalar
            def _(act):
                act.wait_ge(var_done, 1)
                nc.scalar.activation(sd[:], var[:], ACT.Sqrt).then_inc(sd_done, 1)
                for s in range(2):
                    act.wait_ge(turned, s + 1)
                    nc.scalar.activation(normT[:, 4 * s:4 * s + 4, :].rearrange("c t k -> c (t k)"), ps_t[0:CDIM, s, 0:4 * R], ACT.Identity,
                                         scale=m.col("ln_x_g")[0:CDIM], bias=m.col("ln_x_b")[0:CDIM]).then_inc(turned_kept, 1)
                for s in range(4):
                    act.wait_ge(kv_ready, s + 1)
                    bank = ps_k[0:R, s, :].rearrange("p (t n) -> p t n", t=2)
                    nc.scalar.activation(k[:, 2 * s:2 * s + 2, :], bank[:, :, 0:DIM], ACT.Copy).then_inc(k_kept, 1)
                    nc.scalar.activation(sq[:, 2 * s:2 * s + 2, :], bank[:, :, 0:DIM], ACT.Square).then_inc(squares, 1)
                    nc.scalar.activation(v[0:R, s * 6 + 4:s * 6 + 6, :], bank[:, :, DIM:], ACT.Copy).then_inc(v_kept, 1)
                act.wait_ge(ss_done, 1)
                nc.scalar.activation(rms[:], ss[:], ACT.Sqrt, scale=1.0 / L1_DH).then_inc(rms_done, 1)

            @block.tensor
            def _(pe):
                for i in range(N):
                    pe.wait_ge(normed, i + 1)
                    mm = pe.transpose(ps_t[0:CDIM, i // 4, i % 4 * R:(i % 4 + 1) * R], rows[:, i, :], m.ident[0:R, 0:R])
                    if i % 4 == 3:
                        mm.then_inc(turned, 1)
                pe.wait_ge(w_in, 16)
                for i in range(N):
                    pe.wait_ge(turned_kept, i // 4 + 1)
                    mm = pe.matmul(ps_k[0:R, i // 2, i % 2 * 2 * DIM:(i % 2 + 1) * 2 * DIM], normT[:, i, :], w[:], start=True, stop=True)
                    if i % 2:
                        mm.then_inc(kv_ready, 1)
                pe.wait_ge(k_normed, 1)
                for i in range(N):
                    mm = pe.transpose(ps_t[:, i // 4, i % 4 * R:(i % 4 + 1) * R], k[:, i, :], m.ident[0:R, 0:R])
                    if i % 4 == 3:
                        mm.then_inc(k_turned, 1)


def latent_projections(nc, m, a, kT, v, qT, masked):
    with ExitStack() as ctx:
        sb = lambda n, s, dt=FP32: ctx.enter_context(nc.sbuf_tensor(f"latq_{n}", s, dt))
        sem = lambda n: m.semaphore(nc, f"latq_{n}")
        w = sb("w", [DIM, 3 * DIM])
        gain = sb("gain", [PART, 4, L1_DH])
        qk, sq = sb("qk", [PART, 2, 4, 2 * DIM]), sb("sq", [PART, 2, 4, 2 * DIM])
        ss, rms, inv = sb("ss", [PART, 2, 16]), sb("rms", [PART, 2, 16]), sb("inv", [PART, 2, 16])
        ps_p = ctx.enter_context(nc.psum_tensor("latq_ps_p", [PART, 4, BLOCK], FP32))
        ps_t = ctx.enter_context(nc.psum_tensor("latq_ps_t", [PART, 2, BLOCK], FP32))
        names = ("w_in", "zeroed", "gained", "p_ready", "qk_kept", "squares", "v_kept", "ss_done", "rms_done", "steps", "normed", "turned", "q_kept", "k_kept")
        w_in, zeroed, gained, p_ready, qk_kept, squares, v_kept, ss_done, rms_done, steps, normed, turned, q_kept, k_kept = (sem(n) for n in names)
        tiles = qT[:].rearrange("p (i h t) -> p i h t", h=2, t=PART)
        with nc.Block() as block:
            @block.sync
            def _(sp):
                sp.dma_start(w[:], a["L1_xattn_WqkvT"]).then_inc(w_in, 16)
                sp.wait_ge(w_in, 16)

            @block.gpsimd
            def _(pool):
                for n, part in enumerate((kT[:, BATCH, :], masked[:, ALLKEYS:], tiles[64:128, :, 0, :], tiles[0:64, :, 1, :],
                                          tiles[0:64, TILES:, 0, :], tiles[64:128, TILES:, 1, :])):
                    if n:
                        pool.wait_ge(zeroed, n)
                    pool.memset(part, 0.0).then_inc(zeroed, 1)

            @block.tensor
            def _(pe):
                pe.wait_ge(w_in, 16)
                for t in range(BLOCKS):
                    for ahead in ((0, 1) if t == 0 else (t + 1,)):
                        if ahead == BLOCKS:
                            break
                        if ahead:
                            pe.wait_ge(v_kept, ahead)
                        for j in range(4):
                            i = 4 * ahead + j
                            mm = pe.matmul(ps_p[:, j, 0:3 * DIM], m.xt[:, i * PART:(i + 1) * PART], w[:], start=True, stop=True)
                        mm.then_inc(p_ready, 1)
                    pe.wait_ge(normed, t + 1)
                    if t:
                        pe.wait_ge(q_kept, 2 * t)
                    for j in range(4):
                        mm = pe.transpose(ps_t[:, 0, j * PART:(j + 1) * PART], qk[:, t % 2, j, 0:DIM], m.ident[:])
                    mm.then_inc(turned, 1)
                    if t:
                        pe.wait_ge(k_kept, t)
                    for j in range(4):
                        mm = pe.transpose(ps_t[:, 1, j * PART:(j + 1) * PART], qk[:, t % 2, j, DIM:], m.ident[:])
                    mm.then_inc(turned, 1)

            @block.scalar
            def _(act):
                def keep_keys(t):
                    act.wait_ge(turned, 2 * t + 2)
                    nc.scalar.activation(kT[:, t, 0:SEQ], ps_t[:, 1, :], ACT.Copy).then_inc(k_kept, 1)

                for t in range(BLOCKS):
                    act.wait_ge(p_ready, t + 1)
                    if t >= 2:
                        act.wait_ge(turned, 2 * (t - 1))
                    nc.scalar.activation(qk[:, t % 2, :, :], ps_p[:, :, 0:2 * DIM], ACT.Copy).then_inc(qk_kept, 1)
                    nc.scalar.activation(sq[:, t % 2, :, :], ps_p[:, :, 0:2 * DIM], ACT.Square).then_inc(squares, 1)
                    nc.scalar.activation(v[:, t * 6:t * 6 + 4, :], ps_p[:, :, 2 * DIM:3 * DIM], ACT.Copy).then_inc(v_kept, 1)
                    act.wait_ge(ss_done, t + 1)
                    nc.scalar.activation(rms[:, t % 2, :], ss[:, t % 2, :], ACT.Sqrt, scale=1.0 / L1_DH).then_inc(rms_done, 1)
                    if t:
                        keep_keys(t - 1)
                keep_keys(BLOCKS - 1)

            @block.vector
            def _(dve):
                c = Chain(dve, steps)
                step = lambda ins: (c.did(ins), c.wait())
                step(dve.tensor_scalar(gain[:, 0:2, :], m.row("qn_g").unsqueeze(1).to_broadcast([PART, 2, L1_DH]), L1_DH ** -0.5, None, ALU.mult))
                step(dve.tensor_copy(gain[:, 2:4, :], m.row("kn_g").unsqueeze(1).to_broadcast([PART, 2, L1_DH])))
                dve.wait_ge(zeroed, 6)

                def keep_queries(t):
                    dve.wait_ge(turned, 2 * t + 1)
                    for h in range(2):
                        part = slice(64 * h, 64 * h + 64)
                        dve.tensor_copy(tiles[part, 4 * t:4 * t + 4, h, :],
                                        ps_t[part, 0, :].rearrange("p (j t) -> p j t", j=4)).then_inc(q_kept, 1)

                for t in range(BLOCKS):
                    dve.wait_ge(squares, t + 1)
                    heads = qk[:, t % 2, :, :].rearrange("p j (g d) -> p (j g) d", d=L1_DH)
                    dve.tensor_reduce(ss[:, t % 2, :], sq[:, t % 2, :, :].rearrange("p j (g d) -> p (j g) d", d=L1_DH), AX.X,
                                      ALU.add).then_inc(ss_done, 1)
                    dve.wait_ge(rms_done, t + 1)
                    step(dve.tensor_scalar(inv[:, t % 2, :], rms[:, t % 2, :], 1e-8, None, ALU.max))
                    step(dve.reciprocal(inv[:, t % 2, :], inv[:, t % 2, :]))
                    dve.wait_ge(qk_kept, t + 1)
                    step(dve.tensor_tensor(heads, heads, inv[:, t % 2, :].unsqueeze(2).to_broadcast([PART, 16, L1_DH]), ALU.mult))
                    byhead = qk[:, t % 2, :, :].rearrange("p j (g d) -> p j g d", d=L1_DH)
                    dve.tensor_tensor(byhead, byhead, gain[:].unsqueeze(1).to_broadcast([PART, 4, 4, L1_DH]), ALU.mult).then_inc(normed, 1)
                    if t:
                        keep_queries(t - 1)
                keep_queries(BLOCKS - 1)


def latent_tokens(nc, m, kT, v, qT, masked):
    U, TURNS, UNITS = 2, TILES // 2, 4
    keys = kT[:].rearrange("p b k -> p (b k)")
    with ExitStack() as ctx:
        sb = lambda n, s: ctx.enter_context(nc.sbuf_tensor(f"lata_{n}", s, FP32))
        sem = lambda n: m.semaphore(nc, f"lata_{n}")
        tile_q = sb("tile_q", [DIM, 2, 2, PART])
        less, total, share = sb("less", [PART, 2]), sb("total", [PART, 2]), sb("share", [PART, 2])
        prob = sb("prob", [PART, 2, L1_KEYS])
        probT = sb("probT", [PART, 2, 6, PART])
        ps_s = ctx.enter_context(nc.psum_tensor("lata_ps_s", [PART, 2, 2 * BLOCK], FP32))
        ps_a = ctx.enter_context(nc.psum_tensor("lata_ps_a", [PART, 2, BLOCK], FP32))
        ps_b = ctx.enter_context(nc.psum_tensor("lata_ps_b", [PART, BLOCK], FP32))
        ps_o = ctx.enter_context(nc.psum_tensor("lata_ps_o", [PART, BLOCK], FP32))
        names = ("tile_ready", "s_ready", "mask_added", "less_ready", "prob_ready", "share_ready", "t_ready", "t_kept", "pv_done", "o_kept")
        tile_ready, s_ready, mask_added, less_ready, prob_ready, share_ready, t_ready, t_kept, pv_done, o_kept = (sem(n) for n in names)
        CUT = [(c * PART, PART) for c in range(LAT_CHUNKS)] + [(SEQ, CTX_CHUNK), (SEQ + CTX_CHUNK, CTX_CHUNK)]
        with nc.Block() as block:
            @block.tensor
            def _(pe):
                start(pe, t_ready, pv_done)

                def scores(turn, k):
                    if k >= UNITS:
                        turn, k = turn + 1, k - UNITS
                    half, u = divmod(k, U)
                    if u == 0:
                        pe.wait_ge(tile_ready, turn * 2 + half + 1)
                    base = (turn // 2) * L1_KEYS
                    pe.matmul(ps_s[:, k % 2, 0:BLOCK], tile_q[:, half, u, :], keys[:, bass.ds(base, BLOCK)], start=True, stop=True)
                    pe.matmul(ps_s[:, k % 2, BLOCK:L1_KEYS], tile_q[:, half, u, :], keys[:, bass.ds(base + BLOCK, KEYS)],
                              start=True, stop=True).then_inc(s_ready, 1)

                def turned(turn, k, first=False):
                    if k >= UNITS:
                        turn, k = turn + 1, k - UNITS
                    n = turn * UNITS + k
                    pe.wait_ge(prob_ready, n + 1)
                    if not first:
                        pe.wait_ge(t_kept, 2 * n)
                    for c, (at, rows) in enumerate(CUT):
                        out = ps_a[:, k % 2, c * PART:(c + 1) * PART] if c < 4 else ps_b[0:rows, (c - 4) * PART:(c - 3) * PART]
                        mm = pe.transpose(out, prob[:, k % 2, at:at + rows], m.ident[:])
                    mm.then_inc(t_ready, 1)

                scores(0, 0)
                scores(0, 1)
                turned(0, 0, first=True)
                with pe.Fori(0, TURNS) as it:
                    for k in range(UNITS):
                        half, u = divmod(k, U)
                        pe.wait_ge(prob_ready, it * UNITS + k + 1)
                        scores(it, k + 2)
                        turned(it, k + 1)
                        if u == 0:
                            pe.wait_ge(o_kept, it * 4 + 2 * half + START)
                        for c, (at, rows) in enumerate(CUT):
                            values = v[0:rows, bass.ds((it // 2) * 6 + c, 1), u * 64:(u + 1) * 64].rearrange("k o d -> k (o d)")
                            mm = pe.matmul(ps_o[:, u * 64:(u + 1) * 64], probT[0:rows, k % 2, c, :], values, start=(c == 0), stop=(c == 5))
                        mm.then_inc(pv_done, 1)

            @block.scalar
            def _(act):
                def exponentials(turn, k, first=False):
                    if k >= UNITS:
                        turn, k = turn + 1, k - UNITS
                    n = turn * UNITS + k
                    act.wait_ge(less_ready, n + 1)
                    if not first:
                        act.wait_ge(t_ready, n - 1 + START)
                        act.wait_ge(share_ready, n - 1 + START)
                    nc.scalar.activation(prob[:, k % 2, :], ps_s[:, k % 2, 0:L1_KEYS], ACT.Exp, bias=less[:, k % 2:k % 2 + 1],
                                         accum_out=total[:, k % 2:k % 2 + 1]).then_inc(prob_ready, 1)

                exponentials(0, 0, first=True)
                with act.Fori(0, TURNS) as it:
                    for k in range(UNITS):
                        exponentials(it, k + 1)

            @block.vector
            def _(dve):
                start(dve, o_kept, share_ready)

                def fetch(tile, half):
                    dve.tensor_scalar(tile_q[:, half, :, :].rearrange("p h t -> p (h t)"), qT[:, bass.ds(tile * (2 * PART), 2 * PART)],
                                      1.0, None, ALU.mult).then_inc(tile_ready, 1)

                def maxima(turn, k):
                    if k >= UNITS:
                        turn, k = turn + 1, k - UNITS
                    n = turn * UNITS + k
                    dve.wait_ge(s_ready, n + 1)
                    part = ps_s[:, k % 2, SEQ:L1_KEYS]
                    dve.tensor_tensor(part, part, masked[:, bass.ds((turn // 2) * KEYS, KEYS)], ALU.add).then_inc(mask_added, 1)
                    dve.wait_ge(mask_added, n + 1)
                    dve.tensor_reduce(less[:, k % 2:k % 2 + 1], ps_s[:, k % 2, 0:L1_KEYS], AX.X, ALU.max, negate=True).then_inc(less_ready, 1)

                def keep(turn, k):
                    if k >= UNITS:
                        turn, k = turn + 1, k - UNITS
                    n = turn * UNITS + k
                    dve.wait_ge(t_ready, n + 1 + START)
                    dve.wait_ge(pv_done, n - 1 + START)
                    dve.tensor_copy(probT[:, k % 2, 0:4, :], ps_a[:, k % 2, :].rearrange("p (c t) -> p c t", c=4)).then_inc(t_kept, 1)
                    dve.tensor_copy(probT[0:CTX_CHUNK, k % 2, 4:6, :], ps_b[0:CTX_CHUNK, 0:2 * PART].rearrange("p (c t) -> p c t", c=2)).then_inc(t_kept, 1)

                fetch(0, 0)
                fetch(1, 1)
                maxima(0, 0)
                maxima(0, 1)
                dve.wait_ge(t_ready, 1 + START)
                dve.tensor_copy(probT[:, 0, 0:4, :], ps_a[:, 0, :].rearrange("p (c t) -> p c t", c=4)).then_inc(t_kept, 1)
                dve.tensor_copy(probT[0:CTX_CHUNK, 0, 4:6, :], ps_b[0:CTX_CHUNK, 0:2 * PART].rearrange("p (c t) -> p c t", c=2)).then_inc(t_kept, 1)
                with dve.Fori(0, TURNS) as it:
                    for k in range(UNITS):
                        n = it * UNITS + k
                        half, u = divmod(k, U)
                        dve.wait_ge(prob_ready, n + 1)
                        if u == 0:
                            dve.wait_ge(o_kept, it * 4 + 2 * half + START)
                        dve.reciprocal(share[:, k % 2:k % 2 + 1], total[:, k % 2:k % 2 + 1]).then_inc(share_ready, 1)
                        if u == U - 1:
                            dve.wait_ge(s_ready, n + 1)
                            fetch(it * 2 + 2 + half, half)
                        maxima(it, k + 2)
                        keep(it, k + 1)
                        if u == U - 1:
                            dve.wait_ge(pv_done, n + 1 + START)
                            dve.wait_ge(share_ready, n + 1 + START)
                            for h in range(2):
                                out = m.xn[:, bass.ds(it * 2 + half, 1), h * 64:(h + 1) * 64].rearrange("p o d -> p (o d)")
                                dve.tensor_scalar(out, ps_o[:, h * 64:(h + 1) * 64], share[:, h:h + 1], None, ALU.mult).then_inc(o_kept, 1)


def latent_output(nc, m, a):
    with ExitStack() as ctx:
        sb = lambda n, s: ctx.enter_context(nc.sbuf_tensor(f"lato_{n}", s, FP32))
        sem = lambda n: m.semaphore(nc, f"lato_{n}")
        w, bias = sb("w", [DIM, DIM]), sb("bias", [PART, DIM])
        w_in, steps, turned, kept, y_ready, x_added = (sem(n) for n in ("w_in", "steps", "turned", "kept", "y_ready", "x_added"))
        ps_t = ctx.enter_context(nc.psum_tensor("lato_ps_t", [PART, 4, BLOCK], FP32))
        ps_y = ctx.enter_context(nc.psum_tensor("lato_ps_y", [PART, 4, BLOCK], FP32))
        gate = m.gate[:, 1:2]
        with nc.Block() as block:
            @block.sync
            def _(sp):
                sp.dma_start(w[:], a["L1_xattn_WoT"]).then_inc(w_in, 16)
                sp.wait_ge(w_in, 16)

            @block.tensor
            def _(pe):
                for t in range(BLOCKS):
                    for j in range(4):
                        mm = pe.transpose(ps_t[:, t, j * PART:(j + 1) * PART], m.xn[:, 4 * t + j, :], m.ident[:])
                    mm.then_inc(turned, 1)
                pe.wait_ge(w_in, 16)
                for t in range(BLOCKS):
                    pe.wait_ge(kept, t + 1)
                    for j in range(4):
                        i = 4 * t + j
                        mm = pe.matmul(ps_y[:, t, j * PART:(j + 1) * PART], m.xt[:, i * PART:(i + 1) * PART], w[:], start=True, stop=True)
                    mm.then_inc(y_ready, 1)

            @block.scalar
            def _(act):
                for t in range(BLOCKS):
                    act.wait_ge(turned, t + 1)
                    nc.scalar.activation(m.xt[:, t * BLOCK:(t + 1) * BLOCK], ps_t[:, t, :], ACT.Copy).then_inc(kept, 1)

            @block.vector
            def _(dve):
                c = Chain(dve, steps)
                c.did(dve.tensor_scalar(bias[:], m.row("L1_bo"), gate, None, ALU.mult))
                c.wait()
                for t in range(BLOCKS):
                    rows = m.x[:, 4 * t:4 * t + 4, :]
                    c.did(dve.tensor_tensor(rows, rows, bias[:].unsqueeze(1).to_broadcast([PART, 4, DIM]), ALU.add))
                c.wait()
                for t in range(BLOCKS):
                    rows = m.x[:, 4 * t:4 * t + 4, :].rearrange("p t d -> p (t d)")
                    dve.wait_ge(y_ready, t + 1)
                    dve.scalar_tensor_tensor(rows, ps_y[:, t, :], gate, rows, ALU.mult, ALU.add).then_inc(x_added, 1)


def ternary(nc, m, a):
    QB, EPS, ROUND = 128.0, 1e-5, 1.5 * 2.0 ** 23
    with ExitStack() as ctx:
        sb = lambda n, s: ctx.enter_context(nc.sbuf_tensor(f"tern_{n}", s, FP32))
        sem = lambda n: m.semaphore(nc, f"tern_{n}")
        w, wq = sb("w", [DIM, DIM]), sb("wq", [DIM, DIM])
        w_row, w_sum, x_row, x_max = sb("w_row", [PART, 1]), sb("w_sum", [PART, 1]), sb("x_row", [PART, 1]), sb("x_max", [PART, 1])
        beta, w_inv, x_inv, factor = sb("beta", [PART, 1]), sb("w_inv", [PART, 1]), sb("x_inv", [PART, 1]), sb("factor", [PART, 1])
        w_in, steps, rows_done, all_done, w_ready, x_ready, y_ready, x_added = (sem(n) for n in ("w_in", "steps", "rows_done", "all_done", "w_ready", "x_ready", "y_ready", "x_added"))
        ps_y = ctx.enter_context(nc.psum_tensor("tern_ps_y", [PART, 4, BLOCK], FP32))
        with nc.Block() as block:
            @block.sync
            def _(sp):
                sp.dma_start(w[:], a["L0_ffn_weight"]).then_inc(w_in, 16)
                sp.wait_ge(w_in, 16)

            @block.gpsimd
            def _(pool):
                pool.wait_ge(rows_done, 1)
                pool.partition_all_reduce(w_sum[:], w_row[:], PART, bass.bass_isa.ReduceOp.add).then_inc(all_done, 1)
                pool.wait_ge(rows_done, 2)
                pool.partition_all_reduce(x_max[:], x_row[:], PART, bass.bass_isa.ReduceOp.max).then_inc(all_done, 1)

            @block.vector
            def _(dve):
                c = Chain(dve, steps)
                step = lambda ins: (c.did(ins), c.wait())
                dve.wait_ge(w_in, 16)
                dve.tensor_reduce(w_row[:], w[:], AX.X, ALU.add, apply_absolute_value=True).then_inc(rows_done, 1)
                dve.tensor_reduce(x_row[:], m.xt[:, 0:TOKENS], AX.X, ALU.max, apply_absolute_value=True).then_inc(rows_done, 1)
                dve.wait_ge(all_done, 1)
                step(dve.tensor_scalar(beta[:], w_sum[:], 1.0 / (DIM * DIM), None, ALU.mult))
                step(dve.tensor_scalar(w_inv[:], beta[:], EPS, None, ALU.add))
                step(dve.reciprocal(w_inv[:], w_inv[:]))
                step(dve.tensor_scalar(wq[:], w[:], w_inv[:], None, ALU.mult))
                step(dve.tensor_scalar(wq[:], wq[:], ROUND, ROUND, ALU.add, ALU.subtract))
                dve.tensor_scalar(wq[:], wq[:], -1.0, 1.0, ALU.max, ALU.min).then_inc(w_ready, 1)
                dve.wait_ge(all_done, 2)
                step(dve.reciprocal(x_inv[:], x_max[:]))
                step(dve.tensor_scalar(factor[:], x_max[:], beta[:], 1.0 / QB, ALU.mult, ALU.mult))
                step(dve.tensor_scalar(factor[:], factor[:], m.gate[:, LAYERS:LAYERS + 1], None, ALU.mult))
                for t in range(BLOCKS):
                    xt = m.xt[:, t * BLOCK:(t + 1) * BLOCK]
                    step(dve.tensor_scalar(xt, xt, QB, x_inv[:], ALU.mult, ALU.mult))
                    dve.tensor_scalar(xt, xt, -QB + EPS, QB - EPS, ALU.max, ALU.min).then_inc(x_ready, 1)
                for t in range(BLOCKS):
                    rows = m.x[:, 4 * t:4 * t + 4, :].rearrange("p t d -> p (t d)")
                    dve.wait_ge(y_ready, t + 1)
                    dve.scalar_tensor_tensor(rows, ps_y[:, t, :], factor[:], rows, ALU.mult, ALU.add).then_inc(x_added, 1)

            @block.tensor
            def _(pe):
                pe.wait_ge(w_ready, 1)
                for t in range(BLOCKS):
                    pe.wait_ge(x_ready, t + 1)
                    for j in range(4):
                        i = 4 * t + j
                        mm = pe.matmul(ps_y[:, t, j * PART:(j + 1) * PART], m.xt[:, i * PART:(i + 1) * PART], wq[:], start=True, stop=True)
                    mm.then_inc(y_ready, 1)


L0_HEADS, L0_DH, TOP = 4, 32, 32
L0_SCALE = 1.0 / 32 ** 0.5
STATES = 64
FINE, COARSE = 32, 16
ROUND = 1.5 * 2.0 ** 23
TWO_PI = 6.2831845
LOG2_E = 1.4426950408889634
LN2_HIGH = 0.693359375
LN2_LOW = -2.12194440e-4
EXP_SERIES = (1 / 5040, 1 / 720, 1 / 120, 1 / 24, 1 / 6, 1 / 2, 1.0)
FREQ = 4


def film_tables(nc, ctx, m, a, keysT, values, masked, weight):
    H = L0_HEADS
    sb = lambda n, s, dt=FP32: ctx.enter_context(nc.sbuf_tensor(f"filmt_{n}", s, dt))
    sem = lambda n: m.semaphore(nc, f"filmt_{n}")
    wq, wk = sb("wq", [DIM, DIM]), sb("wk", [DIM, CDIM])
    wv, wf = sb("wv", [DIM, CDIM]), sb("wf", [DIM, 4 * DIM])
    qk, vf = sb("qk", [CDIM, H, DIM]), sb("vf", [CDIM, 4 * DIM])
    mask8, maskf = sb("mask8", [PART, ALLKEYS], U8), sb("maskf", [PART, ALLKEYS])
    text8 = sb("text8", [PART, TILES], U8)
    bias = sb("bias", [1, 4 * DIM])
    ps_w = ctx.enter_context(nc.psum_tensor("filmt_ps_w", [PART, 4, BLOCK], FP32))
    ps_k = ctx.enter_context(nc.psum_tensor("filmt_ps_k", [PART, 2, BLOCK], FP32))
    names = ("w_in", "masks_in", "bias_in", "steps", "qk_ready", "qk_kept", "vf_ready", "vf_kept", "k_ready", "k_kept", "v_ready", "v_kept", "bias_ready", "bias_laid", "zeroed")
    w_in, masks_in, bias_in, steps, qk_ready, qk_kept, vf_ready, vf_kept, k_ready, k_kept, v_ready, v_kept, bias_ready, bias_laid, zeroed = (sem(n) for n in names)

    def sync(sp):
        sp.dma_start(wq[:], a["L0_xattn_WqT"]).then_inc(w_in, 16)
        sp.dma_start(wk[:], a["L0_xattn_WkT"]).then_inc(w_in, 16)
        sp.dma_start(wv[:], a["L0_xattn_WvT"]).then_inc(w_in, 16)
        sp.dma_start(wf[:], a["L0_xattn_Wfilm"]).then_inc(w_in, 16)
        sp.dma_start(bias[:], a["L0_xattn_bfilm"].rearrange("(o n) -> o n", o=1)).then_inc(bias_in, 16)
        sp.dma_start(mask8[:], a["mask_BxS2_bf1"].rearrange("(o b) k -> o (b k)", o=1).to_broadcast([PART, ALLKEYS])).then_inc(masks_in, 16)
        sp.dma_start(text8[:], a["mask_BxS_bf1"]).then_inc(masks_in, 16)
        sp.wait_ge(bias_ready, 1)
        for n in range(BATCH * 2):
            sp.dma_start(values[CTX_CHUNK:CTX_CHUNK + 1, n, :], bias[:]).then_inc(bias_laid, 16)
        sp.wait_ge(bias_laid, 16 * BATCH * 2)

    def gpsimd(pool):
        pool.memset(keysT[:, BATCH, :], 0.0).then_inc(zeroed, 1)
        pool.wait_ge(zeroed, 1)
        pool.memset(masked[:, BATCH, :], 0.0).then_inc(zeroed, 1)

    def tensor(pe):
        pe.wait_ge(w_in, 64)
        for h in range(H):
            part = slice(h * L0_DH, (h + 1) * L0_DH)
            mm = pe.matmul(ps_w[0:CDIM, h, 0:DIM], wk[part, :], wq[part, :], start=True, stop=True)
        mm.then_inc(qk_ready, 1)
        for h in range(H):
            pe.wait_ge(qk_kept, 1)
            if h:
                pe.wait_ge(k_kept, h)
            for s in range(2):
                mm = pe.matmul(ps_k[:, s, 0:HALFKEYS], qk[:, h, :], m.ctxT[:, s * HALFKEYS:(s + 1) * HALFKEYS], start=True, stop=True)
            mm.then_inc(k_ready, 1)
        pe.matmul(ps_w[0:CDIM, 0, :], wv[:], wf[:], start=True, stop=True).then_inc(vf_ready, 1)
        pe.wait_ge(vf_kept, 1)
        for n in range(BATCH * 2):
            if n >= 3:
                pe.wait_ge(v_kept, n - 2)
            pe.matmul(ps_w[0:CTX_CHUNK, 1 + n % 3, :], m.ctxT[:, n * CTX_CHUNK:(n + 1) * CTX_CHUNK], vf[:], start=True,
                      stop=True).then_inc(v_ready, 1)

    def scalar(act):
        act.wait_ge(qk_ready, 1)
        nc.scalar.activation(qk[:], ps_w[0:CDIM, :, 0:DIM], ACT.Copy).then_inc(qk_kept, 1)
        act.wait_ge(vf_ready, 1)
        nc.scalar.activation(vf[:], ps_w[0:CDIM, 0, :], ACT.Copy, scale=m.row("mod_gate")[0:CDIM]).then_inc(vf_kept, 1)
        for n in range(BATCH * 2):
            act.wait_ge(v_ready, n + 1)
            nc.scalar.activation(values[0:CTX_CHUNK, n, :], ps_w[0:CTX_CHUNK, 1 + n % 3, :], ACT.Copy).then_inc(v_kept, 1)

    def vector(dve):
        c = Chain(dve, steps)
        step = lambda ins: (c.did(ins), c.wait())
        dve.wait_ge(bias_in, 16)
        step(dve.tensor_scalar(bias[:], bias[:], m.row("mod_gate")[0:1], None, ALU.mult))
        scales = bias[:].rearrange("o (n s d) -> o n s d", n=2, s=2)[:, :, 0, :]
        dve.tensor_scalar(scales, scales, 1.0, None, ALU.add).then_inc(bias_ready, 1)
        dve.wait_ge(masks_in, 32)
        step(dve.memset(weight[:], 0.0))
        step(dve.tensor_copy(weight[:, 1:TILES + 1], text8[:]))
        step(dve.tensor_scalar(weight[:], weight[:], 1.0 / H, None, ALU.mult))
        step(dve.tensor_copy(maskf[:], mask8[:]))
        step(dve.tensor_scalar(masked[:, 0:BATCH, :].rearrange("p b k -> p (b k)"), maskf[:], 1.0, BIG, ALU.subtract, ALU.mult))
        for h in range(H):
            dve.wait_ge(k_ready, h + 1)
            dst = keysT[:, 0:BATCH, h * KEYS:(h + 1) * KEYS]
            dve.tensor_copy(dst, ps_k[:, :, 0:HALFKEYS].rearrange("p s (v k) -> p s v k", v=2)).then_inc(k_kept, 1)

    return {"sync": sync, "gpsimd": gpsimd, "tensor": tensor, "scalar": scalar, "vector": vector}


def film_tokens(nc, m, keysT, values, masked, weight, mod):
    H, W = L0_HEADS, L0_HEADS * KEYS
    keys = keysT[:].rearrange("p b k -> p (b k)")
    with ExitStack() as ctx:
        sb = lambda n, s: ctx.enter_context(nc.sbuf_tensor(f"filma_{n}", s, FP32))
        sem = lambda n: m.semaphore(nc, f"filma_{n}")
        tile_x = sb("tile_x", [DIM, 2, PART])
        score, rest = sb("score", [PART, 2, W]), sb("rest", [PART, 2, W])
        top = sb("top", [PART, 2, H, TOP])
        less, total, share = sb("less", [PART, 2, H]), sb("total", [PART, 2, H]), sb("share", [PART, 2, H])
        e_all, e_rest, e_top = sb("e_all", [PART, 2, W]), sb("e_rest", [PART, 2, W]), sb("e_top", [PART, H, TOP])
        prob = sb("prob", [PART, 2, W])
        probT = sb("probT", [CTX_CHUNK + 1, 2, PART])
        ps_s = ctx.enter_context(nc.psum_tensor("filma_ps_s", [PART, 2, 2 * BLOCK], FP32))
        ps_t = ctx.enter_context(nc.psum_tensor("filma_ps_t", [PART, BLOCK], FP32))
        ps_f = ctx.enter_context(nc.psum_tensor("filma_ps_f", [PART, BLOCK], FP32))
        names = ("tile_ready", "s_ready", "s_kept", "steps", "top_ready", "e_ready", "share_ready", "left_ready", "prob_ready", "t_ready", "t_kept", "f_ready", "f_kept", "zeroed")
        tile_ready, s_ready, s_kept, steps, top_ready, e_ready, share_ready, left_ready, prob_ready, t_ready, t_kept, f_ready, f_kept, zeroed = (sem(n) for n in names)
        with nc.Block() as block:
            @block.tensor
            def _(pe):
                start(pe, f_ready, t_ready)
                def scores(turn, h):
                    if h >= 2:
                        turn, h = turn + 1, h - 2
                    n = turn * 2 + h
                    pe.wait_ge(tile_ready, n + 1)
                    base = (turn // 2) * W
                    pe.matmul(ps_s[:, h, 0:BLOCK], tile_x[:, h, :], keys[:, bass.ds(base, BLOCK)], start=True, stop=True)
                    pe.matmul(ps_s[:, h, BLOCK:W], tile_x[:, h, :], keys[:, bass.ds(base + BLOCK, W - BLOCK)], start=True, stop=True).then_inc(s_ready, 1)

                scores(0, 0)
                scores(0, 1)
                with pe.Fori(0, TILES // 2) as it:
                    for h in range(2):
                        n = it * 2 + h
                        pe.wait_ge(s_kept, n + 1 + START)
                        scores(it, h + 2)
                        pe.wait_ge(prob_ready, n + 2 + START)
                        pe.wait_ge(t_kept, n + START)
                        for c in range(2):
                            for g in range(H):
                                cols = slice(g * KEYS + c * CTX_CHUNK, g * KEYS + (c + 1) * CTX_CHUNK)
                                mm = pe.matmul(ps_t[0:CTX_CHUNK, c * PART:(c + 1) * PART], prob[:, h, cols], m.ident[:],
                                               start=(g == 0), stop=(g == H - 1))
                        mm.then_inc(t_ready, 1)
                        pe.wait_ge(t_kept, n + 1 + START)
                        pe.wait_ge(f_kept, n + 1 + START)
                        for c in range(2):
                            v = values[:, bass.ds((it // 2) * 2 + c, 1), :].rearrange("k o n -> k (o n)")
                            rows = CTX_CHUNK + 1 - c
                            mm = pe.matmul(ps_f[:], probT[0:rows, c, :], v[0:rows], start=(c == 0), stop=(c == 1))
                        mm.then_inc(f_ready, 1)

            @block.scalar
            def _(act):
                start(act, t_kept, e_ready, f_kept)
                act.wait_ge(zeroed, 2)
                nc.scalar.activation(e_top[:, 0, 0:1], total[:, 0, 0:1], ACT.Exp).then_inc(e_ready, 1)
                with act.Fori(0, TILES // 2) as it:
                    for h in range(2):
                        n = it * 2 + h
                        act.wait_ge(top_ready, n + 1)
                        act.wait_ge(prob_ready, n + START)
                        act.wait_ge(share_ready, n + START)
                        act.wait_ge(e_ready, n + 1 + START)
                        for g in range(H):
                            cols = slice(g * KEYS, (g + 1) * KEYS)
                            bias = less[:, h, g:g + 1]
                            nc.scalar.activation(e_all[:, h, cols], score[:, h, cols], ACT.Exp, scale=L0_SCALE, bias=bias)
                            nc.scalar.activation(e_rest[:, h, cols], rest[:, h, cols], ACT.Exp, scale=L0_SCALE, bias=bias)
                            ins = nc.scalar.activation(e_top[:, g, :], top[:, h, g, :], ACT.Exp, scale=L0_SCALE, bias=bias,
                                                       accum_out=total[:, h, g:g + 1])
                        ins.then_inc(e_ready, 1)
                        act.wait_ge(t_ready, n + 1 + START)
                        act.wait_ge(f_ready, n + START)
                        nc.scalar.activation(probT[0:CTX_CHUNK, :, :].rearrange("k c t -> k (c t)"), ps_t[0:CTX_CHUNK, 0:2 * PART],
                                             ACT.Copy).then_inc(t_kept, 1)
                        nc.scalar.activation(mod[:, bass.ds(n + 1, 1), :].rearrange("p o n -> p (o n)"), ps_f[:], ACT.Copy).then_inc(f_kept, 1)
                act.wait_ge(f_ready, TILES + START)
                nc.scalar.activation(mod[:, TILES + 1, :], ps_f[:], ACT.Copy).then_inc(f_kept, 1)

            @block.gpsimd
            def _(pool):
                start(pool, prob_ready)
                pool.memset(probT[:], 1.0).then_inc(prob_ready, 1)
                with pool.Fori(0, TILES // 2) as it:
                    for h in range(2):
                        n = it * 2 + h
                        pool.wait_ge(t_ready, it * 2 + START)
                        pool.wait_ge(e_ready, n + 2 + START)
                        pool.tensor_tensor(prob[:, h, :], e_all[:, h, :], e_rest[:, h, :], ALU.subtract).then_inc(left_ready, 1)
                        pool.wait_ge(left_ready, n + 1)
                        pool.wait_ge(share_ready, n + 2 + START)
                        p3 = prob[:, h, :].rearrange("p (g k) -> p g k", g=H)
                        pool.tensor_tensor(p3, p3, share[:, h, :].unsqueeze(2).to_broadcast([PART, H, KEYS]), ALU.mult).then_inc(prob_ready, 1)

            @block.vector
            def _(dve):
                start(dve, s_kept, share_ready)
                def fetch(tile, half):
                    dve.tensor_scalar(tile_x[:, half, :], m.xt[:, bass.ds(tile * PART, PART)], 1.0, None, ALU.mult).then_inc(tile_ready, 1)

                def use_sums(n, h):
                    dve.wait_ge(e_ready, n + 1 + START)
                    dve.wait_ge(prob_ready, n + START)
                    c.did(dve.reciprocal(share[:, h, :], total[:, h, :]))
                    c.wait()
                    dve.tensor_tensor(share[:, h, :], share[:, h, :], weight[:, bass.ds(n, 1)].to_broadcast([PART, H]),
                                      ALU.mult).then_inc(share_ready, 1)

                dve.memset(total[:], 1.0).then_inc(zeroed, 1)
                dve.memset(ps_f[:], 0.0).then_inc(zeroed, 1)
                dve.wait_ge(zeroed, 2)
                c = Chain(dve, steps)
                fetch(0, 0)
                fetch(1, 1)
                with dve.Fori(0, TILES // 2) as it:
                    for h in range(2):
                        n = it * 2 + h
                        dve.wait_ge(s_ready, n + 1)
                        dve.wait_ge(e_ready, n + START)
                        s3 = score[:, h, :].rearrange("p (g k) -> p g k", g=H)
                        dve.tensor_tensor(s3, ps_s[:, h, 0:W].rearrange("p (g k) -> p g k", g=H),
                                          masked[:, bass.ds(it // 2, 1), :].to_broadcast([PART, H, KEYS]), ALU.add).then_inc(s_kept, 1)
                        dve.wait_ge(s_kept, n + 1 + START)
                        fetch(n + 2, h)
                        found = [0] * H
                        for r in range(TOP // 8):
                            src = score if r == 0 else rest
                            for g in range(H):
                                cols = slice(g * KEYS, (g + 1) * KEYS)
                                c.wait_for(found[g])
                                c.did(dve.max(top[:, h, g, 8 * r:8 * r + 8], src[:, h, cols]))
                                found[g] = c.n
                            for g in range(H):
                                cols = slice(g * KEYS, (g + 1) * KEYS)
                                c.wait_for(found[g])
                                c.did(dve.match_replace(rest[:, h, cols], top[:, h, g, 8 * r:8 * r + 8], src[:, h, cols], -BIG))
                                found[g] = c.n
                            if r == 1:
                                use_sums(n, 1 - h)
                        c.wait()
                        dve.tensor_scalar(less[:, h, :], top[:, h, :, 0], -L0_SCALE, None, ALU.mult).then_inc(top_ready, 1)
                    c.clear()
                use_sums(TILES, 1)


def state_kernel(nc, ctx, m, a, kernel_dram):
    S = STATES
    sb = lambda n, s, dt=FP32: ctx.enter_context(nc.sbuf_tensor(f"ssmk_{n}", s, dt))
    sem = lambda n: m.semaphore(nc, f"ssmk_{n}")
    params = sb("params", [PART, 4, DIM])
    consts = sb("consts", [PART, 3 + FINE + COARSE])
    dt_row = sb("dt", [PART, DIM])
    two_n = sb("two_n", [PART, DIM], mybir.dt.int32)
    x, turns, tmp = sb("x", [PART, DIM]), sb("turns", [PART, DIM]), sb("tmp", [PART, DIM])
    ang_c, ang_s = sb("ang_c", [PART, DIM]), sb("ang_s", [PART, DIM])
    cosy, siny, half, th = sb("cosy", [PART, DIM]), sb("siny", [PART, DIM]), sb("half", [PART, DIM]), sb("th", [PART, DIM])
    wr, wi, qr, qi = sb("wr", [PART, DIM]), sb("wi", [PART, DIM]), sb("qr", [PART, DIM]), sb("qi", [PART, DIM])
    den, c1, c2 = sb("den", [PART, DIM]), sb("c1", [PART, DIM]), sb("c2", [PART, DIM])
    fine, mag, angle = sb("fine", [PART, DIM, FINE]), sb("mag", [PART, DIM, FINE]), sb("angle", [PART, DIM, FINE])
    cmag, cang = sb("cmag", [PART, DIM, COARSE]), sb("cang", [PART, DIM, COARSE])
    ccos, csin, coarse = sb("ccos", [PART, DIM, COARSE]), sb("csin", [PART, DIM, COARSE]), sb("coarse", [PART, DIM, COARSE])
    rows = angle[0:COARSE].rearrange("p d b -> p (d b)")
    ps_k = ctx.enter_context(nc.psum_tensor("ssm_ps_k", [PART, 2, BLOCK], FP32))
    names = ("params_in", "steps", "dve_ready", "act_done", "mags_ready", "k_ready", "k_kept", "k_out", "pool_steps")
    params_in, steps, dve_ready, act_done, mags_ready, k_ready, k_kept, k_out, pool_steps = (sem(n) for n in names)
    off_part, off_part_rad, quarter_rad = consts[:, 0:1], consts[:, 1:2], consts[:, 2:3]
    fine_l, coarse_l = consts[:, 3:3 + FINE], consts[:, 3 + FINE:3 + FINE + COARSE]
    across = lambda v, n: v.unsqueeze(2).to_broadcast([PART, DIM, n])
    along = lambda v, n: v.unsqueeze(1).to_broadcast([PART, DIM, n])

    def sync(sp):
        sp.dma_start(params[:], a["L0_xattn_AC"]).then_inc(params_in, 16)
        sp.dma_start(consts[:], a["ssm_consts"]).then_inc(params_in, 16)
        for half_rows in range(2):
            sp.wait_ge(k_kept, 8)
            part = slice(half_rows * 8, half_rows * 8 + 8)
            sp.dma_start(kernel_dram[:, part, :].rearrange("d a b -> a d b"),
                         rows[part, :].rearrange("a (d b) -> a d b", b=FINE)).then_inc(k_out, 16)
        sp.wait_ge(k_out, 32)

    def gpsimd(pool):
        pool.wait_ge(dve_ready, 1)
        pool.tensor_tensor(mag[:], across(x[:], FINE), along(fine_l, FINE), ALU.mult).then_inc(mags_ready, 1)
        pool.tensor_tensor(cmag[:], across(x[:], COARSE), along(coarse_l, COARSE), ALU.mult).then_inc(mags_ready, 1)

    def scalar(act):
        act.wait_ge(dve_ready, 1)
        nc.scalar.activation(th[:], x[:], ACT.Tanh, scale=0.5).then_inc(act_done, 1)
        act.wait_ge(mags_ready, 2)
        nc.scalar.activation(mag[:], mag[:], ACT.Exp).then_inc(act_done, 1)
        nc.scalar.activation(cmag[:], cmag[:], ACT.Exp).then_inc(act_done, 1)
        act.wait_ge(dve_ready, 2)
        nc.scalar.activation(cosy[:], ang_c[:], ACT.Sin, scale=-TWO_PI, bias=quarter_rad).then_inc(act_done, 1)
        nc.scalar.activation(siny[:], turns[:], ACT.Sin, scale=TWO_PI).then_inc(act_done, 1)
        nc.scalar.activation(half[:], turns[:], ACT.Sin, scale=TWO_PI / 2).then_inc(act_done, 1)
        act.wait_ge(dve_ready, 3)
        nc.scalar.activation(csin[:], csin[:], ACT.Sin, scale=-TWO_PI).then_inc(act_done, 1)
        nc.scalar.activation(ccos[:], ccos[:], ACT.Sin, scale=-TWO_PI, bias=quarter_rad).then_inc(act_done, 1)
        act.wait_ge(dve_ready, 4)
        nc.scalar.activation(fine[:], fine[:], ACT.Sin, scale=-TWO_PI, bias=off_part_rad).then_inc(act_done, 1)
        for g in range(8):
            act.wait_ge(k_ready, g + 1)
            nc.scalar.activation(rows[:, g * BLOCK:(g + 1) * BLOCK], ps_k[0:COARSE, g % 2, :], ACT.Copy).then_inc(k_kept, 1)

    def vector(dve):
        c = Chain(dve, steps)
        step = lambda ins: (c.did(ins), c.wait())
        tt = lambda out, a0, a1, op: step(dve.tensor_tensor(out, a0, a1, op))
        ar, ai, cr, ci = (params[:, n, :] for n in range(4))

        def reduced(out, work, src, offset):
            step(dve.tensor_scalar(work, src, offset, ROUND, ALU.add, ALU.add))
            return dve.scalar_tensor_tensor(out, work, ROUND, src, ALU.subtract, ALU.subtract)

        log_dt = m.row("log_dt")
        step(dve.tensor_scalar(tmp[:], log_dt, LOG2_E, ROUND, ALU.mult, ALU.add))
        step(dve.tensor_scalar(tmp[:], tmp[:], ROUND, None, ALU.subtract))
        step(dve.scalar_tensor_tensor(x[:], tmp[:], -LN2_HIGH, log_dt, ALU.mult, ALU.add))
        step(dve.scalar_tensor_tensor(x[:], tmp[:], -LN2_LOW, x[:], ALU.mult, ALU.add))
        step(dve.tensor_scalar(two_n[:], tmp[:], 127.0, None, ALU.add))
        step(dve.tensor_scalar(two_n[:], two_n[:], 23, None, ALU.logical_shift_left))
        step(dve.tensor_scalar(dt_row[:], x[:], EXP_SERIES[0], None, ALU.mult))
        for factor in EXP_SERIES[1:]:
            step(dve.scalar_tensor_tensor(dt_row[:], dt_row[:], factor, x[:], ALU.add, ALU.mult))
        step(dve.tensor_scalar(dt_row[:], dt_row[:], 1.0, None, ALU.add))
        tt(dt_row[:], dt_row[:], two_n[:].bitcast(FP32), ALU.mult)
        dve.wait_ge(params_in, 32)
        step(dve.tensor_scalar(turns[:], ai, 1.0 / (2 * 3.141592653589793), None, ALU.mult))
        tt(turns[:], turns[:], dt_row[:], ALU.mult)
        dve.tensor_tensor(x[:], ar, dt_row[:], ALU.mult).then_inc(dve_ready, 1)
        step(reduced(tmp[:], ang_s[:], turns[:], 0.0))
        step(dve.tensor_scalar(turns[:], tmp[:], -1.0, None, ALU.mult))
        reduced(ang_c[:], ang_s[:], turns[:], 0.25).then_inc(dve_ready, 1)
        tt(cang[:], across(turns[:], COARSE), along(coarse_l, COARSE), ALU.mult)
        step(reduced(csin[:], coarse[:], cang[:], 0.0))
        reduced(ccos[:], coarse[:], cang[:], 0.25).then_inc(dve_ready, 1)
        tt(angle[:], across(turns[:], FINE), along(fine_l, FINE), ALU.mult)
        step(dve.tensor_scalar(fine[:], angle[:], off_part, ROUND, ALU.add, ALU.add))
        dve.scalar_tensor_tensor(fine[:], fine[:], ROUND, angle[:], ALU.subtract, ALU.subtract).then_inc(dve_ready, 1)
        dve.wait_ge(act_done, 6)
        step(dve.tensor_scalar(tmp[:], th[:], -1.0, 1.0, ALU.mult, ALU.add))
        step(dve.reciprocal(tmp[:], tmp[:]))
        tt(th[:], th[:], tmp[:], ALU.mult)
        step(dve.tensor_scalar(th[:], th[:], 2.0, None, ALU.mult))
        tt(wr[:], th[:], cosy[:], ALU.mult)
        tt(half[:], half[:], half[:], ALU.mult)
        step(dve.scalar_tensor_tensor(wr[:], half[:], -2.0, wr[:], ALU.mult, ALU.add))
        step(dve.scalar_tensor_tensor(wi[:], th[:], 1.0, siny[:], ALU.add, ALU.mult))
        tt(den[:], ar, ar, ALU.mult)
        tt(tmp[:], ai, ai, ALU.mult)
        tt(den[:], den[:], tmp[:], ALU.add)
        step(dve.reciprocal(den[:], den[:]))
        tt(qr[:], wr[:], ar, ALU.mult)
        tt(tmp[:], wi[:], ai, ALU.mult)
        tt(qr[:], qr[:], tmp[:], ALU.add)
        tt(qr[:], qr[:], den[:], ALU.mult)
        tt(qi[:], wi[:], ar, ALU.mult)
        tt(tmp[:], wr[:], ai, ALU.mult)
        tt(qi[:], qi[:], tmp[:], ALU.subtract)
        tt(qi[:], qi[:], den[:], ALU.mult)
        tt(wr[:], cr, qr[:], ALU.mult)
        tt(tmp[:], ci, qi[:], ALU.mult)
        tt(wr[:], wr[:], tmp[:], ALU.subtract)
        tt(wi[:], cr, qi[:], ALU.mult)
        tt(tmp[:], ci, qr[:], ALU.mult)
        tt(wi[:], wi[:], tmp[:], ALU.add)
        top, low = slice(0, S), slice(S, 2 * S)
        step(dve.tensor_scalar(c1[top], wr[top], 2.0, None, ALU.mult))
        step(dve.tensor_scalar(c1[low], wi[low], -2.0, None, ALU.mult))
        step(dve.tensor_scalar(c2[top], wi[top], -2.0, None, ALU.mult))
        step(dve.tensor_scalar(c2[low], wr[low], -2.0, None, ALU.mult))
        dve.wait_ge(act_done, 8)
        tt(ccos[:], ccos[:], across(c1[:], COARSE), ALU.mult)
        tt(csin[:], csin[:], across(c2[:], COARSE), ALU.mult)
        tt(ccos[:], ccos[:], csin[:], ALU.add)
        tt(coarse[:], ccos[:], cmag[:], ALU.mult)
        dve.wait_ge(act_done, 9)
        dve.tensor_tensor(fine[:], fine[:], mag[:], ALU.mult).then_inc(dve_ready, 1)

    def tensor(pe):
        pe.wait_ge(dve_ready, 5)
        for d in range(DIM):
            g, at = divmod(d, BLOCK // FINE)
            if g >= 2 and at == 0:
                pe.wait_ge(k_kept, g - 1)
            mm = pe.matmul(ps_k[0:COARSE, g % 2, at * FINE:(at + 1) * FINE], coarse[:, d, :], fine[:, d, :], start=True, stop=True)
            if at == BLOCK // FINE - 1:
                mm.then_inc(k_ready, 1)

    return {"sync": sync, "gpsimd": gpsimd, "tensor": tensor, "scalar": scalar, "vector": vector}


def state_space(nc, m, tables, u, mod, z):
    with ExitStack() as ctx:
        sb = lambda n, s, dt=FP32: ctx.enter_context(nc.sbuf_tensor(f"conv_{n}", s, dt))
        sem = lambda n: m.semaphore(nc, f"conv_{n}")
        cos, sin, turn, kern, tables_in, kern_in = tables
        kernT = sb("kernT", [PART, FREQ, DIM])
        kr, ki, tmp = sb("kr", [PART, FREQ, DIM]), sb("ki", [PART, FREQ, DIM]), sb("tmp", [PART, DIM])
        kcs = sb("kcs", [PART, 2, DIM])
        p1, p2 = sb("p1", [PART, 2, BLOCK]), sb("p2", [PART, 2, BLOCK])
        yr, yi = sb("yr", [PART, FREQ, BLOCK]), sb("yi", [PART, FREQ, BLOCK])
        ps_t = ctx.enter_context(nc.psum_tensor("conv_ps_t", [PART, BLOCK], FP32))
        ps_k = ctx.enter_context(nc.psum_tensor("conv_ps_k", [PART, BLOCK], FP32))
        ps_x = ctx.enter_context(nc.psum_tensor("conv_ps_x", [PART, 2, 2, BLOCK], FP32))
        ps_y = ctx.enter_context(nc.psum_tensor("conv_ps_y", [PART, 2, BLOCK], FP32))
        names = ("steps", "u_ready", "kern_ready", "kern_turned", "kernT_kept", "k_ready", "k_kept", "x_ready", "products_ready", "yr_ready", "y_ready", "y_kept")
        steps, u_ready, kern_ready, kern_turned, kernT_kept, k_ready, k_kept, x_ready, products_ready, yr_ready, y_ready, y_kept = (sem(n) for n in names)
        wide = lambda v: v.unsqueeze(1).to_broadcast([PART, BATCH, DIM])
        four = lambda v: v.rearrange("p (b d) -> p b d", b=BATCH)
        scaled = sb("scaled", [PART, 2, BLOCK])
        z_begun, pool_steps = sem("z_begun"), sem("pool_steps")
        at_step = lambda v, l: v[:].rearrange("p (b l) d -> p b l d", b=BATCH)[:, :, l, :]
        by_step = lambda l: mod[:, 2:TILES + 2, :].rearrange("p (b l) n -> p b l n", b=BATCH)[:, :, l, :]
        shift_out = lambda l: by_step(l)[:, :, 3 * DIM:4 * DIM]

        def modulate(eng, c, t):
            rows = u[:, 4 * t:4 * t + 4, :]
            part = mod[:, 4 * t + 2:4 * t + 6, :]
            every = lambda name: m.row(name).unsqueeze(1).to_broadcast([PART, 4, DIM])
            c.wait()
            c.did(eng.tensor_tensor(rows, rows, every("in_g"), ALU.mult))
            c.wait()
            c.did(eng.tensor_tensor(rows, rows, every("in_b"), ALU.add))
            c.wait()
            c.did(eng.tensor_tensor(rows, rows, part[:, :, 0:DIM], ALU.mult))
            c.wait()
            eng.tensor_tensor(rows, rows, part[:, :, DIM:2 * DIM], ALU.add).then_inc(u_ready, 1)

        with nc.Block() as block:
            @block.sync
            def _(sp):
                sp.wait_ge(tables_in, 48)

            @block.vector
            def _(dve):
                c = Chain(dve, steps)
                step = lambda ins: (c.did(ins), c.wait())
                dve.wait_ge(kern_in, 16)
                dve.tensor_scalar(kern[:, 0:1], kern[:, 0:1], m.col("D_skip"), None, ALU.add).then_inc(kern_ready, 1)
                modulate(dve, c, 0)
                modulate(dve, c, 1)
                dve.wait_ge(tables_in, 48)
                for f in range(FREQ):
                    dve.wait_ge(k_ready, f + 1)
                    step(dve.tensor_copy(kcs[:], ps_k[:, 0:2 * DIM].rearrange("p (s d) -> p s d", s=2)))
                    kc, ks = kcs[:, 0, :], kcs[:, 1, :]
                    co, si = turn[:, f, 0:1], turn[:, f, 1:2]
                    step(dve.tensor_scalar(tmp[:], ks, si, None, ALU.mult))
                    step(dve.scalar_tensor_tensor(kr[:, f, :], kc, co, tmp[:], ALU.mult, ALU.add))
                    step(dve.tensor_scalar(tmp[:], ks, co, None, ALU.mult))
                    dve.scalar_tensor_tensor(ki[:, f, :], kc, si, tmp[:], ALU.mult, ALU.subtract).then_inc(k_kept, 1)
                for f in range(FREQ):
                    dve.wait_ge(k_kept, f + 1)
                    dve.wait_ge(x_ready, f + 1)
                    if f:
                        dve.wait_ge(yr_ready, 2 * f)
                    xc, xs = four(ps_x[:, f % 2, 0, :]), four(ps_x[:, f % 2, 1, :])
                    k_r, k_i = wide(kr[:, f, :]), wide(ki[:, f, :])
                    c.did(dve.tensor_tensor(four(p1[:, 0, :]), xc, k_r, ALU.mult))
                    c.did(dve.tensor_tensor(four(p1[:, 1, :]), xs, k_i, ALU.mult))
                    c.did(dve.tensor_tensor(four(p2[:, 0, :]), xs, k_r, ALU.mult))
                    c.wait()
                    dve.tensor_tensor(four(p2[:, 1, :]), xc, k_i, ALU.mult).then_inc(products_ready, 1)
                for l in range(FREQ):
                    dve.wait_ge(y_ready, l + 1)
                    dve.tensor_tensor(four(scaled[:, l % 2, :]), four(ps_y[:, l % 2, :]), by_step(l)[:, :, 2 * DIM:3 * DIM], ALU.mult).then_inc(y_kept, 1)
                    dve.wait_ge(y_kept, l + 1)
                    dve.wait_ge(z_begun, l + 1)
                    step(dve.tensor_tensor(at_step(z, l), at_step(z, l), four(scaled[:, l % 2, :]), ALU.add))

            @block.gpsimd
            def _(pool):
                c = Chain(pool, pool_steps)
                modulate(pool, c, 2)
                modulate(pool, c, 3)
                for l in range(FREQ):
                    pool.tensor_tensor(at_step(z, l), at_step(m.xn, l), shift_out(l), ALU.add).then_inc(z_begun, 1)
                for f in range(FREQ):
                    pool.wait_ge(products_ready, f + 1)
                    pool.tensor_tensor(yr[:, f, :], p1[:, 0, :], p1[:, 1, :], ALU.add).then_inc(yr_ready, 1)
                    pool.tensor_tensor(yi[:, f, :], p2[:, 0, :], p2[:, 1, :], ALU.subtract).then_inc(yr_ready, 1)

            @block.scalar
            def _(act):
                act.wait_ge(kern_turned, 1)
                nc.scalar.activation(kernT[:].rearrange("l c d -> l (c d)"), ps_t[:], ACT.Copy).then_inc(kernT_kept, 1)

            @block.tensor
            def _(pe):
                pe.wait_ge(kern_ready, 1)
                for l in range(FREQ):
                    mm = pe.transpose(ps_t[:, l * PART:(l + 1) * PART], kern[:, l * PART:(l + 1) * PART], m.ident[:])
                mm.then_inc(kern_turned, 1)
                pe.wait_ge(tables_in, 48)
                pe.wait_ge(kernT_kept, 1)
                for f in range(FREQ):
                    if f:
                        pe.wait_ge(k_kept, f)
                    for s, table in enumerate((cos, sin)):
                        for l in range(FREQ):
                            mm = pe.matmul(ps_k[:, s * DIM:(s + 1) * DIM], table[:, l, f * PART:(f + 1) * PART], kernT[:, l, :],
                                           start=(l == 0), stop=(l == FREQ - 1))
                    mm.then_inc(k_ready, 1)
                pe.wait_ge(u_ready, BLOCKS)
                for f in range(FREQ):
                    if f >= 2:
                        pe.wait_ge(products_ready, f - 1)
                    for s, table in enumerate((cos, sin)):
                        for l in range(FREQ):
                            mm = pe.matmul(ps_x[:, f % 2, s, :], table[:, l, f * PART:(f + 1) * PART],
                                           u[:].rearrange("p (b l) d -> p b l d", b=BATCH)[:, :, l, :], start=(l == 0), stop=(l == FREQ - 1))
                    mm.then_inc(x_ready, 1)
                pe.wait_ge(yr_ready, 2 * FREQ)
                for l in range(FREQ):
                    if l >= 2:
                        pe.wait_ge(y_kept, l - 1)
                    for s, (table, y) in enumerate(((cos, yr), (sin, yi))):
                        for f in range(FREQ):
                            mm = pe.matmul(ps_y[:, l % 2, :], table[:, f, l * PART:(l + 1) * PART], y[:, f, :],
                                           start=(s == 0 and f == 0), stop=(s == 1 and f == FREQ - 1))
                    mm.then_inc(y_ready, 1)


def feed_forward(nc, m, a, z):
    CH = 4
    with ExitStack() as ctx:
        sb = lambda n, s, dt=FP32: ctx.enter_context(nc.sbuf_tensor(f"ff_{n}", s, dt))
        sem = lambda n: m.semaphore(nc, f"ff_{n}")
        w1, w2 = sb("w1", [DIM, CH * PART]), sb("w2", [PART, CH, DIM])
        hidden, y = sb("hidden", [PART, 3, BLOCK]), sb("y", [PART, TOKENS])
        ps_h = ctx.enter_context(nc.psum_tensor("ff_ps_h", [PART, 2, BLOCK], FP32))
        ps_a = ctx.enter_context(nc.psum_tensor("ff_ps_a", [PART, 2, BLOCK], FP32))
        ps_t = ctx.enter_context(nc.psum_tensor("ff_ps_t", [PART, 2, BLOCK], FP32))
        w_in, h_ready, hidden_ready, a_ready, y_kept, turned, z_added = (sem(n) for n in ("w_in", "h_ready", "hidden_ready", "a_ready", "y_kept", "turned", "z_added"))
        UNITS = BLOCKS * CH
        with nc.Block() as block:
            @block.sync
            def _(sp):
                sp.dma_start(w1[:], a["L0_xattn_W1"]).then_inc(w_in, 16)
                sp.dma_start(w2[:], a["L0_xattn_W2"].rearrange("(c p) d -> p c d", p=PART)).then_inc(w_in, 16)
                sp.wait_ge(w_in, 32)

            @block.tensor
            def _(pe):
                def up(n):
                    t, c = divmod(n, CH)
                    if n >= 2:
                        pe.wait_ge(hidden_ready, n - 1)
                    pe.matmul(ps_h[:, n % 2, :], w1[:, c * PART:(c + 1) * PART], m.xt[:, t * BLOCK:(t + 1) * BLOCK], start=True,
                              stop=True).then_inc(h_ready, 1)

                pe.wait_ge(w_in, 32)
                up(0)
                for n in range(UNITS):
                    t, c = divmod(n, CH)
                    if n + 1 < UNITS:
                        up(n + 1)
                    pe.wait_ge(hidden_ready, n + 1)
                    if c == 0 and t >= 2:
                        pe.wait_ge(y_kept, t - 1)
                    pe.matmul(ps_a[:, t % 2, :], w2[:, c, :], hidden[:, n % 3, :], start=(c == 0), stop=(c == CH - 1)).then_inc(a_ready, 1)
                for t in range(BLOCKS):
                    pe.wait_ge(y_kept, t + 1)
                    if t >= 2:
                        pe.wait_ge(z_added, t - 1)
                    for j in range(4):
                        i = 4 * t + j
                        mm = pe.transpose(ps_t[:, t % 2, j * PART:(j + 1) * PART], y[:, i * PART:(i + 1) * PART], m.ident[:])
                    mm.then_inc(turned, 1)

            @block.scalar
            def _(act):
                for n in range(UNITS):
                    t, c = divmod(n, CH)
                    act.wait_ge(h_ready, n + 1)
                    if n >= 3:
                        act.wait_ge(a_ready, n - 2)
                    nc.scalar.activation(hidden[:, n % 3, :], ps_h[:, n % 2, :], ACT.Gelu, bias=m.col("b1")[:, c:c + 1]).then_inc(hidden_ready, 1)

            @block.vector
            def _(dve):
                for t in range(BLOCKS):
                    dve.wait_ge(a_ready, CH * (t + 1))
                    dve.tensor_scalar(y[:, t * BLOCK:(t + 1) * BLOCK], ps_a[:, t % 2, :], m.col("b2"), None, ALU.add).then_inc(y_kept, 1)
                for t in range(BLOCKS):
                    rows = z[:, 4 * t:4 * t + 4, :].rearrange("p t d -> p (t d)")
                    dve.wait_ge(turned, t + 1)
                    dve.tensor_tensor(rows, rows, ps_t[:, t % 2, :], ALU.add).then_inc(z_added, 1)


def add_out(nc, m, z):
    with ExitStack() as ctx:
        steps = m.semaphore(nc, "addout_steps")
        gain = ctx.enter_context(nc.sbuf_tensor("addout_gain", [PART, 2, DIM], FP32))
        with nc.Block() as block:
            @block.vector
            def _(dve):
                c = Chain(dve, steps)
                c.did(dve.tensor_scalar(gain[:, 0, :], m.row("out_g"), m.gate[:, 0:1], None, ALU.mult))
                c.did(dve.tensor_scalar(gain[:, 1, :], m.row("out_b"), m.gate[:, 0:1], None, ALU.mult))
                every = lambda n: gain[:, n, :].unsqueeze(1).to_broadcast([PART, TILES, DIM])
                c.wait()
                c.did(dve.tensor_tensor(z[:], z[:], every(0), ALU.mult))
                c.wait()
                c.did(dve.tensor_tensor(m.x[:], m.x[:], every(1), ALU.add))
                c.wait()
                c.did(dve.tensor_tensor(m.x[:], m.x[:], z[:], ALU.add))
                c.wait()


def layer0_attention(nc, m, a):
    with ExitStack() as ctx:
        sb = lambda n, s: ctx.enter_context(nc.sbuf_tensor(f"l0_{n}", s, FP32))
        kernel_dram = nc.dram_tensor("state_kernel", (DIM, COARSE, FINE), FP32, kind="Internal").ap()
        z = sb("z", [PART, TILES, DIM])
        with ExitStack() as inner:
            tb = lambda n, s: inner.enter_context(nc.sbuf_tensor(f"l0_{n}", s, FP32))
            cos, sin = tb("cos", [PART, FREQ, SEQ]), tb("sin", [PART, FREQ, SEQ])
            turn = tb("turn", [PART, FREQ, 2])
            kern = tb("kern", [DIM, SEQ])
            tables_in, kern_in = m.semaphore(nc, "l0_tables_in"), m.semaphore(nc, "l0_kern_in")
            keysT = tb("keysT", [DIM, BATCH + 1, L0_HEADS * KEYS])
            values = tb("values", [CTX_CHUNK + 1, BATCH * 2, 4 * DIM])
            masked = tb("masked", [PART, BATCH + 1, KEYS])
            weight = tb("weight", [PART, TILES + 1])
            with ExitStack() as tables:
                film = film_tables(nc, tables, m, a, keysT, values, masked, weight)
                state = state_kernel(nc, tables, m, a, kernel_dram)
                with nc.Block() as block:
                    @block.sync
                    def _(sp):
                        film["sync"](sp)
                        state["sync"](sp)
                        sp.dma_start(kern[:], kernel_dram.rearrange("d a b -> d (a b)")).then_inc(kern_in, 16)
                        sp.dma_start(turn[:], a["half_turn"]).then_inc(tables_in, 16)
                        sp.dma_start(cos[:], a["dft_cos"].rearrange("(c p) f -> p c f", p=PART)).then_inc(tables_in, 16)
                        sp.dma_start(sin[:], a["dft_sin"].rearrange("(c p) f -> p c f", p=PART)).then_inc(tables_in, 16)

                    @block.gpsimd
                    def _(pool):
                        film["gpsimd"](pool)
                        state["gpsimd"](pool)

                    @block.tensor
                    def _(pe):
                        film["tensor"](pe)
                        state["tensor"](pe)

                    @block.scalar
                    def _(act):
                        film["scalar"](act)
                        state["scalar"](act)

                    @block.vector
                    def _(dve):
                        film["vector"](dve)
                        state["vector"](dve)
            mod = tb("mod", [PART, TILES + 2, 4 * DIM])
            film_tokens(nc, m, keysT, values, masked, weight, mod)
            u = inner.enter_context(nc.sbuf_tensor("l0_u", [PART, TILES, DIM], FP32))
            norm(nc, m, "l0_in", m.xn, 1e-5, u)
            state_space(nc, m, (cos, sin, turn, kern, tables_in, kern_in), u, mod, z)
        norm(nc, m, "l0_ffn", z, 1e-5, m.xn, m.xt, m.col("ffn_g"), m.col("ffn_b"))
        feed_forward(nc, m, a, z)
        norm(nc, m, "l0_out", z, 1e-5, z)
        add_out(nc, m, z)


def store(nc, m, out):
    with nc.semaphore("out_done") as out_done, nc.Block() as block:
        @block.sync
        def _(sp):
            sp.dma_start(out.rearrange("b (j p) d -> p (b j) d", p=PART), m.x[:]).then_inc(out_done, 16)
            sp.wait_ge(out_done, 16)


L1_FFN = Mixture("relu2", 1, "L1_ffn", 64)
L2_FFN = Mixture("swiglu", 2, "L2_ffn", 64)
L3_FFN = Mixture("gelu", 3, "L3_ffn", 8)


def norm_x(nc, m, name):
    norm(nc, m, name, m.x, 1e-5, m.xn, m.xt)


def norm_norm_x(nc, m, name, eps, gain, shift):
    norm_x(nc, m, f"{name}_x")
    norm(nc, m, name, m.xn, eps, m.xn, m.xt, m.col(gain), m.col(shift))


def layers(nc, m, a):
    norm_x(nc, m, "n0_att")
    layer0_attention(nc, m, a)
    norm_norm_x(nc, m, "n0_ffn", 1e-3, "tern_g", "tern_b")
    ternary(nc, m, a)
    m.clear_semaphores(nc)
    norm_norm_x(nc, m, "n1_att", 1e-5, "ln_l_g", "ln_l_b")
    latent_attention(nc, m, a)
    norm_x(nc, m, "n1_ffn")
    moe(nc, m, a, L1_FFN)
    m.clear_semaphores(nc)
    norm_x(nc, m, "n2_att")
    attention(nc, m, a, L2_ATT)
    norm_x(nc, m, "n2_ffn")
    moe(nc, m, a, L2_FFN)
    m.clear_semaphores(nc)
    norm_x(nc, m, "n3_att")
    attention(nc, m, a, L3_ATT)
    norm_x(nc, m, "n3_ffn")
    moe(nc, m, a, L3_FFN)


def program(nc, a, out, stages=layers):
    with ExitStack() as ctx:
        m = Memory(nc, ctx)
        setup(nc, m, a)
        stages(nc, m, a)
        store(nc, m, out)


def arrange(inputs):
    import numpy as np
    v = {k: np.asarray(x) for k, x in inputs.items()}
    v["L3_ffn_b1"] = v["L3_ffn_b1"].reshape(32, PART).T
    for p, heads, wo in (("L2_xattn", 16, "Wo"), ("L3_xattn", 8, "Wout")):
        hp = PART * heads // v[f"{p}_Wq"].shape[1]
        for w in ("Wq", "Wk", "Wv"):
            x = v.pop(f"{p}_{w}")
            v[f"{p}_{w}T"] = x.reshape(x.shape[0], heads // hp, PART).transpose(2, 1, 0).reshape(PART, -1)
        x = v.pop(f"{p}_{wo}")
        v[f"{p}_Wo"] = x.reshape(heads // hp, PART, DIM).transpose(1, 0, 2).reshape(PART, -1)
    column = lambda name: np.pad(v[name].reshape(-1, min(PART, v[name].size)).T, ((0, PART - min(PART, v[name].size)), (0, 0)))
    v["columns"] = np.concatenate([column(n) for n in (
        "L1_xattn_ln_l_g", "L1_xattn_ln_l_b", "L1_xattn_ln_x_g", "L1_xattn_ln_x_b", "L0_ffn_ln_gamma", "L0_ffn_ln_beta",
        "L0_xattn_g_ffn", "L0_xattn_b_ffn", "L0_xattn_b1", "L0_xattn_b2", "L0_xattn_D_skip")], axis=1)
    v["rows"] = np.concatenate([v[n].reshape(-1) for n in (
        "L1_xattn_qn_g", "L1_xattn_kn_g", "L1_xattn_bo", "L0_xattn_g_norm_in", "L0_xattn_b_norm_in", "L0_xattn_g_norm_out",
        "L0_xattn_b_norm_out", "L0_xattn_mod_gate", "L0_xattn_log_dt")])
    v["L1_xattn_WkvT"] = v["L1_xattn_Wkv"].T
    v["L1_xattn_WqkvT"] = np.concatenate([v["L1_xattn_Wq"], v["L1_xattn_Wlkv"]]).T
    v["L1_xattn_WoT"] = v["L1_xattn_Wo"].T
    for w in ("Wq", "Wk", "Wv"):
        v[f"L0_xattn_{w}T"] = v.pop(f"L0_xattn_{w}").T
    v["L0_xattn_Wfilm"] = np.concatenate([v.pop("L0_xattn_W_film_in"), v.pop("L0_xattn_W_film_out")], axis=1)
    v["L0_xattn_bfilm"] = np.concatenate([v.pop("L0_xattn_b_film_in"), v.pop("L0_xattn_b_film_out")])
    v["mask_BxS_bf1"] = v["mask_BxS_bf1"].reshape(TILES, PART).T
    v["L0_xattn_AC"] = np.stack([np.concatenate([v[f"L0_xattn_{n}"].T] * 2) for n in ("A_re", "A_im", "C_re", "C_im")], axis=1)
    consts = np.zeros((PART, 3 + FINE + COARSE), np.float32)
    consts[:STATES, 0] = 0.25
    consts[:STATES, 1] = TWO_PI / 4
    consts[:, 2] = TWO_PI / 4
    consts[:, 3:3 + FINE] = np.arange(FINE)
    consts[:, 3 + FINE:] = FINE * np.arange(COARSE)
    v["ssm_consts"] = consts
    half = np.arange(SEQ) + 0.5
    angle = 2 * np.pi / (2 * SEQ) * np.outer(half, half)
    v["dft_cos"], v["dft_sin"] = np.cos(angle).astype(np.float32), np.sin(angle).astype(np.float32)
    omega = (np.pi / (2 * SEQ) * half).reshape(FREQ, PART).T
    v["half_turn"] = (np.stack([np.cos(omega), np.sin(omega)], axis=2) / SEQ).astype(np.float32)
    v["L3_xattn_bo"] = v.pop("L3_xattn_bout")
    return {k: np.ascontiguousarray(x) for k, x in v.items()}


def kernel(**inputs):
    import concourse.bacc as _bacc
    from concourse import mybir as _mybir
    from concourse.bass_utils import run_bass_kernel_spmd as _run

    nc = _bacc.Bacc("TRN2", target_bir_lowering=False, num_devices=1)
    arrays = arrange(inputs)
    a = {n: nc.dram_tensor(n, v.shape, _mybir.dt.from_np(v.dtype), kind="ExternalInput").ap() for n, v in arrays.items()}
    out = nc.dram_tensor("out", (BATCH, SEQ, DIM), FP32, kind="ExternalOutput").ap()
    program(nc, a, out)
    return _run(nc, [arrays], core_ids=[0]).results[0]["out"]
```
